# Optimizing a Trainium2 kernel written in Bass

```python
import numpy as np
import jax
import jax.numpy as jnp

def _softmax(x, axis=-1):
    return jax.nn.softmax(x, axis=axis)

def _gelu(x):
    return jax.nn.gelu(x, approximate=True)

def _silu(x):
    return jax.nn.silu(x)

def _sigmoid(x):
    return jax.nn.sigmoid(x)

def _layernorm(x, axis=-1, eps=1e-05):
    m = jnp.mean(x, axis=axis, keepdims=True)
    v = jnp.var(x, axis=axis, keepdims=True)
    return (x - m) / jnp.sqrt(v + eps)

def _scatter_add(tgt, idx, src, axis=0):
    return tgt.at[idx].add(src)

def _segment_sum(src, seg, n):
    return jax.ops.segment_sum(src, seg, n)
kernel_name = 'mk_adj_ffn_d1_adj_r2_b9e5c7'

def setup_inputs(seed: int=0):
    np.random.seed(seed)
    _w = jnp.asarray

    def _rec_inputs():
        import jax
        import jax.numpy as jnp
        _gk = jax.random.key(seed)
        x = -0.0002928 + 1 * jax.random.normal(jax.random.fold_in(_gk, 1), (2048, 512), jnp.float32)
        _a = jax.random.bernoulli(jax.random.fold_in(_gk, 2), 0.00390625, (2048, 2048))
        _a = jnp.logical_or(_a, jnp.swapaxes(_a, -1, -2))
        _a = jnp.logical_or(_a, jnp.eye(2048, dtype=bool))
        _af = _a.astype(jnp.float32)
        adj = _af
        return (x, adj)
    x, adj = _rec_inputs()

    def _L0_gnn_setup():
        import jax, jax.numpy as jnp
        import numpy as np
        N = 2048
        D_IN = 512
        H = 16
        DH = D_IN // H
        ALPHA = 0.2
        MASK_VAL = -65500.0
        key = jax.random.key(seed)
        ks = jax.random.split(key, 7)
        x = jax.random.normal(ks[0], (N, D_IN), dtype=jnp.float32)
        adj = jax.random.randint(ks[1], (N, N), 0, 2).astype(jnp.float32)
        s = 1.0 / np.sqrt(D_IN)
        W_seq = jax.random.normal(ks[2], (D_IN, D_IN), dtype=jnp.float32) * s
        a1 = jax.random.normal(ks[3], (DH,), dtype=jnp.float32) / np.sqrt(DH)
        a2 = jax.random.normal(ks[4], (DH,), dtype=jnp.float32) / np.sqrt(DH)
        W_out = jax.random.normal(ks[5], (D_IN, D_IN), dtype=jnp.float32) * s
        b_out = jax.random.normal(ks[6], (D_IN,), dtype=jnp.float32) * 0.01
        return {'x': x, 'adj': adj, 'W_seq': W_seq, 'a1': a1, 'a2': a2, 'W_out': W_out, 'b_out': b_out}
    _L0_gnn_all = _L0_gnn_setup()
    _L0_gnn_in = {k: v for k, v in _L0_gnn_all.items() if k in ('W_seq', 'a1', 'a2', 'W_out', 'b_out')}
    del _L0_gnn_all

    def _L0_ffn_setup():
        import jax, jax.numpy as jnp
        import numpy as np
        key = jax.random.key(seed)
        ks = jax.random.split(key, 6)
        B, S, D, F, E = (4, 1024, 512, 2048, 4)
        sd = 1.0 / np.sqrt(D)
        sf = 1.0 / np.sqrt(F)
        return {'x': jax.random.normal(ks[0], (B, S, D), jnp.float32), 'router_w': jax.random.normal(ks[1], (D, E), jnp.float32) * sd, 'w1': jax.random.normal(ks[2], (E, D, F), jnp.float32) * sd, 'b1': jnp.zeros((E, F), jnp.float32), 'w2': jax.random.normal(ks[3], (E, F, D), jnp.float32) * sf, 'b2': jnp.zeros((E, D), jnp.float32)}
    _L0_ffn_all = _L0_ffn_setup()
    _L0_ffn_in = {k: v for k, v in _L0_ffn_all.items() if k in ('router_w', 'w1', 'b1', 'w2', 'b2')}
    del _L0_ffn_all
    return {'x': x, 'adj': adj, 'L0_gnn_W_seq': _L0_gnn_in['W_seq'], 'L0_gnn_a1': _L0_gnn_in['a1'], 'L0_gnn_a2': _L0_gnn_in['a2'], 'L0_gnn_W_out': _L0_gnn_in['W_out'], 'L0_gnn_b_out': _L0_gnn_in['b_out'], 'L0_ffn_router_w': _L0_ffn_in['router_w'], 'L0_ffn_w1': _L0_ffn_in['w1'], 'L0_ffn_b1': _L0_ffn_in['b1'], 'L0_ffn_w2': _L0_ffn_in['w2'], 'L0_ffn_b2': _L0_ffn_in['b2']}

def reference(x, adj, L0_gnn_W_seq, L0_gnn_a1, L0_gnn_a2, L0_gnn_W_out, L0_gnn_b_out, L0_ffn_router_w, L0_ffn_w1, L0_ffn_b1, L0_ffn_w2, L0_ffn_b2):
    import jax
    import jax.numpy as jnp

    def _L0_gnn_ref(x, adj, W_seq, a1, a2, W_out, b_out):
        import jax, jax.numpy as jnp
        import numpy as np
        N = 2048
        D_IN = 512
        H = 16
        DH = D_IN // H
        ALPHA = 0.2
        MASK_VAL = -65500.0
        seq = (x @ W_seq).reshape(N, H, DH)
        score1 = jnp.einsum('nhd,d->hn', seq, a1)
        score2 = jnp.einsum('nhd,d->hn', seq, a2)
        scores = score1[:, :, None] + score2[:, None, :]
        scores = jax.nn.leaky_relu(scores, negative_slope=ALPHA)
        scores = scores + (1.0 - adj)[None, :, :] * MASK_VAL
        attn = jax.nn.softmax(scores, axis=-1)
        hidden = jnp.einsum('hij,jhd->ihd', attn, seq).reshape(N, D_IN)
        hidden = hidden @ W_out + b_out
        return jax.nn.elu(hidden)

    def _L0_ffn_ref(x, router_w, w1, b1, w2, b2):
        import jax, jax.numpy as jnp
        import numpy as np
        B, S, D = x.shape
        E = w1.shape[0]
        denom = jnp.arange(1, S + 1, dtype=x.dtype)[None, :, None]
        ctx = jnp.cumsum(x, axis=1) / denom
        logits = jnp.einsum('bsd,de->bse', ctx, router_w)
        probs = jax.nn.softmax(logits, axis=-1)
        idx = jnp.argmax(probs, axis=-1)
        gate = jnp.take_along_axis(probs, idx[..., None], axis=-1)
        onehot = jax.nn.one_hot(idx, E, dtype=x.dtype)
        y = jnp.zeros_like(x)
        for e in range(E):
            h = jax.nn.gelu(jnp.einsum('bsd,df->bsf', x, w1[e]) + b1[e])
            y_e = jnp.einsum('bsf,fd->bsd', h, w2[e]) + b2[e]
            y = y + onehot[..., e:e + 1] * y_e
        return gate * y
    x = x + _L0_gnn_ref(_layernorm(x, axis=-1), adj, L0_gnn_W_seq, L0_gnn_a1, L0_gnn_a2, L0_gnn_W_out, L0_gnn_b_out)
    x = x + _L0_ffn_ref(_layernorm(x, axis=-1)[None], L0_ffn_router_w, L0_ffn_w1, L0_ffn_b1, L0_ffn_w2, L0_ffn_b2)[0]
    return x

_drawn_inputs = setup_inputs


def setup_inputs(seed=0):
    import zlib

    import numpy as np

    out = dict(_drawn_inputs(seed))
    spreads = {'L0_ffn_b1': (0.0, 0.471), 'L0_ffn_b2': (0.0, 0.313)}
    factors = {}
    for name, (base, spread) in spreads.items():
        noise = np.random.default_rng([zlib.crc32(name.encode()), seed]).standard_normal(out[name].shape)
        drawn = base * np.exp(spread * noise) if base else spread * noise
        out[name] = jnp.asarray(drawn.astype(out[name].dtype))
    for name, factor in factors.items():
        out[name] = (out[name] * factor).astype(out[name].dtype)
    return out
```

```python
import concourse.bass as bass
from concourse import mybir
from contextlib import ExitStack


def gat_moe_kernel(nc, x, adj, w_seq, a1, a2, w_out, b_out, router_w, w1, b1, w2, b2, out):
    fp32, fp16, bf16, i32 = mybir.dt.float32, mybir.dt.float16, mybir.dt.bfloat16, mybir.dt.int32
    ALU = mybir.AluOpType
    ACT = mybir.ActivationFunctionType
    X = mybir.AxisListType.X
    ds = bass.ds

    P = 128
    N, D = x.shape
    DH = a1.shape[0]
    H = D // DH
    NT = N // P
    KC = D // P
    C = DH + 1
    BD = 2 * C
    Q = 3
    ALPHA = 0.2
    EPS = 1e-5

    SCALE = 256.0
    UNSCALE = 1.0 / (SCALE * SCALE)
    STEEP = 2.0 ** 100

    PAIRS = H // 2
    HALF = NT // 2
    SLOTS = 6
    RING = 4
    COMB_BASE = 1
    BD_STEPS = 8
    LOGITS_AT = 5
    EXP_AT = LOGITS_AT + 13
    ONEHOT_AT = EXP_AT + 8
    ROUTE_STEPS = ONEHOT_AT + 22
    FUSED = (5, 13)
    MADE = NT - len(FUSED)
    G_BASE = 2 * NT

    E, F = b1.shape
    FC = F // P
    SLOT = 2 * P
    TT = SLOT // P
    SLOTS_MOE = (N + E * (SLOT - 1)) // SLOT
    CH = 2 * KC
    HSCALE = 64.0

    ctx = ExitStack()
    with ctx:
        at = [16512]

        def sb(name, shape, dt, offset=None):
            size = {fp32: 4, i32: 4, fp16: 2, bf16: 2}[dt]
            for n in shape[1:]:
                size *= n
            if offset is None:
                offset = at[0]
                at[0] += (size + 31) // 32 * 32
            return nc.alloc_sbuf_tensor_at(name, shape, dt, offset=offset)

        ident16 = sb("ident16", [P, P], fp16)
        identb = sb("identb", [P, P], bf16)
        identf = sb("identf", [P, P], fp32)
        ones = sb("ones", [P, P], fp32)
        eps_col = sb("eps_col", [P, 1], fp32)
        tri = sb("tri", [P, P], fp32)
        rw = sb("rw", [P, KC, E], fp32)
        rw_sum = sb("rw_sum", [P, E], fp32)
        mv2 = sb("mv2", [P, NT, 2], fp32)
        std2 = sb("std2", [P, NT], fp32)
        rstd2 = sb("rstd2", [P, NT], fp32)
        token_no = sb("token_no", [P, NT], fp32)
        slot_no = sb("slot_no", [P, SLOTS_MOE], fp32)
        slot_low = sb("slot_low", [P, N // SLOT], fp32)
        gate = sb("gate", [P, NT], fp32)
        row_of = sb("row_of", [P, NT], i32)
        expert_of = sb("expert_of", [P, SLOTS_MOE], i32)
        b1_all = sb("b1_all", [P, E * FC], fp32)
        b1_now = [sb(f"b1_now{b}", [P, FC], fp32) for b in range(2)]
        eps1 = sb("eps1", [P, 1], fp32)
        wo_region = at[0]
        wo_hi = sb("wo_hi", [P, KC, D], fp16)
        wo_lo = sb("wo_lo", [P, KC, D], fp16)
        bo_bc = sb("bo_bc", [P, D], fp32)
        fac_a = sb("fac_a", [P, NT, H], fp32)
        fac_c = sb("fac_c", [P, NT, H], fp32)
        den = sb("den", [P, NT, H], fp32)
        routing_region = at[0]
        steep_bias = sb("steep_bias", [P, NT, H], fp32)
        neg_s2 = sb("neg_s2", [P, NT, H], fp32)
        fac_b = sb("fac_b", [P, NT, H], fp32)
        fac_d = sb("fac_d", [P, NT, H], fp32)
        bias_now = [sb(f"bias_now{b}", [P, NT], fp32) for b in range(2)]
        w0_region = at[0]
        adjT = sb("adjT", [P, NT, N], bf16)
        vals = sb("vals", [P, NT, D], fp32)
        bd_region = at[0]
        bd = sb("bd", [P, SLOTS * NT * Q * BD], bf16)
        tsum = sb("tsum", [P, 2 * NT * 2 * C], fp32)
        s1row = [sb(f"s1row{b}", [P, N], fp32) for b in range(2)]
        gr_region = at[0]
        gmask = [sb(f"gmask{i}", [P, N // 2], bf16) for i in range(RING)]
        steps = [sb(f"steps{i}", [P, N // 2], bf16) for i in range(RING)]
        bdf = sb("bdf", [P, NT, BD], fp32)
        branch_a = sb("branch_a", [P, HALF, C], fp32)
        branch_c = sb("branch_c", [P, HALF, C], fp32)
        ssum = [sb(f"ssum{b}", [P, HALF, BD], fp32) for b in range(2)]
        assert at[0] <= 229344, at[0]
        attention_end = at[0]
        stage_region = 229344 - 2 * 4 * F

        at[0] = bd_region
        x_in = [sb(f"x_in{b}", [P, D], fp32) for b in range(2)]
        adj_in = [sb(f"adj_in{b}", [P, N], fp32) for b in range(2)]
        adj_b = [sb(f"adj_b{b}", [P, N], bf16) for b in range(2)]
        xs = [sb(f"xs{b}", [P, D], fp32) for b in range(2)]
        x_hl = [sb(f"x_hl{b}", [P, 2, D], fp16) for b in range(2)]
        xT = [sb(f"xT{b}", [P, 2, KC, P], fp16) for b in range(2)]
        stats = [sb(f"stats{b}", [P, 6], fp32) for b in range(2)]
        mv = [sb(f"mv{b}", [P, 2], fp32) for b in range(2)]
        std = [sb(f"std{b}", [P, 1], fp32) for b in range(2)]
        rstd = [sb(f"rstd{b}", [P, 1], fp32) for b in range(2)]
        degree = [sb(f"degree{b}", [P, 1], fp32) for b in range(2)]
        alone = [sb(f"alone{b}", [P, 1], fp32) for b in range(2)]
        wf = sb("wf", [P, KC, D], fp32)
        wq_hi = sb("wq_hi", [P, KC, D], fp16)
        wq_lo = sb("wq_lo", [P, KC, D], fp16)
        aw = sb("aw", [P, 2, DH], fp32)
        wa = sb("wa", [P, KC, 2 * H], fp32)
        wa_hi = sb("wa_hi", [P, KC, 2 * H], fp16)
        wa_lo = sb("wa_lo", [P, KC, 2 * H], fp16)
        zeros = sb("zeros", [P, D], fp32)
        assert at[0] <= gr_region
        at[0] = gr_region
        s_row = sb("s_row", [2 * H, N], fp32)
        s_tok = sb("s_tok", [P, NT, 2 * H], fp32)
        top_row = sb("top_row", [2 * H, 1], fp32)
        top_diag = sb("top_diag", [2 * H, 2 * H], fp32)
        top = sb("top", [P, 2 * H], fp32)
        sx = sb("sx", [P, NT, H], fp32)
        sa = sb("sa", [P, NT, H], fp32)
        sc = sb("sc", [P, NT, H], fp32)
        sy = sb("sy", [P, NT, H], fp32)
        assert at[0] <= attention_end
        wprod = vals[:, 0:4, :]
        wo_f = vals[:, 8:8 + KC, :]

        at[0] = bd_region
        px = [sb(f"px{b}", [P, D], fp32) for b in range(2)]
        rden = [sb(f"rden{b}", [P, H], fp32) for b in range(2)]
        hn = [sb(f"hn{b}", [P, D], fp32) for b in range(2)]
        h_hl = [sb(f"h_hl{b}", [P, 2, D], fp16) for b in range(2)]
        hT = [sb(f"hT{b}", [P, 2, KC, P], fp16) for b in range(2)]
        z = [sb(f"z{b}", [P, D], fp32) for b in range(2)]
        zneg = [sb(f"zneg{b}", [P, D], fp32) for b in range(2)]
        ez = [sb(f"ez{b}", [P, D], fp32) for b in range(2)]
        x1 = sb("x1", [P, NT, D], fp32)
        x1_now = [sb(f"x1_now{b}", [P, D], fp32) for b in range(2)]
        x1T = [sb(f"x1T{b}", [P, KC, P], fp32) for b in range(2)]
        stats2 = sb("stats2", [P, NT, 6], fp32)
        assert at[0] <= stage_region
        at[0] = stage_region
        stage = [sb(f"stage{b}", [P, F], fp32) for b in range(2)]

        at[0] = routing_region
        raw = sb("raw", [P, NT, E], fp32)
        shift = sb("shift", [P, NT, E], fp32)
        logit = sb("logit", [P, NT, E], fp32)
        upto = sb("upto", [P, NT, E], fp32)
        before = sb("before", [P, NT, E], fp32)
        ctx_l = sb("ctx_l", [P, NT, E], fp32)
        expd = sb("expd", [P, NT, E], fp32)
        same = sb("same", [P, NT, E], fp32)
        onehot = sb("onehot", [P, NT, E], fp32)
        seen = sb("seen", [P, NT], fp32)
        largest = sb("largest", [P, NT], fp32)
        total = sb("total", [P, NT], fp32)
        above = sb("above", [P, E, N // SLOT], fp32)
        zero_t = sb("zero_t", [P, NT], fp32)
        slot_f = sb("slot_f", [P, SLOTS_MOE], fp32)
        n_slots = sb("n_slots", [P, E], fp32)
        last_slot = sb("last_slot", [P, E], fp32)
        first_row = sb("first_row", [P, E], fp32)
        past = sb("past", [P, SLOTS_MOE, E - 1], fp32)
        assert at[0] <= w0_region

        assert w0_region + 2 * 8 * KC * F // 2 <= bd_region + 4 * NT * D
        wbuf = []
        for b in range(2):
            at[0] = w0_region + b * (8 * KC * F)
            wbuf.append([sb(f"w1_hi{b}", [P, KC, F], fp16), sb(f"w1_lo{b}", [P, KC, F], fp16),
                         sb(f"w2_hi{b}", [P, FC, D], fp16), sb(f"w2_lo{b}", [P, FC, D], fp16)])
        xg = [sb(f"xg{b}", [P, TT, D], fp32) for b in range(2)]
        xg_hl = sb("xg_hl", [P, TT, 2, D], fp16)
        xgT = [sb(f"xgT{b}", [P, 2, KC, SLOT], fp16) for b in range(2)]
        hidT = sb("hidT", [P, 2, FC, SLOT], fp16)
        hid = [sb(f"hid{i}", [P, SLOT], fp32) for i in range(4)]
        assert at[0] <= stage_region, (at[0], attention_end)
        at[0] = wo_region
        b2_now = [sb(f"b2_now{b}", [P, D], fp32) for b in range(2)]
        y_sb = [sb(f"y_sb{b}", [P, D], fp32) for b in range(2)]
        yg = [xgT[b][:, :, :, :].rearrange("p a b c -> p (a b c)").bitcast(fp32)[:, 0:D] for b in range(2)]
        x1r = [xgT[b][:, :, :, :].rearrange("p a b c -> p (a b c)").bitcast(fp32)[:, D:2 * D] for b in range(2)]
        res = [xg[b][:, 0, :] for b in range(2)]

        psum = ctx.enter_context(nc.psum_tensor("psum", [P, 8, 512], fp32))
        bank = [psum[:, i, :] for i in range(8)]
        sums = psum[:, 0:4, :].rearrange("p a (b c) -> p (a b) c", b=2)
        tails = psum[:, 4:6, :].rearrange("p a (b c) -> p (a b) c", b=2)

        sorted_x = nc.dram_tensor("sorted_x", [SLOTS_MOE * SLOT, D], fp32, kind="Internal").ap()
        sorted_y = nc.dram_tensor("sorted_y", [SLOTS_MOE * SLOT, D], fp32, kind="Internal").ap()
        x1_dram = nc.dram_tensor("x1_dram", [N, D], fp32, kind="Internal").ap()
        s1_dram = nc.dram_tensor("s1_dram", [H, N], fp32, kind="Internal").ap()

        def sem(name):
            return ctx.enter_context(nc.semaphore(name))

        passed = sem("passed")
        consts, consts0 = sem("consts"), sem("consts0")
        x_loaded = [sem(f"x_loaded{b}") for b in range(2)]
        adj_loaded = [sem(f"adj_loaded{b}") for b in range(2)]
        wq_loaded, wo_loaded, a_loaded, bo_loaded = sem("wq_loaded"), sem("wo_loaded"), sem("a_loaded"), sem("bo_loaded")
        wprep = sem("wprep")
        whi_done = sem("whi_done")
        wlo_done = sem("wlo_done")
        stats_done, mv_done, std_done, rstd_done, xs_done = (sem(n) for n in ("stats_done", "mv_done", "std_done", "rstd_done", "xs_done"))
        hi_done, lo_done, xtr_done, xT_done = (sem(n) for n in ("hi_done", "lo_done", "xtr_done", "xT_done"))
        cast_done, alone_done, amax_done, atr_done, adjT_a, adjT_v = (sem(n) for n in ("cast_done", "alone_done", "amax_done", "atr_done", "adjT_a", "adjT_v"))
        proj_done, s_done, vals_done, s_copied = (sem(n) for n in ("proj_done", "s_done", "vals_done", "s_copied"))
        factors, top_mm, factors_act = sem("factors"), sem("top_mm"), sem("factors_act")
        s1_stored = sem("s1_stored")
        s1_loaded = [sem(f"s1_loaded{b}") for b in range(2)]
        bd_chain = sem("bd_chain")
        bias_done = sem("bias_done")
        step_ready, g_ready, g_used = sem("step_ready"), sem("g_ready"), sem("g_used")
        t_done, t_free = sem("t_done"), sem("t_free")
        sum_used = sem("sum_used")
        comb, comb_done = sem("comb"), sem("comb_done")
        px_loaded = [sem(f"px_loaded{b}") for b in range(2)]
        rden_done, hn_done, h_hi_done, h_lo_done, htr_done, hT_done = (sem(n) for n in ("rden_done", "hn_done", "h_hi_done", "h_lo_done", "htr_done", "hT_done"))
        out_mm, z_done, zneg_done, ez_done, elu_done, x1_done = (sem(n) for n in ("out_mm", "z_done", "zneg_done", "ez_done", "elu_done", "x1_done"))
        rw_loaded, b1_loaded, cleared = sem("rw_loaded"), sem("b1_loaded"), sem("cleared")
        x1_stored, x1_kept = sem("x1_stored"), sem("x1_kept")
        bn2_done, mv2_done, x1tr_done, x1T_done, logit_mm, srw_mm = (sem(n) for n in ("bn2_done", "mv2_done", "x1tr_done", "x1T_done", "logit_mm", "srw_mm"))
        route, route_mm, route_act, xn_done = sem("route"), sem("route_mm"), sem("route_act"), sem("xn_done")
        scattered = sem("scattered")
        stage_loaded = [sem(f"stage_loaded{b}") for b in range(2)]
        bias_loaded = [sem(f"bias_loaded{b}") for b in range(2)]
        xg_loaded = [sem(f"xg_loaded{b}") for b in range(2)]
        w_hi_done, w_lo_done = sem("w_hi_done"), sem("w_lo_done")
        xg_hi_done, xg_lo_done, xgtr_done, xgT_a, xgT_v = (sem(n) for n in ("xg_hi_done", "xg_lo_done", "xgtr_done", "xgT_a", "xgT_v"))
        up_mm, gelu_done, hid_hi, hid_lo, down_mm, y_done = (sem(n) for n in ("up_mm", "gelu_done", "hid_hi", "hid_lo", "down_mm", "y_done"))
        y_stored = [sem(f"y_stored{b}") for b in range(2)]
        yg_loaded = [sem(f"yg_loaded{b}") for b in range(2)]
        x1r_loaded = [sem(f"x1r_loaded{b}") for b in range(2)]
        res_done = sem("res_done")
        out_stored = [sem(f"out_stored{b}") for b in range(2)]

        def at_least(eng, s, n):
            if not isinstance(n, int) or n > 0:
                eng.wait_ge(s, n)

        def wait_apart(eng, s, n):
            eng.wait_ge(s, n)
            eng.sem_inc(passed, 1)

        def chain(eng, s, ins, n):
            ins.then_inc(s, 1)
            eng.wait_ge(s, n)

        def chain_apart(eng, s, ins, n):
            ins.then_inc(s, 1)
            wait_apart(eng, s, n)

        x_t = x.rearrange("(t p) d -> p t d", p=P)
        adj_t = adj.rearrange("(t p) n -> p t n", p=P)
        out_t = out.rearrange("(t p) d -> p t d", p=P)

        x1_t = x1_dram.rearrange("(t p) d -> p t d", p=P)
        sorted_x_t = sorted_x.rearrange("(s p) d -> p s d", p=P)
        sorted_y_t = sorted_y.rearrange("(s p) d -> p s d", p=P)

        def slot_loop(eng, body):
            body(0, 0, 0, True)
            body(1, 1, 0, True)
            with eng.Fori(1, SLOTS_MOE // 2) as k:
                body(2 * k, 0, k, True)
                body(2 * k + 1, 1, k, True)
            assert SLOTS_MOE % 2
            body(SLOTS_MOE - 1, 0, SLOTS_MOE // 2, False)

        block = ctx.enter_context(nc.Block())

        @block.sync
        def _(sp):
            sp.dma_start(wf[:, :, :], w_seq.rearrange("(c p) n -> p c n", p=P)).then_inc(wq_loaded, 16)
            sp.dma_start(aw[:, 0, :], a1.partition_broadcast(P)).then_inc(a_loaded, 16)
            sp.dma_start(aw[:, 1, :], a2.partition_broadcast(P)).then_inc(a_loaded, 16)
            sp.dma_start(wo_f, w_out.rearrange("(c p) n -> p c n", p=P)).then_inc(wo_loaded, 16)
            sp.dma_start(bo_bc[:, :], b_out.partition_broadcast(P)).then_inc(bo_loaded, 16)
            sp.dma_start(rw[:, :, :], router_w.rearrange("(c p) e -> p c e", p=P)).then_inc(rw_loaded, 16)

            def load_tile(t, b):
                at_least(sp, xs_done, t - 1)
                at_least(sp, cast_done, t - 1)
                sp.dma_start(x_in[b][:, :], x_t[:, ds(t, 1), :]).then_inc(x_loaded[b], 16)
                sp.dma_start(adj_in[b][:, :], adj_t[:, ds(t, 1), :]).then_inc(adj_loaded[b], 16)

            load_tile(0, 0)
            load_tile(1, 1)
            with sp.Fori(1, NT // 2) as k:
                t = 2 * k
                load_tile(t, 0)
                load_tile(t + 1, 1)

            sp.wait_ge(s_copied, 2 * NT)
            sp.dma_start(s1_dram, s_row[0:H, :]).then_inc(s1_stored, 16)
            sp.wait_ge(s1_stored, 16)

            def load_row(h, b):
                at_least(sp, step_ready, 2 * MADE * (h - 1))
                if not isinstance(h, int):
                    sp.wait_ge(g_ready, G_BASE + 2 * NT * (h - 1))
                sp.dma_start(s1row[b][:, :], s1_dram[ds(h, 1), :].partition_broadcast(P)).then_inc(s1_loaded[b], 16)

            sp.wait_ge(factors, 9)
            sp.wait_ge(cleared, 16)
            load_row(0, 0)
            load_row(1, 1)
            with sp.Fori(1, H // 2) as k:
                h = 2 * k
                load_row(h, 0)
                load_row(h + 1, 1)

            sp.wait_ge(comb_done, COMB_BASE + 2 * H)

            def load_px(t, b):
                at_least(sp, x1_done, t - 1)
                sp.dma_start(px[b][:, :], x_t[:, ds(t, 1), :]).then_inc(px_loaded[b], 16)

            load_px(0, 0)
            load_px(1, 1)
            with sp.Fori(1, NT // 2) as k:
                t = 2 * k
                load_px(t, 0)
                load_px(t + 1, 1)
            for t in range(NT):
                sp.wait_ge(x1_kept, t + 1)
                sp.dma_start(x1_t[:, t, :], x1[:, t, :]).then_inc(x1_stored, 16)

            sp.wait_ge(b1_loaded, 16)
            sp.wait_ge(route, ROUTE_STEPS)
            for t in range(SLOTS_MOE):
                b = t % 2
                e = sp.value_load(expert_of[0:1, t:t + 1], min_val=0, max_val=E - 1)
                for c in range(CH):
                    g = CH * t + c
                    at_least(sp, w_hi_done, g - 1)
                    at_least(sp, w_lo_done, g - 1)
                    if c < KC:
                        src = w1[ds(e, 1), c * P:(c + 1) * P, :].rearrange("a p f -> p (a f)")
                        dst = stage[g % 2][:, :]
                    else:
                        r = (c - KC) * (F // KC)
                        src = w2[ds(e, 1), r:r + F // KC, :].rearrange("a (q p) d -> p (a q) d", p=P)
                        dst = stage[g % 2][:, :].rearrange("p (q d) -> p q d", d=D)
                    sp.dma_start(dst, src).then_inc(stage_loaded[g % 2], 16)
                at_least(sp, gelu_done, FC * (t - 1))
                at_least(sp, y_done, TT * (t - 1))
                sp.dma_start(b1_now[b][:, :], b1_all[:, ds(e * FC, FC)]).then_inc(bias_loaded[b], 16)
                sp.dma_start(b2_now[b][:, :], b2[ds(e, 1), :].partition_broadcast(P)).then_inc(bias_loaded[b], 16)

            sp.wait_ge(down_mm, TT * SLOTS_MOE)
            for t in range(NT):
                b = t % 2
                at_least(sp, res_done, t - 1)
                sp.dma_start(x1r[b], x1_t[:, t, :]).then_inc(x1r_loaded[b], 16)
                if t > 0:
                    sp.wait_ge(res_done, t)
                    sp.dma_start(out_t[:, t - 1, :], res[1 - b]).then_inc(out_stored[1 - b], 16)
            sp.wait_ge(res_done, NT)
            sp.dma_start(out_t[:, NT - 1, :], res[(NT - 1) % 2]).then_inc(out_stored[(NT - 1) % 2], 16)
            for b in range(2):
                sp.wait_ge(out_stored[b], 16 * NT // 2)

        @block.gpsimd
        def _(pool):
            pool.sem_inc(comb_done, COMB_BASE)
            pool.memset(ones[:, :], 1.0).then_inc(consts0, 1)
            pool.memset(eps_col[:, :], EPS / (SCALE * SCALE)).then_inc(consts0, 1)
            pool.memset(eps1[:, :], EPS).then_inc(consts0, 1)
            pool.memset(zeros[:, :], 0.0).then_inc(consts0, 1)
            pool.wait_ge(consts0, 4)
            pool.dma_start(sorted_x_t, zeros[:, :].rearrange("p (a d) -> p a d", a=1).to_broadcast([P, SLOTS_MOE * TT, D])).then_inc(cleared, 16)
            with nc.allow_non_contiguous_dma(reason="one bias per partition, once"):
                pool.dma_start(b1_all[:, :].rearrange("p (e c) -> p e c", e=E), b1.rearrange("e (c p) -> p e c", p=P)).then_inc(b1_loaded, 16)
            pool.affine_select(out=tri[:, :], in_=ones[:, :], compare_op=ALU.is_ge, fill=0.0,
                               base=0, pattern=[[1, P]], channel_multiplier=-1).then_inc(consts, 1)
            pool.iota(token_no[:, :], pattern=[[P, NT]], base=1, channel_multiplier=1, allow_small_or_imprecise_dtypes=True).then_inc(consts, 1)
            pool.iota(slot_no[:, :], pattern=[[1, SLOTS_MOE]], base=0, channel_multiplier=0, allow_small_or_imprecise_dtypes=True).then_inc(consts, 1)
            pool.iota(slot_low[:, :], pattern=[[SLOT, N // SLOT]], base=0, channel_multiplier=0, allow_small_or_imprecise_dtypes=True).then_inc(consts, 1)
            for m in (ident16, identb, identf):
                pool.affine_select(out=m[:, :], in_=ones[:, :], compare_op=ALU.is_equal, fill=0.0,
                                   base=0, pattern=[[-1, P]], channel_multiplier=1).then_inc(consts, 1)

            def make_bd(h, slot, n):
                v = vals[:, :, ds(h * DH, DH)]
                fb = fac_b[:, :, ds(h, 1)]
                fd = fac_d[:, :, ds(h, 1)]
                dst = bd[:, ds(slot * (NT * Q * BD), NT * Q * BD)].rearrange("p (t q c) -> p t q c", t=NT, q=Q)
                pool.tensor_tensor(bdf[:, :, 0:DH], v, fb.to_broadcast([P, NT, DH]), ALU.mult).then_inc(bd_chain, 1)
                pool.tensor_tensor(bdf[:, :, C:C + DH], v, fd.to_broadcast([P, NT, DH]), ALU.mult).then_inc(bd_chain, 1)
                pool.tensor_copy(bdf[:, :, DH:C], fb).then_inc(bd_chain, 1)
                chain_apart(pool, bd_chain, pool.tensor_copy(bdf[:, :, C + DH:BD], fd), n + 4)
                chain_apart(pool, bd_chain, pool.tensor_copy(dst[:, :, 0, :], bdf[:, :, :]), n + 5)
                chain_apart(pool, bd_chain, pool.tensor_tensor(bdf[:, :, :], bdf[:, :, :], dst[:, :, 0, :], ALU.subtract), n + 6)
                chain_apart(pool, bd_chain, pool.tensor_copy(dst[:, :, 1, :], bdf[:, :, :]), n + 7)
                chain_apart(pool, bd_chain, pool.tensor_tensor(dst[:, :, 2, :], bdf[:, :, :], dst[:, :, 1, :], ALU.subtract), n + 8)

            COMB_STEPS = 4

            def combine(h, half, b, tbuf, hh, w):
                n = w * COMB_STEPS
                i0 = half * HALF
                pool.wait_ge(comb_done, COMB_BASE + w)
                wait_apart(pool, sum_used, w + 1)
                fa = fac_a[:, i0:i0 + HALF, ds(h, 1)].to_broadcast([P, HALF, C])
                fc = fac_c[:, i0:i0 + HALF, ds(h, 1)].to_broadcast([P, HALF, C])
                t_all = tsum[:, ds(tbuf * (NT * 2 * C), NT * 2 * C)].rearrange("p (t g c) -> p t g c", t=NT, g=2)
                pool.tensor_tensor(branch_a[:, :, :], ssum[b][:, :, 0:C], fa, ALU.mult).then_inc(comb, 1)
                chain_apart(pool, comb, pool.tensor_tensor(branch_c[:, :, :], t_all[:, i0:i0 + HALF, hh, :], ssum[b][:, :, C:BD], ALU.subtract), n + 2)
                chain_apart(pool, comb, pool.tensor_tensor(branch_c[:, :, :], branch_c[:, :, :], fc, ALU.mult), n + 3)
                chain_apart(pool, comb, pool.tensor_tensor(vals[:, i0:i0 + HALF, ds(h * DH, DH)], branch_a[:, :, 0:DH], branch_c[:, :, 0:DH], ALU.add), n + 4)
                pool.tensor_tensor(den[:, i0:i0 + HALF, ds(h, 1)], branch_a[:, :, DH:C], branch_c[:, :, DH:C], ALU.add).then_inc(comb_done, 1)

            pool.wait_ge(factors_act, 4)
            pool.wait_ge(vals_done, NT)
            pool.wait_ge(s1_stored, 16)
            for h in range(4):
                make_bd(h, h, h * BD_STEPS)

            def pair(p, prepare):
                if prepare:
                    wait_apart(pool, g_used, RING + 4 * NT * p)
                for hh in range(2):
                    for half in range(2):
                        if prepare and hh == 0:
                            h = 2 * p + 4 + half
                            make_bd(h, h % SLOTS, h * BD_STEPS)
                        combine(2 * p + hh, half, half, p % 2, hh, 4 * p + 2 * hh + half)

            with pool.Fori(0, PAIRS - 2) as p:
                pair(p, True)
            with pool.Fori(PAIRS - 2, PAIRS) as p:
                pair(p, False)

            def keep(t, b):
                wait_apart(pool, x1_done, t + 1)
                pool.tensor_copy(x1[:, ds(t, 1), :].rearrange("p a d -> p (a d)"), x1_now[b][:, :]).then_inc(x1_kept, 1)

            with pool.Fori(0, NT // 2) as k:
                keep(2 * k, 0)
                keep(2 * k + 1, 1)

            pool.wait_ge(cleared, 16)
            pool.wait_ge(xn_done, NT)
            pool.wait_ge(route, ROUTE_STEPS)
            for t in range(NT):
                pool.indirect_dma_start(out=sorted_x, out_offset=bass.IndirectOffsetOnAxis(ap=row_of[:, t:t + 1], axis=0),
                                        in_=x1[:, t, :], in_offset=None).then_inc(scattered, 16)
            pool.wait_ge(scattered, 16 * NT)

            def load_slot(t, b):
                if not isinstance(t, int):
                    wait_apart(pool, xg_lo_done, t - 1)
                else:
                    at_least(pool, xg_lo_done, t - 1)
                pool.dma_start(xg[b][:, :, :], sorted_x_t[:, ds(t * TT, TT), :]).then_inc(xg_loaded[b], 16)

            def slot(t, b, k, ahead):
                if ahead and not (isinstance(t, int) and t == SLOTS_MOE - 2):
                    load_slot(t + 1, 1 - b)
                for tt in range(TT):
                    wait_apart(pool, y_done, TT * t + tt + 1)
                    pool.dma_start(sorted_y_t[:, ds(t * TT + tt, 1), :], y_sb[tt][:, :]).then_inc(y_stored[tt], 16)

            load_slot(0, 0)
            slot_loop(pool, slot)

            for tt in range(TT):
                pool.wait_ge(y_stored[tt], 16 * SLOTS_MOE)
            for t in range(NT):
                b = t % 2
                at_least(pool, res_done, t - 1)
                pool.indirect_dma_start(out=yg[b], out_offset=None, in_=sorted_y,
                                        in_offset=bass.IndirectOffsetOnAxis(ap=row_of[:, t:t + 1], axis=0)).then_inc(yg_loaded[b], 16)

        @block.scalar
        def _(act):
            act.wait_ge(wq_loaded, 16)
            act.activation(wq_hi[:, :, :], wf[:, :, :], ACT.Copy, scale=SCALE).then_inc(whi_done, 1)
            act.wait_ge(wo_loaded, 16)
            act.activation(wo_hi[:, :, :], wo_f, ACT.Copy, scale=SCALE).then_inc(whi_done, 1)
            act.wait_ge(wprep, 4)
            act.activation(wa_hi[:, :, :], wa[:, :, :], ACT.Copy, scale=SCALE).then_inc(whi_done, 1)
            act.wait_ge(consts0, 2)

            def std_and_cast(t, b, k):
                act.wait_ge(mv_done, t + 1)
                act.activation(std[b][:, :], mv[b][:, 1:2], ACT.Sqrt, bias=eps_col[:, :],
                               scale=1.0 / (SCALE * SCALE)).then_inc(std_done, 1)
                act.wait_ge(adj_loaded[b], 16 * (k + 1))
                at_least(act, atr_done, 2 * (t - 1))
                at_least(act, alone_done, t - 1)
                act.activation(adj_b[b][:, :], adj_in[b][:, :], ACT.Copy, accum_out=degree[b][:, :]).then_inc(cast_done, 1)

            def hi_and_copies(t, b):
                act.wait_ge(xs_done, t + 1)
                at_least(act, xtr_done, t - 1)
                act.activation(x_hl[b][:, 0, :], xs[b][:, :], ACT.Copy).then_inc(hi_done, 1)
                act.wait_ge(xtr_done, t + 1)
                at_least(act, s_done, t - 1)
                act.activation(xT[b][:, :, :, :].rearrange("p a b c -> p (a b c)"), bank[b].bitcast(fp16), ACT.Copy).then_inc(xT_done, 1)
                act.wait_ge(atr_done, 2 * t + 1)
                act.activation(adjT[:, 0:NT // 2, ds(t * P, P)],
                               bank[4].bitcast(bf16).rearrange("p (j c) -> p j c", c=P), ACT.Copy).then_inc(adjT_a, 1)

            def copy_vals(t, b):
                act.wait_ge(proj_done, t + 1)
                act.activation(vals[:, ds(t, 1), :], bank[2 + b], ACT.Copy, scale=UNSCALE).then_inc(vals_done, 1)

            def first_stage(t, b, k, ahead=True):
                if ahead:
                    std_and_cast(t + 1, 1 - b, k + b)
                hi_and_copies(t, b)
                if not isinstance(t, int) or t > 0:
                    copy_vals(t - 1, 1 - b)

            std_and_cast(0, 0, 0)
            first_stage(0, 0, 0)
            act.wait_ge(wlo_done, 3)
            first_stage(1, 1, 0)
            with act.Fori(1, NT // 2 - 1) as k:
                first_stage(2 * k, 0, k)
                first_stage(2 * k + 1, 1, k)
            first_stage(NT - 2, 0, NT // 2 - 1)
            first_stage(NT - 1, 1, NT // 2 - 1, ahead=False)
            copy_vals(NT - 1, 1)

            act.wait_ge(factors, 8)
            act.activation(fac_a[:, :, :], sa[:, :, :], ACT.Exp).then_inc(factors_act, 1)
            act.activation(fac_c[:, :, :], sc[:, :, :], ACT.Exp).then_inc(factors_act, 1)
            act.activation(fac_b[:, :, :], sy[:, :, :], ACT.Exp).then_inc(factors_act, 1)
            act.activation(fac_d[:, :, :], sy[:, :, :], ACT.Exp, scale=ALPHA).then_inc(factors_act, 1)
            act.wait_ge(factors_act, 4)
            act.wait_ge(factors, 9)

            with act.Fori(0, PAIRS) as p:
                made = 0
                for hh in range(2):
                    h = 2 * p + hh
                    act.activation(bias_now[hh][:, :], steep_bias[:, :, ds(h, 1)].rearrange("p t a -> p (t a)"), ACT.Copy).then_inc(bias_done, 1)
                    act.wait_ge(bias_done, h + 1)
                    act.wait_ge(s1_loaded[hh], 16 * (p + 1))
                    for half in range(2):
                        w = 2 * hh + half
                        for j in range(NT):
                            if j in FUSED:
                                continue
                            back = [(ww, jj) for ww in range(-1, w + 1) for jj in range(NT) if jj not in FUSED and (ww, jj) < (w, j)][-RING]
                            act.wait_ge(g_ready, G_BASE + 4 * NT * p + back[0] * NT + back[1] + 1)
                            ins = act.activation(steps[made % RING][:, :], s1row[hh][:, half * (N // 2):(half + 1) * (N // 2)],
                                                 ACT.Relu, bias=bias_now[hh][:, j:j + 1], scale=STEEP)
                            ins.then_inc(step_ready, 1)
                            made += 1

            def project(t, b):
                act.wait_ge(hn_done, t + 1)
                at_least(act, htr_done, t - 1)
                act.activation(h_hl[b][:, 0, :], hn[b][:, :], ACT.Copy, scale=SCALE).then_inc(h_hi_done, 1)
                act.wait_ge(htr_done, t + 1)
                at_least(act, out_mm, t - 1)
                act.activation(hT[b][:, :, :, :].rearrange("p a b c -> p (a b c)"), bank[b].bitcast(fp16), ACT.Copy).then_inc(hT_done, 1)

            def expo(t, b):
                act.wait_ge(zneg_done, t + 1)
                at_least(act, elu_done, t - 1)
                act.activation(ez[b][:, :], zneg[b][:, :], ACT.Exp).then_inc(ez_done, 1)

            def last_stage(t, b):
                project(t, b)
                if not isinstance(t, int) or t > 0:
                    expo(t - 1, 1 - b)

            def copy_x1T(t, b):
                act.wait_ge(x1tr_done, t + 1)
                act.activation(x1T[b][:, :, :].rearrange("p c q -> p (c q)"), bank[4 + b], ACT.Copy).then_inc(x1T_done, 1)

            last_stage(0, 0)
            last_stage(1, 1)
            with act.Fori(1, NT // 2) as k:
                t = 2 * k
                last_stage(t, 0)
                copy_x1T(t - 2, 0)
                last_stage(t + 1, 1)
                copy_x1T(t - 1, 1)
            expo(NT - 1, 1)
            copy_x1T(NT - 2, 0)
            copy_x1T(NT - 1, 1)
            act.wait_ge(mv2_done, NT)
            act.activation(std2[:, :].rearrange("p (t a) -> p t a", a=1), mv2[:, :, 1:2], ACT.Sqrt, bias=eps1[:, :]).then_inc(route_act, 1)
            act.wait_ge(route, EXP_AT)
            act.activation(expd[:, :, :], ctx_l[:, :, :], ACT.Exp).then_inc(route_act, 1)

            def chunk_hi(t, b, c, k):
                act.wait_ge(stage_loaded[c % 2], 16 * ((CH // 2) * t + c // 2 + 1))
                if c == 0:
                    at_least(act, down_mm, TT * (t - 1))
                dst = wbuf[b][0][:, c, :] if c < KC else wbuf[b][2][:, (c - KC) * KC:(c - KC + 1) * KC, :].rearrange("p q d -> p (q d)")
                act.activation(dst, stage[c % 2][:, :], ACT.Copy, scale=SCALE).then_inc(w_hi_done, 1)

            def tokens_hi(t, b, k):
                act.wait_ge(xg_loaded[b], 16 * (k + 1))
                at_least(act, xgtr_done, TT * t)
                act.activation(xg_hl[:, :, 0, :], xg[b][:, :, :], ACT.Copy, scale=SCALE).then_inc(xg_hi_done, 1)

            def tokens_T(t, b):
                act.wait_ge(xgtr_done, TT * t + 1)
                at_least(act, up_mm, FC * (t - 1))
                act.activation(xgT[b][:, :, :, 0:P].rearrange("p a c q -> p (a c) q"), bank[6].bitcast(fp16).rearrange("p (a q) -> p a q", q=P), ACT.Copy).then_inc(xgT_a, 1)

            def slot(t, b, k, ahead):
                act.wait_ge(bias_loaded[b], 32 * (k + 1))
                for f in range(FC):
                    act.wait_ge(up_mm, FC * t + f + 1)
                    at_least(act, hid_lo, FC * t + f - 3)
                    act.activation(hid[f % 4][:, :], bank[f % 4][:, 0:SLOT], ACT.Gelu_apprx_tanh, bias=b1_now[b][:, f:f + 1], scale=UNSCALE).then_inc(gelu_done, 1)
                    if ahead and f % 4 == 3:
                        chunk_hi(t + 1, 1 - b, f // 4, k)
                if ahead:
                    tokens_hi(t + 1, 1 - b, k + b)
                    for c in range(KC, CH):
                        chunk_hi(t + 1, 1 - b, c, k)
                    tokens_T(t + 1, 1 - b)

            for c in range(CH):
                chunk_hi(0, 0, c, 0)
            tokens_hi(0, 0, 0)
            tokens_T(0, 0)
            slot_loop(act, slot)

        @block.vector
        def _(dve):
            dve.sem_inc(g_ready, G_BASE)
            dve.wait_ge(wq_loaded, 16)
            dve.wait_ge(a_loaded, 32)
            wv = wf[:, :, :].rearrange("p c (h d) -> p (c h) d", d=DH)
            pv = wprod.rearrange("p c (h d) -> p (c h) d", d=DH)
            n = 0
            for i in range(2):
                n += 1
                chain(dve, wprep, dve.tensor_tensor(pv, wv, aw[:, i:i + 1, :].to_broadcast([P, KC * H, DH]), ALU.mult), n)
                n += 1
                chain(dve, wprep, dve.tensor_reduce(wa[:, :, i * H:(i + 1) * H], wprod.rearrange("p c (h d) -> p c h d", d=DH), X, ALU.add), n)
            dve.wait_ge(whi_done, 3)
            dve.scalar_tensor_tensor(wq_lo[:, :, :].rearrange("p c n -> p (c n)"), wf[:, :, :].rearrange("p c n -> p (c n)"), SCALE, wq_hi[:, :, :].rearrange("p c n -> p (c n)"), ALU.mult, ALU.subtract).then_inc(wlo_done, 1)
            dve.scalar_tensor_tensor(wa_lo[:, :, :], wa[:, :, :], SCALE, wa_hi[:, :, :], ALU.mult, ALU.subtract).then_inc(wlo_done, 1)
            dve.scalar_tensor_tensor(wo_lo[:, :, :], wo_f, SCALE, wo_hi[:, :, :], ALU.mult, ALU.subtract).then_inc(wlo_done, 1)

            def statistics(t, b, k):
                dve.wait_ge(x_loaded[b], 16 * (k + 1))
                dve.bn_stats(stats[b][:, :], x_in[b][:, :]).then_inc(stats_done, 1)
                at_least(dve, std_done, t - 1)
                wait_apart(dve, stats_done, t + 1)
                dve.bn_aggr(mv[b][:, :], stats[b][:, :]).then_inc(mv_done, 1)

            def normalise(t, b):
                dve.wait_ge(std_done, t + 1)
                dve.reciprocal(rstd[b][:, :], std[b][:, :]).then_inc(rstd_done, 1)
                dve.wait_ge(rstd_done, t + 1)
                at_least(dve, hi_done, t - 1)
                dve.tensor_scalar(xs[b][:, :], x_in[b][:, :], mv[b][:, 0:1], rstd[b][:, :], ALU.subtract, ALU.mult).then_inc(xs_done, 1)
                dve.wait_ge(cast_done, t + 1)
                dve.tensor_scalar(alone[b][:, :], degree[b][:, :], 0.5, None, ALU.is_lt).then_inc(alone_done, 1)
                dve.wait_ge(alone_done, t + 1)
                dve.tensor_scalar(adj_b[b][:, :], adj_b[b][:, :], alone[b][:, :], None, ALU.max).then_inc(amax_done, 1)
                dve.wait_ge(hi_done, t + 1)
                dve.tensor_tensor(x_hl[b][:, 1, :], xs[b][:, :], x_hl[b][:, 0, :], ALU.subtract).then_inc(lo_done, 1)

            def copy_adj(t):
                dve.wait_ge(atr_done, 2 * t + 2)
                dve.tensor_copy(adjT[:, NT // 2:NT, ds(t * P, P)], bank[5].bitcast(bf16).rearrange("p (j c) -> p j c", c=P)).then_inc(adjT_v, 1)

            def copy_scores(t, b):
                dve.wait_ge(s_done, t + 1)
                dve.tensor_scalar(s_tok[:, ds(t, 1), :], bank[6 + b][:, 0:2 * H], UNSCALE, None, ALU.mult).then_inc(s_copied, 1)
                dve.tensor_scalar(s_row[:, ds(t * P, P)], bank[6 + b][0:2 * H, P:2 * P], UNSCALE, None, ALU.mult).then_inc(s_copied, 1)

            def first_stage(t, b, k, ahead=True):
                if ahead:
                    statistics(t + 1, 1 - b, k + b)
                normalise(t, b)
                copy_adj(t)
                if not isinstance(t, int) or t > 0:
                    copy_scores(t - 1, 1 - b)

            statistics(0, 0, 0)
            first_stage(0, 0, 0)
            first_stage(1, 1, 0)
            with dve.Fori(1, NT // 2 - 1) as k:
                first_stage(2 * k, 0, k)
                first_stage(2 * k + 1, 1, k)
            first_stage(NT - 2, 0, NT // 2 - 1)
            first_stage(NT - 1, 1, NT // 2 - 1, ahead=False)
            copy_scores(NT - 1, 1)

            dve.wait_ge(s_copied, 2 * NT)
            chain(dve, factors, dve.reduce_max(top_row[:, :], s_row[:, :], X), 1)
            chain(dve, factors, dve.tensor_scalar(top_diag[:, :], identf[0:2 * H, 0:2 * H], top_row[:, :], None, ALU.mult), 2)
            dve.wait_ge(top_mm, 1)
            chain(dve, factors, dve.tensor_copy(top[:, :], bank[0][:, 0:2 * H]), 3)
            top2 = top[:, H:2 * H].rearrange("p (a h) -> p a h", a=1).to_broadcast([P, NT, H])
            chain(dve, factors, dve.tensor_tensor(sx[:, :, :], s_tok[:, :, 0:H], top2, ALU.add), 4)
            dve.tensor_scalar(sa[:, :, :], sx[:, :, :], 1.0 - ALPHA, 0.0, ALU.mult, ALU.min).then_inc(factors, 1)
            dve.tensor_scalar(sc[:, :, :], sx[:, :, :], ALPHA - 1.0, 0.0, ALU.mult, ALU.min).then_inc(factors, 1)
            dve.tensor_tensor(sy[:, :, :], s_tok[:, :, H:2 * H], top2, ALU.subtract).then_inc(factors, 1)
            dve.tensor_scalar(steep_bias[:, :, :], s_tok[:, :, H:2 * H], STEEP, None, ALU.mult).then_inc(factors, 1)
            dve.tensor_scalar(neg_s2[:, :, :], s_tok[:, :, H:2 * H], -1.0, None, ALU.mult).then_inc(factors, 1)
            dve.wait_ge(factors_act, 4)

            def copy_tails(pair, r):
                dst = tsum[:, ds((pair % 2) * (NT * 2 * C), NT * 2 * C)].rearrange("p (t g c) -> p t g c", t=NT, g=2)
                for g in range(2):
                    src = tails[:, :, g * Q * C:(g + 1) * Q * C].rearrange("p t (q c) -> p t c q", q=Q)
                    ins = dve.tensor_reduce(dst[:, 4 * r:4 * r + 4, g, :], src, X, ALU.add)
                ins.then_inc(t_free, 1)

            for r in range(4):
                dve.wait_ge(t_done, r + 1)
                copy_tails(0, r)

            def pair(p, ahead):
                made = 0
                for hh in range(2):
                    h = 2 * p + hh
                    dve.wait_ge(s1_loaded[hh], 16 * (p + 1))
                    for half in range(2):
                        w = 4 * p + 2 * hh + half
                        q0 = half * (N // 2)
                        for j in range(NT):
                            dve.wait_ge(g_used, NT * w + j + 1)
                            mask = adjT[:, j, q0:q0 + N // 2]
                            if j in FUSED:
                                ins = dve.scalar_tensor_tensor(gmask[j % RING][:, :], s1row[hh][:, q0:q0 + N // 2],
                                                               neg_s2[:, j, ds(h, 1)], mask, ALU.is_gt, ALU.mult)
                            else:
                                dve.wait_ge(step_ready, 4 * MADE * p + made + 1)
                                ins = dve.tensor_tensor(gmask[j % RING][:, :], steps[made % RING][:, :], mask, ALU.min)
                                made += 1
                            ins.then_inc(g_ready, 1)
                            if j == 5 and ahead:
                                dve.wait_ge(t_done, w + 5)
                                dve.wait_ge(comb_done, COMB_BASE + 4 * p)
                                copy_tails(p + 1, 2 * hh + half)
                        dve.wait_ge(g_used, RING + NT * (w + 1))
                        src = sums[:, :, 0:Q * BD].rearrange("p t (q c) -> p t c q", q=Q)
                        at_least(dve, comb_done, w)
                        dve.tensor_reduce(ssum[half][:, :, :], src, X, ALU.add).then_inc(sum_used, 1)

            pair(0, True)
            with dve.Fori(1, PAIRS - 1) as p:
                pair(p, True)
            pair(PAIRS - 1, False)

            def hidden(t, b):
                dve.reciprocal(rden[b][:, :], den[:, ds(t, 1), :].rearrange("p a h -> p (a h)")).then_inc(rden_done, 1)
                dve.wait_ge(rden_done, t + 1)
                at_least(dve, h_hi_done, t - 1)
                dve.tensor_tensor(hn[b][:, :].rearrange("p (h d) -> p h d", d=DH),
                                  vals[:, ds(t, 1), :].rearrange("p a (h d) -> p (a h) d", d=DH),
                                  rden[b][:, :].rearrange("p (h a) -> p h a", a=1).to_broadcast([P, H, DH]), ALU.mult).then_inc(hn_done, 1)
                dve.wait_ge(h_hi_done, t + 1)
                dve.scalar_tensor_tensor(h_hl[b][:, 1, :], hn[b][:, :], SCALE, h_hl[b][:, 0, :], ALU.mult, ALU.subtract).then_inc(h_lo_done, 1)

            def pre_elu(t, b):
                at_least(dve, x1_done, t - 1)
                dve.wait_ge(out_mm, t + 1)
                dve.scalar_tensor_tensor(z[b][:, :], bank[2 + b], UNSCALE, bo_bc[:, :], ALU.mult, ALU.add).then_inc(z_done, 1)
                dve.wait_ge(z_done, t + 1)
                dve.tensor_scalar(zneg[b][:, :], z[b][:, :], 0.0, None, ALU.min).then_inc(zneg_done, 1)

            def residual(t, b, k):
                dve.wait_ge(ez_done, t + 1)
                dve.scalar_tensor_tensor(z[b][:, :], z[b][:, :], 0.0, ez[b][:, :], ALU.max, ALU.add).then_inc(elu_done, 1)
                dve.wait_ge(elu_done, t + 1)
                dve.wait_ge(px_loaded[b], 16 * (k + 1))
                at_least(dve, x1_kept, t - 1)
                at_least(dve, x1tr_done, t - 1)
                dve.scalar_tensor_tensor(x1_now[b][:, :], z[b][:, :], -1.0, px[b][:, :], ALU.add, ALU.add).then_inc(x1_done, 1)
                dve.wait_ge(x1_done, t + 1)
                dve.bn_stats(stats2[:, ds(t, 1), :].rearrange("p a d -> p (a d)"), x1_now[b][:, :]).then_inc(bn2_done, 1)

            dve.wait_ge(comb_done, COMB_BASE + 2 * H)
            dve.wait_ge(bo_loaded, 16)
            def last_stage(t, b, k):
                hidden(t, b)
                if not isinstance(t, int) or t > 0:
                    pre_elu(t - 1, 1 - b)
                if not isinstance(t, int) or t > 1:
                    residual(t - 2, b, k - 1)

            for t in range(4):
                last_stage(t, t % 2, t // 2)
            with dve.Fori(2, NT // 2) as k:
                last_stage(2 * k, 0, k)
                last_stage(2 * k + 1, 1, k)
            pre_elu(NT - 1, 1)
            residual(NT - 2, 0, NT // 2 - 1)
            residual(NT - 1, 1, NT // 2 - 1)

            steps_done = [0]

            def step(ins):
                steps_done[0] += 1
                chain(dve, route, ins, steps_done[0])

            def over_e(a):
                return a.rearrange("p (t a) -> p t a", a=1).to_broadcast([P, NT, E])

            def over_t(a):
                return a.rearrange("p (a e) -> p a e", a=1).to_broadcast([P, NT, E])

            dve.wait_ge(bn2_done, NT)
            for t in range(NT):
                dve.bn_aggr(mv2[:, t, :], stats2[:, t, :]).then_inc(mv2_done, 1)
            dve.wait_ge(srw_mm, 1)
            step(dve.tensor_copy(rw_sum[:, :], bank[7][:, 0:E]))
            dve.wait_ge(logit_mm, NT)
            dve.wait_ge(mv2_done, NT)
            step(dve.tensor_tensor(shift[:, :, :], mv2[:, :, 0:1].to_broadcast([P, NT, E]), over_t(rw_sum[:, :]), ALU.mult))
            step(dve.tensor_tensor(raw[:, :, :], bank[6][:, 0:NT * E].rearrange("p (t e) -> p t e", e=E), shift[:, :, :], ALU.subtract))
            dve.wait_ge(route_act, 1)
            step(dve.reciprocal(rstd2[:, :], std2[:, :]))
            step(dve.tensor_tensor(logit[:, :, :], raw[:, :, :], over_e(rstd2[:, :]), ALU.mult))
            assert steps_done[0] == LOGITS_AT

            def running(mm, src_all, src_tile):
                dve.wait_ge(route_mm, mm)
                step(dve.tensor_copy(upto[:, :, :], src_tile.rearrange("p (t e) -> p t e", e=E)))
                step(dve.tensor_copy(shift[:, :, :], src_all.rearrange("p (t e) -> p t e", e=E)))
                for e in range(E):
                    step(dve.tensor_tensor_scan(before[:, :, e], zero_t[:, :], shift[:, :, e], 0.0, ALU.add, ALU.add))
                step(dve.tensor_tensor(raw[:, :, :], before[:, :, :], shift[:, :, :], ALU.subtract))
                step(dve.tensor_tensor(upto[:, :, :], upto[:, :, :], raw[:, :, :], ALU.add))

            step(dve.memset(zero_t[:, :], 0.0))
            running(1, bank[1][:, 0:NT * E], bank[0][:, 0:NT * E])
            step(dve.reciprocal(total[:, :], token_no[:, :]))
            step(dve.tensor_tensor(ctx_l[:, :, :], upto[:, :, :], over_e(total[:, :]), ALU.mult))
            step(dve.reduce_max(largest[:, :], ctx_l[:, :, :], X))
            step(dve.tensor_tensor(ctx_l[:, :, :], ctx_l[:, :, :], over_e(largest[:, :]), ALU.subtract))
            assert steps_done[0] == EXP_AT
            step(dve.tensor_scalar(same[:, :, :], ctx_l[:, :, :], 0.0, None, ALU.is_equal))
            step(dve.tensor_copy(onehot[:, :, 0], same[:, :, 0]))
            step(dve.tensor_copy(seen[:, :], same[:, :, 0]))
            for e in range(1, E):
                step(dve.tensor_tensor(onehot[:, :, e], same[:, :, e], seen[:, :], ALU.is_gt))
                if e < E - 1:
                    step(dve.tensor_tensor(seen[:, :], seen[:, :], same[:, :, e], ALU.max))
            assert steps_done[0] == ONEHOT_AT
            dve.wait_ge(route_act, 2)
            step(dve.reduce_sum(total[:, :], expd[:, :, :], X))
            step(dve.reciprocal(gate[:, :], total[:, :]))
            running(2, bank[3][:, 0:NT * E], bank[2][:, 0:NT * E])
            counts = before[:, NT - 1, :]
            step(dve.tensor_tensor(above[:, :, :], counts.rearrange("p (e a) -> p e a", a=1).to_broadcast([P, E, N // SLOT]),
                                   slot_low[:, :].rearrange("p (a s) -> p a s", a=1).to_broadcast([P, E, N // SLOT]), ALU.is_gt))
            step(dve.reduce_sum(n_slots[:, :], above[:, :, :], X))
            step(dve.tensor_tensor_scan(last_slot[:, :], zero_t[:, 0:E], n_slots[:, :], 0.0, ALU.add, ALU.add))
            step(dve.tensor_tensor(first_row[:, :], last_slot[:, :], n_slots[:, :], ALU.subtract))
            step(dve.tensor_scalar(first_row[:, :], first_row[:, :], float(SLOT), -1.0, ALU.mult, ALU.add))
            step(dve.tensor_tensor(upto[:, :, :], upto[:, :, :], over_t(first_row[:, :]), ALU.add))
            step(dve.tensor_tensor(upto[:, :, :], upto[:, :, :], onehot[:, :, :], ALU.mult))
            step(dve.reduce_sum(total[:, :], upto[:, :, :], X))
            step(dve.tensor_copy(row_of[:, :], total[:, :]))
            step(dve.tensor_tensor(past[:, :, :], slot_no[:, :].rearrange("p (s a) -> p s a", a=1).to_broadcast([P, SLOTS_MOE, E - 1]),
                                   last_slot[:, 0:E - 1].rearrange("p (a e) -> p a e", a=1).to_broadcast([P, SLOTS_MOE, E - 1]), ALU.is_ge))
            step(dve.reduce_sum(slot_f[:, :], past[:, :, :], X))
            step(dve.tensor_copy(expert_of[:, :], slot_f[:, :]))
            assert steps_done[0] == ROUTE_STEPS

            dve.wait_ge(x1_stored, 16 * NT)
            dve.wait_ge(x1tr_done, NT)
            for t in range(NT):
                dve.tensor_scalar(x1[:, t, :], x1[:, t, :], mv2[:, t, 0:1], rstd2[:, t:t + 1], ALU.subtract, ALU.mult).then_inc(xn_done, 1)

            def chunk_lo(t, b, c):
                dve.wait_ge(w_hi_done, CH * t + c + 1)
                if c < KC:
                    hi, lo = wbuf[b][0][:, c, :], wbuf[b][1][:, c, :]
                else:
                    hi, lo = (wbuf[b][i][:, (c - KC) * KC:(c - KC + 1) * KC, :].rearrange("p q d -> p (q d)") for i in (2, 3))
                dve.scalar_tensor_tensor(lo, stage[c % 2][:, :], SCALE, hi, ALU.mult, ALU.subtract).then_inc(w_lo_done, 1)

            def tokens_lo(t, b):
                dve.wait_ge(xg_hi_done, t + 1)
                dve.scalar_tensor_tensor(xg_hl[:, :, 1, :], xg[b][:, :, :], SCALE, xg_hl[:, :, 0, :], ALU.mult, ALU.subtract).then_inc(xg_lo_done, 1)

            def tokens_T(t, b):
                dve.wait_ge(xgtr_done, TT * t + 2)
                dve.tensor_copy(xgT[b][:, :, :, P:2 * P].rearrange("p a c q -> p (a c) q"), bank[7].bitcast(fp16).rearrange("p (a q) -> p a q", q=P)).then_inc(xgT_v, 1)

            def copy_y(t, tt, b):
                dve.wait_ge(down_mm, TT * t + tt + 1)
                at_least(dve, y_stored[tt], 16 * t)
                dve.scalar_tensor_tensor(y_sb[tt][:, :], bank[4 + tt], 1.0 / (SCALE * HSCALE), b2_now[b][:, :], ALU.mult, ALU.add).then_inc(y_done, 1)

            def slot(t, b, k, ahead):
                for f in range(FC):
                    n = FC * t + f
                    dve.wait_ge(gelu_done, n + 1)
                    if f == 0:
                        at_least(dve, down_mm, TT * t)
                    dve.tensor_scalar(hidT[:, 0, f, :], hid[f % 4][:, :], HSCALE, None, ALU.mult).then_inc(hid_hi, 1)
                    dve.wait_ge(hid_hi, n + 1)
                    dve.scalar_tensor_tensor(hidT[:, 1, f, :], hid[f % 4][:, :], HSCALE, hidT[:, 0, f, :], ALU.mult, ALU.subtract).then_inc(hid_lo, 1)
                    if ahead and f % 4 == 3:
                        chunk_lo(t + 1, 1 - b, f // 4)
                if ahead:
                    tokens_lo(t + 1, 1 - b)
                    for c in range(KC, CH - 1):
                        chunk_lo(t + 1, 1 - b, c)
                copy_y(t, 0, b)
                if ahead:
                    chunk_lo(t + 1, 1 - b, CH - 1)
                    tokens_T(t + 1, 1 - b)
                copy_y(t, 1, b)

            for c in range(CH):
                chunk_lo(0, 0, c)
            tokens_lo(0, 0)
            tokens_T(0, 0)
            slot_loop(dve, slot)

            for t in range(NT):
                b = t % 2
                dve.wait_ge(yg_loaded[b], 16 * (t // 2 + 1))
                dve.wait_ge(x1r_loaded[b], 16 * (t // 2 + 1))
                at_least(dve, out_stored[b], 16 * (t // 2))
                dve.scalar_tensor_tensor(res[b], yg[b], gate[:, t:t + 1], x1r[b], ALU.mult, ALU.add).then_inc(res_done, 1)

        @block.tensor
        def _(pe):
            pe.wait_ge(consts, 7)

            def transposes(t, b):
                pe.wait_ge(lo_done, t + 1)
                at_least(pe, xT_done, t - 1)
                dst = bank[b].bitcast(fp16)
                for i in range(2 * KC):
                    ins = pe.transpose(dst[:, i * P:(i + 1) * P], x_hl[b][:, i // KC, (i % KC) * P:(i % KC + 1) * P], ident16[:, :])
                ins.then_inc(xtr_done, 1)
                pe.wait_ge(amax_done, t + 1)
                for half, copied in enumerate((adjT_a, adjT_v)):
                    at_least(pe, copied, t)
                    dst = bank[4 + half].bitcast(bf16)
                    for i in range(NT // 2):
                        j = half * (NT // 2) + i
                        ins = pe.transpose(dst[:, i * P:(i + 1) * P], adj_b[b][:, j * P:(j + 1) * P], identb[:, :])
                    ins.then_inc(atr_done, 1)

            def products(t, b):
                pe.wait_ge(xT_done, t + 1)
                at_least(pe, vals_done, t - 1)
                at_least(pe, s_copied, 2 * (t - 1))
                terms = [(c, s, w) for c in range(KC) for s, w in ((0, 0), (0, 1), (1, 0))]
                for i, (c, s, w) in enumerate(terms):
                    first, last = i == 0, i == len(terms) - 1
                    ins = pe.matmul(bank[2 + b], xT[b][:, s, c, :], (wq_hi, wq_lo)[w][:, c, :], start=first, stop=last)
                ins.then_inc(proj_done, 1)
                for i, (c, s, w) in enumerate(terms):
                    first, last = i == 0, i == len(terms) - 1
                    pe.matmul(bank[6 + b][:, 0:2 * H], xT[b][:, s, c, :], (wa_hi, wa_lo)[w][:, c, :], start=first, stop=last)
                for i, (c, s, w) in enumerate(terms):
                    first, last = i == 0, i == len(terms) - 1
                    ins = pe.matmul(bank[6 + b][0:2 * H, P:2 * P], (wa_hi, wa_lo)[w][:, c, :], xT[b][:, s, c, :], start=first, stop=last)
                ins.then_inc(s_done, 1)

            transposes(0, 0)
            pe.wait_ge(wlo_done, 3)
            transposes(1, 1)
            products(0, 0)
            with pe.Fori(1, NT // 2) as k:
                t = 2 * k
                transposes(t, 0)
                products(t - 1, 1)
                transposes(t + 1, 1)
                products(t, 0)
            products(NT - 1, 1)

            pe.wait_ge(factors, 2)
            pe.matmul(bank[0][:, 0:2 * H], ones[0:2 * H, :], top_diag[:, :], start=True, stop=True).then_inc(top_mm, 1)

            def all_neighbours(pair, r):
                src = bd[:, ds((pair % 3) * (2 * NT * Q * BD), 2 * NT * Q * BD)].rearrange("p (g t q c) -> p t g q c", g=2, t=NT, q=Q)
                for i in range(4):
                    it = 4 * r + i
                    for j in range(NT):
                        ins = pe.matmul(tails[:, i, 0:2 * Q * C], adjT[:, j, it * P:(it + 1) * P], src[:, j, :, :, C:BD],
                                        start=(j == 0 and i % 2 == 0), stop=(j == NT - 1), skip_group_check=True)
                ins.then_inc(t_done, 1)

            pe.wait_ge(bd_chain, 2 * BD_STEPS)
            pe.wait_ge(adjT_a, NT)
            pe.wait_ge(adjT_v, NT)
            for r in range(4):
                if r:
                    pe.wait_ge(t_free, r)
                all_neighbours(0, r)
            pe.sem_inc(g_used, RING)

            def pair(p, ahead):
                if ahead:
                    pe.wait_ge(bd_chain, BD_STEPS * (2 * p + 4))
                for hh in range(2):
                    src = bd[:, ds((p % 3) * (2 * NT * Q * BD) + hh * (NT * Q * BD), NT * Q * BD)].rearrange("p (t c) -> p t c", t=NT)
                    for half in range(2):
                        w = 4 * p + 2 * hh + half
                        if ahead:
                            pe.wait_ge(t_free, w + 4)
                            all_neighbours(p + 1, 2 * hh + half)
                        at_least(pe, sum_used, w)
                        for j in range(NT):
                            pe.wait_ge(g_ready, G_BASE + NT * w + j + 1)
                            for i in range(HALF):
                                ins = pe.matmul(sums[:, i, 0:Q * BD], gmask[j % RING][:, i * P:(i + 1) * P], src[:, j, :],
                                                start=(j == 0 and i % 2 == 0), stop=(j == NT - 1), skip_group_check=True)
                            ins.then_inc(g_used, 1)

            pair(0, True)
            with pe.Fori(1, PAIRS - 1) as p:
                pair(p, True)
            pair(PAIRS - 1, False)

            def h_transposes(t, b):
                pe.wait_ge(h_lo_done, t + 1)
                at_least(pe, hT_done, t - 1)
                dst = bank[b].bitcast(fp16)
                for i in range(2 * KC):
                    ins = pe.transpose(dst[:, i * P:(i + 1) * P], h_hl[b][:, i // KC, (i % KC) * P:(i % KC + 1) * P], ident16[:, :])
                ins.then_inc(htr_done, 1)

            def out_products(t, b):
                pe.wait_ge(hT_done, t + 1)
                at_least(pe, z_done, t - 1)
                terms = [(c, s, w) for c in range(KC) for s, w in ((0, 0), (0, 1), (1, 0))]
                for i, (c, s, w) in enumerate(terms):
                    ins = pe.matmul(bank[2 + b], hT[b][:, s, c, :], (wo_hi, wo_lo)[w][:, c, :], start=(i == 0), stop=(i == len(terms) - 1))
                ins.then_inc(out_mm, 1)

            def x1_transposes(t, b):
                pe.wait_ge(x1_done, t + 1)
                at_least(pe, x1T_done, t - 1)
                for c in range(KC):
                    ins = pe.transpose(bank[4 + b][:, c * P:(c + 1) * P], x1_now[b][:, c * P:(c + 1) * P], identf[:, :])
                ins.then_inc(x1tr_done, 1)

            def logits(t, b):
                pe.wait_ge(x1T_done, t + 1)
                for c in range(KC):
                    ins = pe.matmul(bank[6][:, ds(t * E, E)], x1T[b][:, c, :], rw[:, c, :], start=(c == 0), stop=(c == KC - 1))
                ins.then_inc(logit_mm, 1)

            pe.wait_ge(rw_loaded, 16)
            for c in range(KC):
                ins = pe.matmul(bank[7][:, 0:E], ones[:, :], rw[:, c, :], start=(c == 0), stop=(c == KC - 1))
            ins.then_inc(srw_mm, 1)
            def last_stage(t, b):
                h_transposes(t, b)
                if not isinstance(t, int) or t > 0:
                    out_products(t - 1, 1 - b)
                if not isinstance(t, int) or t > 1:
                    x1_transposes(t - 2, b)
                if not isinstance(t, int) or t > 2:
                    logits(t - 3, 1 - b)

            for t in range(4):
                last_stage(t, t % 2)
            with pe.Fori(2, NT // 2) as k:
                last_stage(2 * k, 0)
                last_stage(2 * k + 1, 1)
            logits(NT - 3, 1)
            out_products(NT - 1, 1)
            for t in (NT - 2, NT - 1):
                x1_transposes(t, t % 2)
                logits(t, t % 2)

            for i, (src, known) in enumerate(((logit, LOGITS_AT), (onehot, ONEHOT_AT))):
                pe.wait_ge(route, known)
                flat = src[:, :, :].rearrange("p t e -> p (t e)")
                pe.matmul(bank[2 * i][:, 0:NT * E], tri[:, :], flat, start=True, stop=True)
                pe.matmul(bank[2 * i + 1][:, 0:NT * E], ones[:, :], flat, start=True, stop=True).then_inc(route_mm, 1)

            def token_transposes(t):
                pe.wait_ge(xg_lo_done, t + 1)
                for tt, copied in enumerate((xgT_a, xgT_v)):
                    at_least(pe, copied, t)
                    dst = bank[6 + tt].bitcast(fp16)
                    for i in range(2 * KC):
                        ins = pe.transpose(dst[:, i * P:(i + 1) * P], xg_hl[:, tt, i // KC, (i % KC) * P:(i % KC + 1) * P], ident16[:, :])
                    ins.then_inc(xgtr_done, 1)

            def slot(t, b, k, ahead):
                w1_hi, w1_lo, w2_hi, w2_lo = wbuf[b]
                pe.wait_ge(xgT_a, t + 1)
                pe.wait_ge(xgT_v, t + 1)
                pe.wait_ge(w_lo_done, CH * t + KC)
                for f in range(FC):
                    at_least(pe, gelu_done, FC * t + f - 3)
                    terms = [(w, c, s) for c in range(KC) for w, s in ((w1_hi, 0), (w1_hi, 1), (w1_lo, 0))]
                    for i, (w, c, s) in enumerate(terms):
                        ins = pe.matmul(bank[f % 4][:, 0:SLOT], w[:, c, f * P:(f + 1) * P], xgT[b][:, s, c, :], start=(i == 0), stop=(i == len(terms) - 1))
                    ins.then_inc(up_mm, 1)
                pe.wait_ge(w_lo_done, CH * t + CH)
                for tt in range(TT):
                    if tt == 1 and ahead:
                        token_transposes(t + 1)
                    at_least(pe, y_done, TT * t + tt - 1)
                    for f in range(FC):
                        if tt == 0:
                            pe.wait_ge(hid_lo, FC * t + f + 1)
                        for i, (s, w) in enumerate(((0, w2_hi), (0, w2_lo), (1, w2_hi))):
                            ins = pe.matmul(bank[4 + tt], hidT[:, s, f, tt * P:(tt + 1) * P], w[:, f, :], start=(f == 0 and i == 0), stop=(f == FC - 1 and i == 2))
                    ins.then_inc(down_mm, 1)

            token_transposes(0)
            slot_loop(pe, slot)


_INS = ['x', 'adj', 'L0_gnn_W_seq', 'L0_gnn_a1', 'L0_gnn_a2', 'L0_gnn_W_out', 'L0_gnn_b_out', 'L0_ffn_router_w',
        'L0_ffn_w1', 'L0_ffn_b1', 'L0_ffn_w2', 'L0_ffn_b2']
_OUTS = [((2048, 512), 'float32')]


def kernel(**inputs):
    import numpy as _np
    import concourse.bacc as _bacc
    from concourse import mybir as _mybir
    from concourse.bass_utils import run_bass_kernel_spmd as _run

    nc = _bacc.Bacc("TRN2", target_bir_lowering=False, num_devices=1)
    arrays, args = {}, []
    for name in _INS:
        a = _np.ascontiguousarray(inputs[name])
        arrays[f"in_{name}_dram"] = a
        args.append(nc.dram_tensor(f"in_{name}_dram", a.shape, _mybir.dt.from_np(a.dtype), kind="ExternalInput").ap())
    for i, (shape, dtype) in enumerate(_OUTS):
        dt = _mybir.dt.from_np(_np.dtype(dtype))
        args.append(nc.dram_tensor(f"out_{i}_dram", shape, dt, kind="ExternalOutput").ap())
    gat_moe_kernel(nc, *args)
    r = _run(nc, [arrays], core_ids=[0])
    return r.results[0]["out_0_dram"]
```

```python
import concourse.bass as bass
from concourse import mybir
from contextlib import ExitStack


def gat_moe_kernel(nc, x, adj, w_seq, a1, a2, w_out, b_out, router_w, w1, b1, w2, b2, out):
    fp32, fp16, bf16, i32 = mybir.dt.float32, mybir.dt.float16, mybir.dt.bfloat16, mybir.dt.int32
    ALU = mybir.AluOpType
    ACT = mybir.ActivationFunctionType
    X = mybir.AxisListType.X
    ds = bass.ds

    P = 128
    N, D = x.shape
    DH = a1.shape[0]
    H = D // DH
    NT = N // P
    KC = D // P
    C = DH + 1
    BD = 2 * C
    Q = 3
    ALPHA = 0.2
    EPS = 1e-5

    SCALE = 256.0
    UNSCALE = 1.0 / (SCALE * SCALE)
    STEEP = 2.0 ** 100

    PAIRS = H // 2
    HALF = NT // 2
    SLOTS = 6
    RING = 4
    G_RING = 8
    COMB_BASE = 1
    BD_STEPS = 8
    LOGITS_AT = 5
    EXP_AT = LOGITS_AT + 8
    ONEHOT_AT = EXP_AT + 7
    ROUTE_STEPS = ONEHOT_AT + 18
    FUSED = (5, 13)
    MADE = NT - len(FUSED)
    G_BASE = 2 * NT

    E, F = b1.shape
    FC = F // P
    SLOT = 2 * P
    TT = SLOT // P
    SLOTS_MOE = (N + E * (SLOT - 1)) // SLOT
    CH = 2 * KC
    HSCALE = 64.0

    ctx = ExitStack()
    with ctx:
        at = [16512]

        def sb(name, shape, dt, offset=None):
            size = {fp32: 4, i32: 4, fp16: 2, bf16: 2}[dt]
            for n in shape[1:]:
                size *= n
            if offset is None:
                offset = at[0]
                at[0] += (size + 31) // 32 * 32
            return nc.alloc_sbuf_tensor_at(name, shape, dt, offset=offset)

        ident16 = sb("ident16", [P, P], fp16)
        identb = sb("identb", [P, P], bf16)
        identf = sb("identf", [P, P], fp32)
        ones = sb("ones", [P, P], fp32)
        eps_col = sb("eps_col", [P, 1], fp32)
        rw = sb("rw", [P, KC, E], fp32)
        rw_sum = sb("rw_sum", [P, E], fp32)
        mv2 = sb("mv2", [P, NT, 2], fp32)
        std2 = sb("std2", [P, NT], fp32)
        rstd2 = sb("rstd2", [P, NT], fp32)
        token_no = sb("token_no", [P, NT], fp32)
        slot_no = sb("slot_no", [P, SLOTS_MOE], fp32)
        slot_low = sb("slot_low", [P, E, N // SLOT], fp32)
        per_token = sb("per_token", [P, NT], fp32)
        zero_t = sb("zero_t", [P, NT], fp32)
        after = sb("after", [P, P], fp32)
        gate = sb("gate", [P, NT], fp32)
        row_of = sb("row_of", [P, NT], i32)
        expert_of = sb("expert_of", [P, SLOTS_MOE], i32)
        b1_all = sb("b1_all", [P, E * FC], fp32)
        b1_now = [sb(f"b1_now{b}", [P, FC], fp32) for b in range(2)]
        eps1 = sb("eps1", [P, 1], fp32)
        fac_a = sb("fac_a", [P, NT, H], fp32)
        fac_c = sb("fac_c", [P, NT, H], fp32)
        den = sb("den", [P, NT, H], fp32)
        routing_region = at[0]
        steep_bias = sb("steep_bias", [P, NT, H], fp32)
        neg_s2 = sb("neg_s2", [P, NT, H], fp32)
        fac_b = sb("fac_b", [P, NT, H], fp32)
        fac_d = sb("fac_d", [P, NT, H], fp32)
        bias_now = [sb(f"bias_now{b}", [P, NT], fp32) for b in range(2)]
        w0_region = at[0]
        adjT = sb("adjT", [P, NT, N], bf16)
        vals = sb("vals", [P, NT, D], fp32)
        bd_region = at[0]
        bd = sb("bd", [P, SLOTS * NT * Q * BD], bf16)
        tsum = sb("tsum", [P, 2 * NT * 2 * C], fp32)
        s1row = [sb(f"s1row{b}", [P, N], fp32) for b in range(2)]
        gr_region = at[0]
        gmask = [sb(f"gmask{i}", [P, N // 2], bf16) for i in range(G_RING)]
        steps = [sb(f"steps{i}", [P, N // 2], bf16) for i in range(RING)]
        bdf = sb("bdf", [P, NT, BD], fp32)
        branch_a = sb("branch_a", [P, HALF, C], fp32)
        branch_c = sb("branch_c", [P, HALF, C], fp32)
        sums_region = at[0]
        ssum = [sb(f"ssum{b}", [P, HALF, BD], fp32) for b in range(2)]
        assert at[0] <= 229344, at[0]
        attention_end = at[0]
        bdf_first = sb("bdf_first", [P, NT, BD], fp32, offset=sums_region)
        zeros = sb("zeros", [P, D], fp32)
        assert at[0] <= 229344, at[0]
        stage_region = 229344 - 2 * 4 * F

        at[0] = bd_region
        x_in = [sb(f"x_in{b}", [P, D], fp32) for b in range(2)]
        adj_in = [sb(f"adj_in{b}", [P, N], fp32) for b in range(2)]
        adj_b = [sb(f"adj_b{b}", [P, N], bf16) for b in range(2)]
        xs = [sb(f"xs{b}", [P, D], fp32) for b in range(2)]
        x_hl = [sb(f"x_hl{b}", [P, 2, D], fp16) for b in range(2)]
        xT = [sb(f"xT{b}", [P, 2, KC, P], fp16) for b in range(2)]
        stats = [sb(f"stats{b}", [P, 6], fp32) for b in range(2)]
        mv = [sb(f"mv{b}", [P, 2], fp32) for b in range(2)]
        std = [sb(f"std{b}", [P, 1], fp32) for b in range(2)]
        rstd = [sb(f"rstd{b}", [P, 1], fp32) for b in range(2)]
        degree = [sb(f"degree{b}", [P, 1], fp32) for b in range(2)]
        alone = [sb(f"alone{b}", [P, 1], fp32) for b in range(2)]
        wf = sb("wf", [P, KC, D], fp32)
        wq_hi = sb("wq_hi", [P, KC, D], fp16)
        wq_lo = sb("wq_lo", [P, KC, D], fp16)
        aw = sb("aw", [P, 2, DH], fp32)
        wa = sb("wa", [P, KC, 2 * H], fp32)
        wa_hi = sb("wa_hi", [P, KC, 2 * H], fp16)
        wa_lo = sb("wa_lo", [P, KC, 2 * H], fp16)
        assert at[0] <= gr_region
        at[0] = gr_region
        s_row = sb("s_row", [2 * H, N], fp32)
        s_tok = sb("s_tok", [P, NT, 2 * H], fp32)
        top_row = sb("top_row", [2 * H, 1], fp32)
        top_diag = sb("top_diag", [2 * H, 2 * H], fp32)
        top = sb("top", [P, 2 * H], fp32)
        sx = sb("sx", [P, NT, H], fp32)
        sa = sb("sa", [P, NT, H], fp32)
        sc = sb("sc", [P, NT, H], fp32)
        sy = sb("sy", [P, NT, H], fp32)
        assert at[0] <= attention_end
        wprod = [vals[:, i * KC:(i + 1) * KC, :] for i in range(2)]

        at[0] = bd_region
        wo_f = sb("wo_f", [P, KC, D], fp32, offset=bd_region)
        hT = [sb(f"hT{b}", [P, 2, KC, P], fp16) for b in range(2)]
        px = [sb(f"px{b}", [P, D], fp32) for b in range(2)]
        assert at[0] == bd_region + 4 * KC * D
        hn = [sb(f"hn{b}", [P, D], fp32) for b in range(2)]
        h_hl = [sb(f"h_hl{b}", [P, 2, D], fp16) for b in range(2)]
        rden = [sb(f"rden{b}", [P, H], fp32) for b in range(2)]
        z = [sb(f"z{b}", [P, D], fp32) for b in range(2)]
        zneg = [sb(f"zneg{b}", [P, D], fp32) for b in range(2)]
        assert (PAIRS - 1) % 3 == 1
        assert at[0] <= bd_region + 4 * (2 * NT * Q * BD)
        at[0] = bd_region + 4 * (2 * NT * Q * BD)
        wo_hi = sb("wo_hi", [P, KC, D], fp16)
        wo_lo = sb("wo_lo", [P, KC, D], fp16)
        bo_bc = sb("bo_bc", [P, D], fp32)
        assert at[0] <= bd_region + 6 * (2 * NT * Q * BD)
        ez = [sb(f"ez{b}", [P, D], fp32) for b in range(2)]
        x1 = sb("x1", [P, NT, D], fp32)
        x1_now = [sb(f"x1_now{b}", [P, D], fp32) for b in range(2)]
        x1T = [sb(f"x1T{b}", [P, KC, P], fp32) for b in range(2)]
        stats2 = sb("stats2", [P, NT, 6], fp32)
        assert at[0] <= stage_region
        at[0] = stage_region
        stage = [sb(f"stage{b}", [P, F], fp32) for b in range(2)]

        at[0] = routing_region
        raw = sb("raw", [P, NT, E], fp32)
        shift = sb("shift", [P, NT, E], fp32)
        logit = sb("logit", [P, NT, E], fp32)
        upto = sb("upto", [P, NT, E], fp32)
        before = sb("before", [P, NT, E], fp32)
        ctx_l = sb("ctx_l", [P, NT, E], fp32)
        expd = sb("expd", [P, NT, E], fp32)
        same = sb("same", [P, NT, E], fp32)
        onehot = sb("onehot", [P, NT, E], fp32)
        seen = sb("seen", [P, NT, E], fp32)
        largest = sb("largest", [P, NT], fp32)
        total = sb("total", [P, NT], fp32)
        above = sb("above", [P, E, N // SLOT], fp32)
        slot_f = sb("slot_f", [P, SLOTS_MOE], fp32)
        n_slots = sb("n_slots", [P, E], fp32)
        last_slot = sb("last_slot", [P, E], fp32)
        first_slot = sb("first_slot", [P, E], fp32)
        past = sb("past", [P, SLOTS_MOE, E - 1], fp32)
        assert at[0] <= w0_region

        assert w0_region + 2 * 8 * KC * F // 2 <= bd_region + 4 * NT * D
        wbuf = []
        for b in range(2):
            at[0] = w0_region + b * (8 * KC * F)
            wbuf.append([sb(f"w1_hi{b}", [P, KC, F], fp16), sb(f"w1_lo{b}", [P, KC, F], fp16),
                         sb(f"w2_hi{b}", [P, FC, D], fp16), sb(f"w2_lo{b}", [P, FC, D], fp16)])
        xg = [sb(f"xg{b}", [P, TT, D], fp32) for b in range(2)]
        xg_hl = sb("xg_hl", [P, TT, 2, D], fp16)
        xgT = [sb(f"xgT{b}", [P, 2, KC, SLOT], fp16) for b in range(2)]
        hidT = sb("hidT", [P, 2, FC, SLOT], fp16)
        hid = [sb(f"hid{i}", [P, SLOT], fp32) for i in range(4)]
        b2_now = [sb(f"b2_now{b}", [P, D], fp32) for b in range(2)]
        y_sb = [sb(f"y_sb{b}", [P, D], fp32) for b in range(2)]
        assert at[0] <= stage_region
        at[0] = w0_region + 8 * KC * F
        x1_back = sb("x1_back", [P, NT, D], fp32)
        y_back = sb("y_back", [P, NT, D], fp32)

        psum = ctx.enter_context(nc.psum_tensor("psum", [P, 8, 512], fp32))
        bank = [psum[:, i, :] for i in range(8)]
        sums = psum[:, 0:4, :].rearrange("p a (b c) -> p (a b) c", b=2)
        tails = psum[:, 4:6, :].rearrange("p a (b c) -> p (a b) c", b=2)

        sorted_x = nc.dram_tensor("sorted_x", [SLOTS_MOE * SLOT, D], fp32, kind="Internal").ap()
        sorted_y = nc.dram_tensor("sorted_y", [SLOTS_MOE * SLOT, D], fp32, kind="Internal").ap()
        x1_dram = nc.dram_tensor("x1_dram", [N, D], fp32, kind="Internal").ap()
        s1_dram = nc.dram_tensor("s1_dram", [H, N], fp32, kind="Internal").ap()

        def sem(name):
            return ctx.enter_context(nc.semaphore(name))

        passed = sem("passed")
        consts, consts0 = sem("consts"), sem("consts0")
        x_loaded = [sem(f"x_loaded{b}") for b in range(2)]
        adj_loaded = [sem(f"adj_loaded{b}") for b in range(2)]
        wq_loaded, wo_loaded, a_loaded, bo_loaded = sem("wq_loaded"), sem("wo_loaded"), sem("a_loaded"), sem("bo_loaded")
        wprod_done = sem("wprod_done")
        wprep = sem("wprep")
        whi_done = sem("whi_done")
        wlo_done = sem("wlo_done")
        stats_done, mv_done, std_done, rstd_done, xs_done = (sem(n) for n in ("stats_done", "mv_done", "std_done", "rstd_done", "xs_done"))
        hi_done, lo_done, xtr_done, xT_done = (sem(n) for n in ("hi_done", "lo_done", "xtr_done", "xT_done"))
        cast_done, alone_done, amax_done, atr_done, adjT_a, adjT_v = (sem(n) for n in ("cast_done", "alone_done", "amax_done", "atr_done", "adjT_a", "adjT_v"))
        proj_done, s_done, vals_done, s_copied = (sem(n) for n in ("proj_done", "s_done", "vals_done", "s_copied"))
        factors, top_mm, factors_act = sem("factors"), sem("top_mm"), sem("factors_act")
        s1_stored = sem("s1_stored")
        s1_loaded = [sem(f"s1_loaded{b}") for b in range(2)]
        bd_first = sem("bd_first")
        bd_chain = sem("bd_chain")
        bias_done = sem("bias_done")
        step_ready, g_ready, g_used = sem("step_ready"), sem("g_ready"), sem("g_used")
        t_done, t_free = sem("t_done"), sem("t_free")
        sum_used = sem("sum_used")
        comb, comb_done = sem("comb"), sem("comb_done")
        px_loaded = [sem(f"px_loaded{b}") for b in range(2)]
        rden_done, hn_done, h_hi_done, h_lo_done, htr_done, hT_done = (sem(n) for n in ("rden_done", "hn_done", "h_hi_done", "h_lo_done", "htr_done", "hT_done"))
        out_mm, z_done, zneg_done, ez_done, elu_done, x1_done = (sem(n) for n in ("out_mm", "z_done", "zneg_done", "ez_done", "elu_done", "x1_done"))
        rw_loaded, b1_loaded, cleared = sem("rw_loaded"), sem("b1_loaded"), sem("cleared")
        x1_stored, x1_kept = sem("x1_stored"), sem("x1_kept")
        bn2_done, mv2_done, x1tr_done, x1T_done, logit_mm, srw_mm = (sem(n) for n in ("bn2_done", "mv2_done", "x1tr_done", "x1T_done", "logit_mm", "srw_mm"))
        route, route_mm, route_act, xn_done = sem("route"), sem("route_mm"), sem("route_act"), sem("xn_done")
        scattered = sem("scattered")
        stage_loaded = [sem(f"stage_loaded{b}") for b in range(2)]
        bias_loaded = [sem(f"bias_loaded{b}") for b in range(2)]
        xg_loaded = [sem(f"xg_loaded{b}") for b in range(2)]
        w_hi_done, w_lo_done = sem("w_hi_done"), sem("w_lo_done")
        xg_hi_done, xg_lo_done, xgtr_done, xgT_a, xgT_v = (sem(n) for n in ("xg_hi_done", "xg_lo_done", "xgtr_done", "xgT_a", "xgT_v"))
        up_mm, gelu_done, hid_hi, hid_lo, down_mm, y_done = (sem(n) for n in ("up_mm", "gelu_done", "hid_hi", "hid_lo", "down_mm", "y_done"))
        y_stored = [sem(f"y_stored{b}") for b in range(2)]
        yg_loaded = [sem(f"yg_loaded{t}") for t in range(NT)]
        x1r_loaded = sem("x1r_loaded")
        res_done = sem("res_done")
        out_stored = sem("out_stored")

        def at_least(eng, s, n):
            if not isinstance(n, int) or n > 0:
                eng.wait_ge(s, n)

        def wait_apart(eng, s, n):
            eng.wait_ge(s, n)
            eng.sem_inc(passed, 1)

        def chain(eng, s, ins, n):
            ins.then_inc(s, 1)
            eng.wait_ge(s, n)

        def chain_apart(eng, s, ins, n):
            ins.then_inc(s, 1)
            wait_apart(eng, s, n)

        x_t = x.rearrange("(t p) d -> p t d", p=P)
        adj_t = adj.rearrange("(t p) n -> p t n", p=P)
        out_t = out.rearrange("(t p) d -> p t d", p=P)

        x1_t = x1_dram.rearrange("(t p) d -> p t d", p=P)
        sorted_x_t = sorted_x.rearrange("(s p) d -> p s d", p=P)
        sorted_y_t = sorted_y.rearrange("(s p) d -> p s d", p=P)

        def pipeline(eng, first, steady, ebbing, end, body):
            def turn(i, b, k):
                def tile(lag):
                    if isinstance(i, int):
                        t = i + lag
                        return (t, t % 2, t // 2) if 0 <= t < NT else None
                    return i + lag, (b + lag) % 2, k + (b + lag) // 2
                return tile
            for i in range(first, steady):
                body(i, turn(i, i % 2, i // 2))
            with eng.Fori(steady // 2, ebbing // 2) as k:
                for b in range(2):
                    body(None, turn(2 * k + b, b, k))
            for i in range(ebbing, end):
                body(i, turn(i, i % 2, i // 2))

        FIRST_STAGE = (-2, 4, NT - 2, NT + 1)
        LAST_STAGE = (-1, 8, NT - 2, NT + 5)

        def slot_loop(eng, body):
            body(0, 0, 0, True)
            body(1, 1, 0, True)
            with eng.Fori(1, SLOTS_MOE // 2) as k:
                body(2 * k, 0, k, True)
                body(2 * k + 1, 1, k, True)
            assert SLOTS_MOE % 2
            body(SLOTS_MOE - 1, 0, SLOTS_MOE // 2, False)

        def make_bd(eng, made, work, h, slot, n):
            v = vals[:, :, ds(h * DH, DH)]
            fb = fac_b[:, :, ds(h, 1)]
            fd = fac_d[:, :, ds(h, 1)]
            dst = bd[:, ds(slot * (NT * Q * BD), NT * Q * BD)].rearrange("p (t q c) -> p t q c", t=NT, q=Q)
            eng.tensor_tensor(work[:, :, 0:DH], v, fb.to_broadcast([P, NT, DH]), ALU.mult).then_inc(made, 1)
            eng.tensor_tensor(work[:, :, C:C + DH], v, fd.to_broadcast([P, NT, DH]), ALU.mult).then_inc(made, 1)
            eng.tensor_copy(work[:, :, DH:C], fb).then_inc(made, 1)
            chain_apart(eng, made, eng.tensor_copy(work[:, :, C + DH:BD], fd), n + 4)
            chain_apart(eng, made, eng.tensor_copy(dst[:, :, 0, :], work[:, :, :]), n + 5)
            chain_apart(eng, made, eng.tensor_tensor(work[:, :, :], work[:, :, :], dst[:, :, 0, :], ALU.subtract), n + 6)
            chain_apart(eng, made, eng.tensor_copy(dst[:, :, 1, :], work[:, :, :]), n + 7)
            chain_apart(eng, made, eng.tensor_tensor(dst[:, :, 2, :], work[:, :, :], dst[:, :, 1, :], ALU.subtract), n + 8)

        block = ctx.enter_context(nc.Block())

        @block.sync
        def _(sp):
            def load_tile(t, b):
                at_least(sp, cast_done, t - 1)
                sp.dma_start(adj_in[b][:, :], adj_t[:, ds(t, 1), :]).then_inc(adj_loaded[b], 16)
                at_least(sp, xs_done, t - 1)
                sp.dma_start(x_in[b][:, :], x_t[:, ds(t, 1), :]).then_inc(x_loaded[b], 16)

            load_tile(0, 0)
            sp.dma_start(wf[:, :, :], w_seq.rearrange("(c p) n -> p c n", p=P)).then_inc(wq_loaded, 16)
            sp.dma_start(aw[:, 0, :], a1.partition_broadcast(P)).then_inc(a_loaded, 16)
            sp.dma_start(aw[:, 1, :], a2.partition_broadcast(P)).then_inc(a_loaded, 16)
            load_tile(1, 1)
            sp.dma_start(rw[:, :, :], router_w.rearrange("(c p) e -> p c e", p=P)).then_inc(rw_loaded, 16)
            with sp.Fori(1, NT // 2) as k:
                t = 2 * k
                load_tile(t, 0)
                load_tile(t + 1, 1)

            sp.wait_ge(s_copied, 2 * NT)
            sp.dma_start(s1_dram, s_row[0:H, :]).then_inc(s1_stored, 16)
            sp.wait_ge(s1_stored, 16)

            def load_row(h, b):
                at_least(sp, step_ready, 2 * MADE * (h - 1))
                if not isinstance(h, int):
                    sp.wait_ge(g_ready, G_BASE + 2 * NT * (h - 1))
                sp.dma_start(s1row[b][:, :], s1_dram[ds(h, 1), :].partition_broadcast(P)).then_inc(s1_loaded[b], 16)

            sp.wait_ge(factors, 9)
            load_row(0, 0)
            load_row(1, 1)
            with sp.Fori(1, H // 2) as k:
                h = 2 * k
                load_row(h, 0)
                load_row(h + 1, 1)

            sp.wait_ge(g_used, G_RING + 4 * NT * (PAIRS - 1))
            sp.dma_start(wo_f[:, :, :], w_out.rearrange("(c p) n -> p c n", p=P)).then_inc(wo_loaded, 16)
            sp.dma_start(bo_bc[:, :], b_out.partition_broadcast(P)).then_inc(bo_loaded, 16)

            sp.wait_ge(comb_done, COMB_BASE + 2 * H)

            def load_chunk(t, e, c):
                g = CH * t + c
                at_least(sp, w_hi_done, g - 1)
                at_least(sp, w_lo_done, g - 1)
                if c < KC:
                    src = w1[ds(e, 1), c * P:(c + 1) * P, :].rearrange("a p f -> p (a f)")
                    dst = stage[g % 2][:, :]
                else:
                    r = (c - KC) * (F // KC)
                    src = w2[ds(e, 1), r:r + F // KC, :].rearrange("a (q p) d -> p (a q) d", p=P)
                    dst = stage[g % 2][:, :].rearrange("p (q d) -> p q d", d=D)
                sp.dma_start(dst, src).then_inc(stage_loaded[g % 2], 16)

            AHEAD = 3
            sp.wait_ge(wlo_done, 3)
            sp.wait_ge(cleared, 16)
            for c in range(2):
                load_chunk(0, 0, c)
            for t in range(2):
                sp.dma_start(px[t][:, :], x_t[:, t, :]).then_inc(px_loaded[t], 16)
            for c in range(2, 2 + AHEAD):
                load_chunk(0, 0, c)
            for t in range(2, NT):
                sp.wait_ge(x1_done, t - 1)
                sp.dma_start(px[t % 2][:, :], x_t[:, t, :]).then_inc(px_loaded[t % 2], 16)
                if t + AHEAD < CH:
                    load_chunk(0, 0, t + AHEAD)
                sp.wait_ge(x1_kept, t - 1)
                sp.dma_start(x1_t[:, t - 2, :], x1[:, t - 2, :]).then_inc(x1_stored, 16)
            for t in range(NT - 2, NT):
                sp.wait_ge(x1_kept, t + 1)
                sp.dma_start(x1_t[:, t, :], x1[:, t, :]).then_inc(x1_stored, 16)

            sp.wait_ge(b1_loaded, 16)
            sp.wait_ge(route, ROUTE_STEPS)
            for t in range(SLOTS_MOE):
                b = t % 2
                e = sp.value_load(expert_of[0:1, t:t + 1], min_val=0, max_val=E - 1)
                if t > 0:
                    for c in range(CH):
                        load_chunk(t, e, c)
                at_least(sp, gelu_done, FC * (t - 1))
                at_least(sp, y_done, TT * (t - 1))
                sp.dma_start(b1_now[b][:, :], b1_all[:, ds(e * FC, FC)]).then_inc(bias_loaded[b], 16)
                sp.dma_start(b2_now[b][:, :], b2[ds(e, 1), :].partition_broadcast(P)).then_inc(bias_loaded[b], 16)

            sp.wait_ge(down_mm, TT * (SLOTS_MOE - 1))
            sp.dma_start(x1_back[:, :, :], x1_t).then_inc(x1r_loaded, 16)
            for t in range(NT):
                sp.wait_ge(res_done, t + 1)
                sp.dma_start(out_t[:, t, :], y_back[:, t, :]).then_inc(out_stored, 16)
            sp.wait_ge(out_stored, 16 * NT)

        @block.gpsimd
        def _(pool):
            pool.sem_inc(comb_done, COMB_BASE)
            pool.memset(ones[:, :], 1.0).then_inc(consts0, 1)
            pool.memset(eps_col[:, :], EPS / (SCALE * SCALE)).then_inc(consts0, 1)
            pool.memset(eps1[:, :], EPS).then_inc(consts0, 1)
            pool.memset(zeros[:, :], 0.0).then_inc(consts0, 1)
            pool.memset(after[:, :], 0.0).then_inc(consts0, 1)
            pool.memset(zero_t[:, :], 0.0).then_inc(consts0, 1)
            pool.wait_ge(consts0, 6)
            pool.affine_select(out=after[:, :], in_=after[:, :], compare_op=ALU.is_ge, fill=-1.0,
                               base=0, pattern=[[1, P]], channel_multiplier=-1).then_inc(consts, 1)
            pool.iota(token_no[:, :], pattern=[[P, NT]], base=1, channel_multiplier=1, allow_small_or_imprecise_dtypes=True).then_inc(consts, 1)
            pool.iota(slot_no[:, :], pattern=[[1, SLOTS_MOE]], base=0, channel_multiplier=0, allow_small_or_imprecise_dtypes=True).then_inc(consts, 1)
            pool.iota(slot_low[:, :, :], pattern=[[0, E], [SLOT, N // SLOT]], base=0, channel_multiplier=0, allow_small_or_imprecise_dtypes=True).then_inc(consts, 1)
            pool.wait_ge(consts, 4)
            pool.memset(slot_low[:, 0, 0:1], -1.0).then_inc(consts, 1)
            for m in (ident16, identb, identf):
                pool.affine_select(out=m[:, :], in_=ones[:, :], compare_op=ALU.is_equal, fill=0.0,
                                   base=0, pattern=[[-1, P]], channel_multiplier=1).then_inc(consts, 1)
            pool.wait_ge(wq_loaded, 16)
            pool.wait_ge(a_loaded, 32)
            for i in range(2):
                pool.tensor_tensor(wprod[i].rearrange("p c (h d) -> p (c h) d", d=DH), wf[:, :, :].rearrange("p c (h d) -> p (c h) d", d=DH),
                                   aw[:, i:i + 1, :].to_broadcast([P, KC * H, DH]), ALU.mult).then_inc(wprod_done, 1)
            with nc.allow_non_contiguous_dma(reason="one bias per partition, once"):
                pool.dma_start(b1_all[:, :].rearrange("p (e c) -> p e c", e=E), b1.rearrange("e (c p) -> p e c", p=P)).then_inc(b1_loaded, 16)

            COMB_STEPS = 4

            def combine(h, half, b, tbuf, hh, w):
                n = w * COMB_STEPS
                i0 = half * HALF
                pool.wait_ge(comb_done, COMB_BASE + w)
                wait_apart(pool, sum_used, w + 1)
                fa = fac_a[:, i0:i0 + HALF, ds(h, 1)].to_broadcast([P, HALF, C])
                fc = fac_c[:, i0:i0 + HALF, ds(h, 1)].to_broadcast([P, HALF, C])
                t_all = tsum[:, ds(tbuf * (NT * 2 * C), NT * 2 * C)].rearrange("p (t g c) -> p t g c", t=NT, g=2)
                pool.tensor_tensor(branch_a[:, :, :], ssum[b][:, :, 0:C], fa, ALU.mult).then_inc(comb, 1)
                chain_apart(pool, comb, pool.tensor_tensor(branch_c[:, :, :], t_all[:, i0:i0 + HALF, hh, :], ssum[b][:, :, C:BD], ALU.subtract), n + 2)
                chain_apart(pool, comb, pool.tensor_tensor(branch_c[:, :, :], branch_c[:, :, :], fc, ALU.mult), n + 3)
                chain_apart(pool, comb, pool.tensor_tensor(vals[:, i0:i0 + HALF, ds(h * DH, DH)], branch_a[:, :, 0:DH], branch_c[:, :, 0:DH], ALU.add), n + 4)
                pool.tensor_tensor(den[:, i0:i0 + HALF, ds(h, 1)], branch_a[:, :, DH:C], branch_c[:, :, DH:C], ALU.add).then_inc(comb_done, 1)

            pool.wait_ge(factors_act, 4)
            pool.wait_ge(vals_done, NT)
            pool.wait_ge(s1_stored, 16)
            pool.dma_start(sorted_x_t, zeros[:, :].rearrange("p (a d) -> p a d", a=1).to_broadcast([P, SLOTS_MOE * TT, D])).then_inc(cleared, 16)
            for h in range(2, 4):
                make_bd(pool, bd_chain, bdf, h, h, (h - 2) * BD_STEPS)

            def pair(p, prepare):
                if prepare:
                    wait_apart(pool, g_used, G_RING + 4 * NT * p)
                for hh in range(2):
                    for half in range(2):
                        if prepare and hh == 0:
                            h = 2 * p + 4 + half
                            make_bd(pool, bd_chain, bdf, h, h % SLOTS, (h - 2) * BD_STEPS)
                        combine(2 * p + hh, half, half, p % 2, hh, 4 * p + 2 * hh + half)

            with pool.Fori(0, PAIRS - 2) as p:
                pair(p, True)
            with pool.Fori(PAIRS - 2, PAIRS) as p:
                pair(p, False)

            pool.wait_ge(comb_done, COMB_BASE + 2 * H)

            def last_stage(i, tile):
                if tile(1):
                    t, b, k = tile(1)
                    if not isinstance(t, int) or t > 1:
                        wait_apart(pool, h_hi_done, t - 1)
                    wait_apart(pool, rden_done, t + 1)
                    pool.tensor_tensor(hn[b][:, :].rearrange("p (h d) -> p h d", d=DH),
                                       vals[:, ds(t, 1), :].rearrange("p a (h d) -> p (a h) d", d=DH),
                                       rden[b][:, :].rearrange("p (h a) -> p h a", a=1).to_broadcast([P, H, DH]), ALU.mult).then_inc(hn_done, 1)
                if tile(-4):
                    t, b, k = tile(-4)
                    wait_apart(pool, x1_done, t + 1)
                    pool.tensor_copy(x1[:, ds(t, 1), :].rearrange("p a d -> p (a d)"), x1_now[b][:, :]).then_inc(x1_kept, 1)

            pipeline(pool, *LAST_STAGE, last_stage)

            pool.wait_ge(cleared, 16)
            pool.wait_ge(route, ROUTE_STEPS)
            for t in range(NT):
                pool.wait_ge(xn_done, t + 1)
                pool.indirect_dma_start(out=sorted_x, out_offset=bass.IndirectOffsetOnAxis(ap=row_of[:, t:t + 1], axis=0),
                                        in_=vals[:, t, :], in_offset=None).then_inc(scattered, 16)
            pool.wait_ge(scattered, 16 * NT)
            pool.wait_ge(x1_stored, 16 * NT)

            def load_slot(t, b):
                if not isinstance(t, int):
                    wait_apart(pool, xg_lo_done, t - 1)
                else:
                    at_least(pool, xg_lo_done, t - 1)
                pool.dma_start(xg[b][:, :, :], sorted_x_t[:, ds(t * TT, TT), :]).then_inc(xg_loaded[b], 16)

            def slot(t, b, k, ahead):
                if ahead:
                    load_slot(t + 1, 1 - b)
                for tt in range(TT):
                    wait_apart(pool, y_done, TT * t + tt + 1)
                    pool.dma_start(sorted_y_t[:, ds(t * TT + tt, 1), :], y_sb[tt][:, :]).then_inc(y_stored[tt], 16)

            load_slot(0, 0)
            slot_loop(pool, slot)

            for tt in range(TT):
                pool.wait_ge(y_stored[tt], 16 * SLOTS_MOE)
            for t in range(NT):
                pool.indirect_dma_start(out=y_back[:, t, :], out_offset=None, in_=sorted_y,
                                        in_offset=bass.IndirectOffsetOnAxis(ap=row_of[:, t:t + 1], axis=0)).then_inc(yg_loaded[t], 16)

        @block.scalar
        def _(act):
            act.wait_ge(wq_loaded, 16)
            act.activation(wq_hi[:, :, :], wf[:, :, :], ACT.Copy, scale=SCALE).then_inc(whi_done, 1)
            act.wait_ge(consts0, 2)

            def first_stage(i, tile):
                if i == 1:
                    act.wait_ge(wprep, 3)
                    act.activation(wa_hi[:, :, :], wa[:, :, :], ACT.Copy, scale=SCALE).then_inc(whi_done, 1)
                if tile(1):
                    t, b, k = tile(1)
                    act.wait_ge(mv_done, t + 1)
                    act.activation(std[b][:, :], mv[b][:, 1:2], ACT.Sqrt, bias=eps_col[:, :],
                                   scale=1.0 / (SCALE * SCALE)).then_inc(std_done, 1)
                if tile(0):
                    t, b, k = tile(0)
                    act.wait_ge(atr_done, 2 * t + 1)
                    act.activation(adjT[:, 0:NT // 2, ds(t * P, P)],
                                   bank[4].bitcast(bf16).rearrange("p (j c) -> p j c", c=P), ACT.Copy).then_inc(adjT_a, 1)
                if tile(1):
                    t, b, k = tile(1)
                    act.wait_ge(xs_done, t + 1)
                    at_least(act, xtr_done, t - 1)
                    act.activation(x_hl[b][:, 0, :], xs[b][:, :], ACT.Copy).then_inc(hi_done, 1)
                if tile(2):
                    t, b, k = tile(2)
                    act.wait_ge(adj_loaded[b], 16 * (k + 1))
                    at_least(act, atr_done, 2 * (t - 1))
                    at_least(act, alone_done, t - 1)
                    act.activation(adj_b[b][:, :], adj_in[b][:, :], ACT.Copy, accum_out=degree[b][:, :]).then_inc(cast_done, 1)
                if tile(-1):
                    t, b, k = tile(-1)
                    act.wait_ge(proj_done, t + 1)
                    act.activation(vals[:, ds(t, 1), :], bank[2 + b], ACT.Copy, scale=UNSCALE).then_inc(vals_done, 1)

            pipeline(act, *FIRST_STAGE, first_stage)

            act.wait_ge(factors, 8)
            act.activation(fac_a[:, :, :], sa[:, :, :], ACT.Exp).then_inc(factors_act, 1)
            act.activation(fac_c[:, :, :], sc[:, :, :], ACT.Exp).then_inc(factors_act, 1)
            act.activation(fac_b[:, :, :], sy[:, :, :], ACT.Exp).then_inc(factors_act, 1)
            act.activation(fac_d[:, :, :], sy[:, :, :], ACT.Exp, scale=ALPHA).then_inc(factors_act, 1)
            act.wait_ge(factors_act, 4)
            act.wait_ge(factors, 9)

            with act.Fori(0, PAIRS) as p:
                made = 0
                for hh in range(2):
                    h = 2 * p + hh
                    act.activation(bias_now[hh][:, :], steep_bias[:, :, ds(h, 1)].rearrange("p t a -> p (t a)"), ACT.Copy).then_inc(bias_done, 1)
                    act.wait_ge(bias_done, h + 1)
                    act.wait_ge(s1_loaded[hh], 16 * (p + 1))
                    for half in range(2):
                        w = 2 * hh + half
                        for j in range(NT):
                            if j in FUSED:
                                continue
                            back = [(ww, jj) for ww in range(-1, w + 1) for jj in range(NT) if jj not in FUSED and (ww, jj) < (w, j)][-RING]
                            act.wait_ge(g_ready, G_BASE + 4 * NT * p + back[0] * NT + back[1] + 1)
                            ins = act.activation(steps[made % RING][:, :], s1row[hh][:, half * (N // 2):(half + 1) * (N // 2)],
                                                 ACT.Relu, bias=bias_now[hh][:, j:j + 1], scale=STEEP)
                            ins.then_inc(step_ready, 1)
                            made += 1

            def chunk_hi(t, b, c, k):
                act.wait_ge(stage_loaded[c % 2], 16 * ((CH // 2) * t + c // 2 + 1))
                if c == 0:
                    at_least(act, down_mm, TT * (t - 1))
                dst = wbuf[b][0][:, c, :] if c < KC else wbuf[b][2][:, (c - KC) * KC:(c - KC + 1) * KC, :].rearrange("p q d -> p (q d)")
                act.activation(dst, stage[c % 2][:, :], ACT.Copy, scale=SCALE).then_inc(w_hi_done, 1)

            act.wait_ge(wo_loaded, 16)
            act.activation(wo_hi[:, :, :], wo_f[:, :, :], ACT.Copy, scale=SCALE).then_inc(whi_done, 1)

            def last_stage(i, tile):
                if i is not None and 0 <= i < CH:
                    chunk_hi(0, 0, i, 0)
                if tile(-4):
                    t, b, k = tile(-4)
                    act.wait_ge(x1tr_done, t + 1)
                    at_least(act, logit_mm, t - 1)
                    act.activation(x1T[b][:, :, :].rearrange("p c q -> p (c q)"), bank[4 + b], ACT.Copy).then_inc(x1T_done, 1)
                if tile(0):
                    t, b, k = tile(0)
                    act.wait_ge(htr_done, t + 1)
                    at_least(act, out_mm, t - 1)
                    act.activation(hT[b][:, :, :, :].rearrange("p a b c -> p (a b c)"), bank[b].bitcast(fp16), ACT.Copy).then_inc(hT_done, 1)
                if tile(-2):
                    t, b, k = tile(-2)
                    act.wait_ge(z_done, t + 1)
                    at_least(act, ez_done, t - 1)
                    act.activation(zneg[b][:, :], z[b][:, :], ACT.Relu, scale=-1.0).then_inc(zneg_done, 1)
                    act.wait_ge(zneg_done, t + 1)
                    at_least(act, elu_done, t - 1)
                    act.activation(ez[b][:, :], zneg[b][:, :], ACT.Exp, scale=-1.0).then_inc(ez_done, 1)
                if tile(1):
                    t, b, k = tile(1)
                    act.wait_ge(hn_done, t + 1)
                    at_least(act, htr_done, t - 1)
                    act.activation(h_hl[b][:, 0, :], hn[b][:, :], ACT.Copy, scale=SCALE).then_inc(h_hi_done, 1)

            pipeline(act, *LAST_STAGE, last_stage)
            act.wait_ge(mv2_done, NT)
            act.activation(std2[:, :].rearrange("p (t a) -> p t a", a=1), mv2[:, :, 1:2], ACT.Sqrt, bias=eps1[:, :]).then_inc(route_act, 1)
            act.wait_ge(route, EXP_AT)
            act.activation(expd[:, :, :], ctx_l[:, :, :], ACT.Exp).then_inc(route_act, 1)

            def tokens_hi(t, b, k):
                act.wait_ge(xg_loaded[b], 16 * (k + 1))
                at_least(act, xgtr_done, TT * t)
                act.activation(xg_hl[:, :, 0, :], xg[b][:, :, :], ACT.Copy, scale=SCALE).then_inc(xg_hi_done, 1)

            def tokens_T(t, b):
                act.wait_ge(xgtr_done, TT * t + 1)
                at_least(act, up_mm, FC * (t - 1))
                act.activation(xgT[b][:, :, :, 0:P].rearrange("p a c q -> p (a c) q"), bank[6].bitcast(fp16).rearrange("p (a q) -> p a q", q=P), ACT.Copy).then_inc(xgT_a, 1)

            def slot(t, b, k, ahead):
                act.wait_ge(bias_loaded[b], 32 * (k + 1))
                for f in range(FC):
                    act.wait_ge(up_mm, FC * t + f + 1)
                    at_least(act, hid_lo, FC * t + f - 3)
                    act.activation(hid[f % 4][:, :], bank[f % 4][:, 0:SLOT], ACT.Gelu_apprx_tanh, bias=b1_now[b][:, f:f + 1], scale=UNSCALE).then_inc(gelu_done, 1)
                    if ahead and f % 4 == 3:
                        chunk_hi(t + 1, 1 - b, f // 4, k)
                if ahead:
                    tokens_hi(t + 1, 1 - b, k + b)
                    for c in range(KC, CH - 1):
                        chunk_hi(t + 1, 1 - b, c, k)
                    tokens_T(t + 1, 1 - b)
                    chunk_hi(t + 1, 1 - b, CH - 1, k)

            tokens_hi(0, 0, 0)
            tokens_T(0, 0)
            slot_loop(act, slot)

        @block.vector
        def _(dve):
            dve.sem_inc(g_ready, G_BASE)
            def weights():
                dve.wait_ge(consts, 8)
                dve.reciprocal(per_token[:, :], token_no[:, :]).then_inc(wprep, 1)
                for i in range(2):
                    dve.wait_ge(wprod_done, i + 1)
                    dve.tensor_reduce(wa[:, :, i * H:(i + 1) * H], wprod[i].rearrange("p c (h d) -> p c h d", d=DH), X, ALU.add).then_inc(wprep, 1)
                dve.wait_ge(whi_done, 1)
                dve.scalar_tensor_tensor(wq_lo[:, :, :].rearrange("p c n -> p (c n)"), wf[:, :, :].rearrange("p c n -> p (c n)"), SCALE, wq_hi[:, :, :].rearrange("p c n -> p (c n)"), ALU.mult, ALU.subtract).then_inc(wlo_done, 1)
                dve.wait_ge(whi_done, 2)
                dve.scalar_tensor_tensor(wa_lo[:, :, :], wa[:, :, :], SCALE, wa_hi[:, :, :], ALU.mult, ALU.subtract).then_inc(wlo_done, 1)

            def first_stage(i, tile):
                if i == 1:
                    weights()
                if tile(1):
                    t, b, k = tile(1)
                    dve.wait_ge(x_loaded[b], 16 * (k + 1))
                    dve.bn_stats(stats[b][:, :], x_in[b][:, :]).then_inc(stats_done, 1)
                    at_least(dve, std_done, t - 1)
                    wait_apart(dve, stats_done, t + 1)
                    dve.bn_aggr(mv[b][:, :], stats[b][:, :]).then_inc(mv_done, 1)
                if tile(0):
                    t, b, k = tile(0)
                    dve.wait_ge(xtr_done, t + 1)
                    at_least(dve, s_done, t - 1)
                    dve.tensor_copy(xT[b][:, :, :, :].rearrange("p a b c -> p (a b c)"), bank[b].bitcast(fp16)).then_inc(xT_done, 1)
                if tile(1):
                    t, b, k = tile(1)
                    dve.wait_ge(std_done, t + 1)
                    dve.reciprocal(rstd[b][:, :], std[b][:, :]).then_inc(rstd_done, 1)
                    dve.wait_ge(rstd_done, t + 1)
                    at_least(dve, hi_done, t - 1)
                    dve.tensor_scalar(xs[b][:, :], x_in[b][:, :], mv[b][:, 0:1], rstd[b][:, :], ALU.subtract, ALU.mult).then_inc(xs_done, 1)
                    dve.wait_ge(cast_done, t + 1)
                    dve.tensor_scalar(alone[b][:, :], degree[b][:, :], 0.5, None, ALU.is_lt).then_inc(alone_done, 1)
                    dve.wait_ge(alone_done, t + 1)
                    dve.tensor_scalar(adj_b[b][:, :], adj_b[b][:, :], alone[b][:, :], None, ALU.max).then_inc(amax_done, 1)
                if tile(1):
                    t, b, k = tile(1)
                    dve.wait_ge(hi_done, t + 1)
                    dve.tensor_tensor(x_hl[b][:, 1, :], xs[b][:, :], x_hl[b][:, 0, :], ALU.subtract).then_inc(lo_done, 1)
                if tile(-1):
                    t, b, k = tile(-1)
                    dve.wait_ge(s_done, t + 1)
                    dve.tensor_scalar(s_tok[:, ds(t, 1), :], bank[6 + b][:, 0:2 * H], UNSCALE, None, ALU.mult).then_inc(s_copied, 1)
                    dve.tensor_scalar(s_row[:, ds(t * P, P)], bank[6 + b][0:2 * H, P:2 * P], UNSCALE, None, ALU.mult).then_inc(s_copied, 1)
                if tile(0):
                    t, b, k = tile(0)
                    dve.wait_ge(atr_done, 2 * t + 2)
                    dve.tensor_copy(adjT[:, NT // 2:NT, ds(t * P, P)], bank[5].bitcast(bf16).rearrange("p (j c) -> p j c", c=P)).then_inc(adjT_v, 1)

            pipeline(dve, *FIRST_STAGE, first_stage)

            dve.wait_ge(s_copied, 2 * NT)
            chain(dve, factors, dve.reduce_max(top_row[:, :], s_row[:, :], X), 1)
            chain(dve, factors, dve.tensor_scalar(top_diag[:, :], identf[0:2 * H, 0:2 * H], top_row[:, :], None, ALU.mult), 2)
            dve.wait_ge(top_mm, 1)
            chain(dve, factors, dve.tensor_copy(top[:, :], bank[0][:, 0:2 * H]), 3)
            top2 = top[:, H:2 * H].rearrange("p (a h) -> p a h", a=1).to_broadcast([P, NT, H])
            chain(dve, factors, dve.tensor_tensor(sx[:, :, :], s_tok[:, :, 0:H], top2, ALU.add), 4)
            dve.tensor_scalar(sa[:, :, :], sx[:, :, :], 1.0 - ALPHA, 0.0, ALU.mult, ALU.min).then_inc(factors, 1)
            dve.tensor_scalar(sc[:, :, :], sx[:, :, :], ALPHA - 1.0, 0.0, ALU.mult, ALU.min).then_inc(factors, 1)
            dve.tensor_tensor(sy[:, :, :], s_tok[:, :, H:2 * H], top2, ALU.subtract).then_inc(factors, 1)
            dve.tensor_scalar(steep_bias[:, :, :], s_tok[:, :, H:2 * H], STEEP, None, ALU.mult).then_inc(factors, 1)
            dve.tensor_scalar(neg_s2[:, :, :], s_tok[:, :, H:2 * H], -1.0, None, ALU.mult).then_inc(factors, 1)
            dve.wait_ge(factors_act, 4)
            dve.wait_ge(vals_done, NT)
            for h in range(2):
                make_bd(dve, bd_first, bdf_first, h, h, h * BD_STEPS)

            def copy_tails(pair, r):
                dst = tsum[:, ds((pair % 2) * (NT * 2 * C), NT * 2 * C)].rearrange("p (t g c) -> p t g c", t=NT, g=2)
                for g in range(2):
                    src = tails[:, :, g * Q * C:(g + 1) * Q * C].rearrange("p t (q c) -> p t c q", q=Q)
                    ins = dve.tensor_reduce(dst[:, 4 * r:4 * r + 4, g, :], src, X, ALU.add)
                ins.then_inc(t_free, 1)

            for r in range(4):
                dve.wait_ge(t_done, r + 1)
                copy_tails(0, r)

            def pair(p, ahead):
                made = 0
                for hh in range(2):
                    h = 2 * p + hh
                    dve.wait_ge(s1_loaded[hh], 16 * (p + 1))
                    for half in range(2):
                        w = 4 * p + 2 * hh + half
                        q0 = half * (N // 2)
                        for j in range(NT):
                            dve.wait_ge(g_used, NT * w + j + 1)
                            mask = adjT[:, j, q0:q0 + N // 2]
                            if j in FUSED:
                                ins = dve.scalar_tensor_tensor(gmask[j % G_RING][:, :], s1row[hh][:, q0:q0 + N // 2],
                                                               neg_s2[:, j, ds(h, 1)], mask, ALU.is_gt, ALU.mult)
                            else:
                                dve.wait_ge(step_ready, 4 * MADE * p + made + 1)
                                ins = dve.tensor_tensor(gmask[j % G_RING][:, :], steps[made % RING][:, :], mask, ALU.min)
                                made += 1
                            ins.then_inc(g_ready, 1)
                            if j == 5 and ahead:
                                dve.wait_ge(t_done, w + 5)
                                dve.wait_ge(comb_done, COMB_BASE + 4 * p)
                                copy_tails(p + 1, 2 * hh + half)
                        dve.wait_ge(g_used, G_RING + NT * (w + 1))
                        src = sums[:, :, 0:Q * BD].rearrange("p t (q c) -> p t c q", q=Q)
                        at_least(dve, comb_done, w)
                        dve.tensor_reduce(ssum[half][:, :, :], src, X, ALU.add).then_inc(sum_used, 1)

            pair(0, True)
            with dve.Fori(1, PAIRS - 1) as p:
                pair(p, True)
            pair(PAIRS - 1, False)

            def chunk_lo(t, b, c):
                dve.wait_ge(w_hi_done, CH * t + c + 1)
                if c < KC:
                    hi, lo = wbuf[b][0][:, c, :], wbuf[b][1][:, c, :]
                else:
                    hi, lo = (wbuf[b][i][:, (c - KC) * KC:(c - KC + 1) * KC, :].rearrange("p q d -> p (q d)") for i in (2, 3))
                dve.scalar_tensor_tensor(lo, stage[c % 2][:, :], SCALE, hi, ALU.mult, ALU.subtract).then_inc(w_lo_done, 1)

            def last_stage(i, tile):
                if tile(0):
                    t, b, k = tile(0)
                    dve.wait_ge(h_hi_done, t + 1)
                    dve.scalar_tensor_tensor(h_hl[b][:, 1, :], hn[b][:, :], SCALE, h_hl[b][:, 0, :], ALU.mult, ALU.subtract).then_inc(h_lo_done, 1)
                if tile(-2):
                    t, b, k = tile(-2)
                    if i == 2:
                        dve.wait_ge(comb_done, COMB_BASE + 2 * H)
                    at_least(dve, x1_done, t - 1)
                    dve.wait_ge(out_mm, t + 1)
                    dve.scalar_tensor_tensor(z[b][:, :], bank[2 + b], UNSCALE, bo_bc[:, :], ALU.mult, ALU.add).then_inc(z_done, 1)
                if tile(1):
                    t, b, k = tile(1)
                    at_least(dve, hn_done, t - 1)
                    dve.reciprocal(rden[b][:, :], den[:, ds(t, 1), :].rearrange("p a h -> p (a h)")).then_inc(rden_done, 1)
                if tile(-3):
                    t, b, k = tile(-3)
                    dve.wait_ge(ez_done, t + 1)
                    dve.scalar_tensor_tensor(z[b][:, :], z[b][:, :], 0.0, ez[b][:, :], ALU.max, ALU.add).then_inc(elu_done, 1)
                    dve.wait_ge(elu_done, t + 1)
                    dve.wait_ge(px_loaded[b], 16 * (k + 1))
                    at_least(dve, x1_kept, t - 1)
                    at_least(dve, x1tr_done, t - 1)
                    dve.scalar_tensor_tensor(x1_now[b][:, :], z[b][:, :], -1.0, px[b][:, :], ALU.add, ALU.add).then_inc(x1_done, 1)
                    dve.wait_ge(x1_done, t + 1)
                    dve.bn_stats(stats2[:, ds(t, 1), :].rearrange("p a d -> p (a d)"), x1_now[b][:, :]).then_inc(bn2_done, 1)
                if i is not None and 0 <= i < CH:
                    chunk_lo(0, 0, i)

            dve.wait_ge(whi_done, 3)
            dve.scalar_tensor_tensor(wo_lo[:, :, :], wo_f[:, :, :], SCALE, wo_hi[:, :, :], ALU.mult, ALU.subtract).then_inc(wlo_done, 1)
            dve.wait_ge(comb_done, COMB_BASE + 2 * H - 1)
            dve.wait_ge(bo_loaded, 16)
            pipeline(dve, *LAST_STAGE, last_stage)

            steps_done = [0]

            def step(ins):
                steps_done[0] += 1
                chain(dve, route, ins, steps_done[0])

            def free_step(ins):
                steps_done[0] += 1
                ins.then_inc(route, 1)

            def await_steps():
                dve.wait_ge(route, steps_done[0])

            def over_e(a):
                return a.rearrange("p (t a) -> p t a", a=1).to_broadcast([P, NT, E])

            def over_t(a):
                return a.rearrange("p (a e) -> p a e", a=1).to_broadcast([P, NT, E])

            dve.wait_ge(bn2_done, NT)
            for t in range(NT):
                dve.bn_aggr(mv2[:, t, :], stats2[:, t, :]).then_inc(mv2_done, 1)
            dve.wait_ge(srw_mm, 1)
            step(dve.tensor_copy(rw_sum[:, :], bank[7][:, 0:E]))
            dve.wait_ge(logit_mm, NT)
            dve.wait_ge(mv2_done, NT)
            step(dve.tensor_tensor(shift[:, :, :], mv2[:, :, 0:1].to_broadcast([P, NT, E]), over_t(rw_sum[:, :]), ALU.mult))
            raw_ins = dve.tensor_tensor(raw[:, :, :], bank[6][:, 0:NT * E].rearrange("p (t e) -> p t e", e=E), shift[:, :, :], ALU.subtract)
            free_step(raw_ins)
            dve.wait_ge(route_act, 1)
            step(dve.reciprocal(rstd2[:, :], std2[:, :]))
            step(dve.tensor_tensor(logit[:, :, :], raw[:, :, :], over_e(rstd2[:, :]), ALU.mult))
            assert steps_done[0] == LOGITS_AT
            dve.wait_ge(x1_kept, NT)

            def normalise(t0, t1):
                for t in range(t0, t1):
                    dve.tensor_scalar(vals[:, t, :], x1[:, t, :], mv2[:, t, 0:1], rstd2[:, t:t + 1], ALU.subtract, ALU.mult).then_inc(xn_done, 1)

            def running(mm, all_sums, after):
                dve.wait_ge(route_mm, mm)
                tile_sums = all_sums.rearrange("p (t e) -> p t e", e=E)
                for e in range(E):
                    free_step(dve.tensor_tensor_scan(before[:, :, e], zero_t[:, :], tile_sums[:, :, e], 0.0, ALU.add, ALU.add))
                await_steps()
                step(dve.tensor_tensor(upto[:, :, :], before[:, :, :], after.rearrange("p (t e) -> p t e", e=E), ALU.add))

            normalise(0, 5)
            running(1, bank[1][:, 0:NT * E], bank[0][:, 0:NT * E])
            step(dve.tensor_tensor(ctx_l[:, :, :], upto[:, :, :], over_e(per_token[:, :]), ALU.mult))
            step(dve.reduce_max(largest[:, :], ctx_l[:, :, :], X))
            step(dve.tensor_tensor(ctx_l[:, :, :], ctx_l[:, :, :], over_e(largest[:, :]), ALU.subtract))
            assert steps_done[0] == EXP_AT
            step(dve.tensor_scalar(same[:, :, :], ctx_l[:, :, :], 0.0, None, ALU.is_equal))
            free_step(dve.tensor_copy(onehot[:, :, 0], same[:, :, 0]))
            for e in range(1, E):
                before_e = same[:, :, 0] if e == 1 else seen[:, :, e - 1]
                free_step(dve.tensor_tensor(onehot[:, :, e], same[:, :, e], before_e, ALU.is_gt))
                if e < E - 1:
                    step(dve.tensor_tensor(seen[:, :, e], same[:, :, e], before_e, ALU.max))
            await_steps()
            assert steps_done[0] == ONEHOT_AT
            dve.wait_ge(route_act, 2)
            free_step(dve.reduce_sum(total[:, :], expd[:, :, :], X))
            normalise(5, 6)
            await_steps()
            free_step(dve.reciprocal(gate[:, :], total[:, :]))
            normalise(6, 9)
            running(2, bank[3][:, 0:NT * E], bank[2][:, 0:NT * E])
            counts = before[:, NT - 1, :]
            step(dve.tensor_tensor(above[:, :, :], counts.rearrange("p (e a) -> p e a", a=1).to_broadcast([P, E, N // SLOT]),
                                   slot_low[:, :, :], ALU.is_gt))
            step(dve.reduce_sum(n_slots[:, :], above[:, :, :], X))
            step(dve.tensor_tensor_scan(last_slot[:, :], zero_t[:, 0:E], n_slots[:, :], 0.0, ALU.add, ALU.add))
            free_step(dve.tensor_tensor(first_slot[:, :], last_slot[:, :], n_slots[:, :], ALU.subtract))
            step(dve.tensor_tensor(past[:, :, :], slot_no[:, :].rearrange("p (s a) -> p s a", a=1).to_broadcast([P, SLOTS_MOE, E - 1]),
                                   last_slot[:, 0:E - 1].rearrange("p (a e) -> p a e", a=1).to_broadcast([P, SLOTS_MOE, E - 1]), ALU.is_ge))
            free_step(dve.reduce_sum(slot_f[:, :], past[:, :, :], X))
            step(dve.scalar_tensor_tensor(upto[:, :, :], over_t(first_slot[:, :]), float(SLOT), upto[:, :, :], ALU.mult, ALU.add))
            free_step(dve.tensor_copy(expert_of[:, :], slot_f[:, :]))
            step(dve.tensor_tensor(upto[:, :, :], upto[:, :, :], onehot[:, :, :], ALU.mult))
            step(dve.reduce_sum(total[:, :], upto[:, :, :], X))
            step(dve.tensor_scalar(row_of[:, :], total[:, :], -1.0, None, ALU.add))
            assert steps_done[0] == ROUTE_STEPS, steps_done
            normalise(9, NT)

            def tokens_lo(t, b):
                dve.wait_ge(xg_hi_done, t + 1)
                dve.scalar_tensor_tensor(xg_hl[:, :, 1, :], xg[b][:, :, :], SCALE, xg_hl[:, :, 0, :], ALU.mult, ALU.subtract).then_inc(xg_lo_done, 1)

            def tokens_T(t, b):
                dve.wait_ge(xgtr_done, TT * t + 2)
                dve.tensor_copy(xgT[b][:, :, :, P:2 * P].rearrange("p a c q -> p (a c) q"), bank[7].bitcast(fp16).rearrange("p (a q) -> p a q", q=P)).then_inc(xgT_v, 1)

            def copy_y(t, tt, b):
                dve.wait_ge(down_mm, TT * t + tt + 1)
                at_least(dve, y_stored[tt], 16 * t)
                dve.scalar_tensor_tensor(y_sb[tt][:, :], bank[4 + tt], 1.0 / (SCALE * HSCALE), b2_now[b][:, :], ALU.mult, ALU.add).then_inc(y_done, 1)

            def slot(t, b, k, ahead):
                for f in range(FC):
                    n = FC * t + f
                    dve.wait_ge(gelu_done, n + 1)
                    if f == 0:
                        at_least(dve, down_mm, TT * t)
                    dve.tensor_scalar(hidT[:, 0, f, :], hid[f % 4][:, :], HSCALE, None, ALU.mult).then_inc(hid_hi, 1)
                    dve.wait_ge(hid_hi, n + 1)
                    dve.scalar_tensor_tensor(hidT[:, 1, f, :], hid[f % 4][:, :], HSCALE, hidT[:, 0, f, :], ALU.mult, ALU.subtract).then_inc(hid_lo, 1)
                    if ahead and f % 4 == 3:
                        chunk_lo(t + 1, 1 - b, f // 4)
                if ahead:
                    tokens_lo(t + 1, 1 - b)
                    for c in range(KC, CH - 1):
                        chunk_lo(t + 1, 1 - b, c)
                copy_y(t, 0, b)
                if ahead:
                    tokens_T(t + 1, 1 - b)
                    chunk_lo(t + 1, 1 - b, CH - 1)
                copy_y(t, 1, b)

            tokens_lo(0, 0)
            tokens_T(0, 0)
            slot_loop(dve, slot)

            dve.wait_ge(x1r_loaded, 16)
            for t in range(NT):
                dve.wait_ge(yg_loaded[t], 16)
                dve.scalar_tensor_tensor(y_back[:, t, :], y_back[:, t, :], gate[:, t:t + 1], x1_back[:, t, :], ALU.mult, ALU.add).then_inc(res_done, 1)

        @block.tensor
        def _(pe):
            pe.wait_ge(consts, 8)

            terms = [(c, s, w) for c in range(KC) for s, w in ((0, 0), (0, 1), (1, 0))]
            ends = {0: dict(start=True, stop=False), len(terms) - 1: dict(start=False, stop=True)}

            def first_stage(i, tile):
                if tile(0):
                    t, b, k = tile(0)
                    pe.wait_ge(lo_done, t + 1)
                    at_least(pe, xT_done, t - 1)
                    dst = bank[b].bitcast(fp16)
                    for n in range(2 * KC):
                        ins = pe.transpose(dst[:, n * P:(n + 1) * P], x_hl[b][:, n // KC, (n % KC) * P:(n % KC + 1) * P], ident16[:, :])
                    ins.then_inc(xtr_done, 1)
                    pe.wait_ge(amax_done, t + 1)
                    for half, copied in enumerate((adjT_a, adjT_v)):
                        at_least(pe, copied, t)
                        dst = bank[4 + half].bitcast(bf16)
                        for n in range(NT // 2):
                            j = half * (NT // 2) + n
                            ins = pe.transpose(dst[:, n * P:(n + 1) * P], adj_b[b][:, j * P:(j + 1) * P], identb[:, :])
                        ins.then_inc(atr_done, 1)
                if tile(-1):
                    t, b, k = tile(-1)
                    if i == 1:
                        pe.wait_ge(wlo_done, 2)
                    pe.wait_ge(xT_done, t + 1)
                    at_least(pe, vals_done, t - 1)
                    at_least(pe, s_copied, 2 * (t - 1))
                    for n, (c, s, w) in enumerate(terms):
                        ins = pe.matmul(bank[2 + b], xT[b][:, s, c, :], (wq_hi, wq_lo)[w][:, c, :], **ends.get(n, dict(start=False, stop=False)))
                    ins.then_inc(proj_done, 1)
                    for n, (c, s, w) in enumerate(terms):
                        pe.matmul(bank[6 + b][:, 0:2 * H], xT[b][:, s, c, :], (wa_hi, wa_lo)[w][:, c, :], **ends.get(n, dict(start=False, stop=False)))
                    for n, (c, s, w) in enumerate(terms):
                        ins = pe.matmul(bank[6 + b][0:2 * H, P:2 * P], (wa_hi, wa_lo)[w][:, c, :], xT[b][:, s, c, :], **ends.get(n, dict(start=False, stop=False)))
                    ins.then_inc(s_done, 1)

            pipeline(pe, *FIRST_STAGE, first_stage)

            pe.wait_ge(factors, 2)
            pe.matmul(bank[0][:, 0:2 * H], ones[0:2 * H, :], top_diag[:, :], start=True, stop=True).then_inc(top_mm, 1)

            def all_neighbours(pair, r):
                src = bd[:, ds((pair % 3) * (2 * NT * Q * BD), 2 * NT * Q * BD)].rearrange("p (g t q c) -> p t g q c", g=2, t=NT, q=Q)
                for i in range(4):
                    it = 4 * r + i
                    for j in range(NT):
                        ins = pe.matmul(tails[:, i, 0:2 * Q * C], adjT[:, j, it * P:(it + 1) * P], src[:, j, :, :, C:BD],
                                        start=(j == 0 and i % 2 == 0), stop=(j == NT - 1), skip_group_check=True)
                ins.then_inc(t_done, 1)

            pe.wait_ge(bd_first, 2 * BD_STEPS)
            pe.wait_ge(adjT_a, NT)
            pe.wait_ge(adjT_v, NT)
            for r in range(4):
                if r:
                    pe.wait_ge(t_free, r)
                all_neighbours(0, r)
            pe.sem_inc(g_used, G_RING)

            def pair(p, ahead):
                if ahead:
                    pe.wait_ge(bd_chain, BD_STEPS * (2 * p + 2))
                for hh in range(2):
                    src = bd[:, ds((p % 3) * (2 * NT * Q * BD) + hh * (NT * Q * BD), NT * Q * BD)].rearrange("p (t c) -> p t c", t=NT)
                    for half in range(2):
                        w = 4 * p + 2 * hh + half
                        if ahead:
                            pe.wait_ge(t_free, w + 4)
                            all_neighbours(p + 1, 2 * hh + half)
                        at_least(pe, sum_used, w)
                        for j in range(NT):
                            pe.wait_ge(g_ready, G_BASE + NT * w + j + 1)
                            for i in range(HALF):
                                ins = pe.matmul(sums[:, i, 0:Q * BD], gmask[j % G_RING][:, i * P:(i + 1) * P], src[:, j, :],
                                                start=(j == 0 and i % 2 == 0), stop=(j == NT - 1), skip_group_check=True)
                            ins.then_inc(g_used, 1)

            pair(0, True)
            with pe.Fori(1, PAIRS - 1) as p:
                pair(p, True)
            pair(PAIRS - 1, False)

            pe.wait_ge(rw_loaded, 16)
            for c in range(KC):
                ins = pe.matmul(bank[7][:, 0:E], ones[:, :], rw[:, c, :], start=(c == 0), stop=(c == KC - 1))
            ins.then_inc(srw_mm, 1)

            def last_stage(i, tile):
                if tile(-4):
                    t, b, k = tile(-4)
                    pe.wait_ge(x1_done, t + 1)
                    at_least(pe, x1T_done, t - 1)
                    for c in range(KC):
                        ins = pe.transpose(bank[4 + b][:, c * P:(c + 1) * P], x1_now[b][:, c * P:(c + 1) * P], identf[:, :])
                    ins.then_inc(x1tr_done, 1)
                if tile(0):
                    t, b, k = tile(0)
                    pe.wait_ge(h_lo_done, t + 1)
                    at_least(pe, hT_done, t - 1)
                    dst = bank[b].bitcast(fp16)
                    for n in range(2 * KC):
                        ins = pe.transpose(dst[:, n * P:(n + 1) * P], h_hl[b][:, n // KC, (n % KC) * P:(n % KC + 1) * P], ident16[:, :])
                    ins.then_inc(htr_done, 1)
                if tile(-1):
                    t, b, k = tile(-1)
                    pe.wait_ge(hT_done, t + 1)
                    at_least(pe, z_done, t - 1)
                    for n, (c, s, w) in enumerate(terms):
                        ins = pe.matmul(bank[2 + b], hT[b][:, s, c, :], (wo_hi, wo_lo)[w][:, c, :], **ends.get(n, dict(start=False, stop=False)))
                    ins.then_inc(out_mm, 1)
                if tile(-5):
                    t, b, k = tile(-5)
                    pe.wait_ge(x1T_done, t + 1)
                    for c in range(KC):
                        ins = pe.matmul(bank[6][:, ds(t * E, E)], x1T[b][:, c, :], rw[:, c, :], start=(c == 0), stop=(c == KC - 1))
                    ins.then_inc(logit_mm, 1)

            pe.wait_ge(wlo_done, 3)
            pipeline(pe, *LAST_STAGE, last_stage)

            for i, (src, known) in enumerate(((logit, LOGITS_AT), (onehot, ONEHOT_AT))):
                pe.wait_ge(route, known)
                flat = src[:, :, :].rearrange("p t e -> p (t e)")
                pe.matmul(bank[2 * i][:, 0:NT * E], after[:, :], flat, start=True, stop=True)
                pe.matmul(bank[2 * i + 1][:, 0:NT * E], ones[:, :], flat, start=True, stop=True).then_inc(route_mm, 1)

            def token_transposes(t):
                pe.wait_ge(xg_lo_done, t + 1)
                for tt, copied in enumerate((xgT_a, xgT_v)):
                    at_least(pe, copied, t)
                    dst = bank[6 + tt].bitcast(fp16)
                    for i in range(2 * KC):
                        ins = pe.transpose(dst[:, i * P:(i + 1) * P], xg_hl[:, tt, i // KC, (i % KC) * P:(i % KC + 1) * P], ident16[:, :])
                    ins.then_inc(xgtr_done, 1)

            def slot(t, b, k, ahead):
                w1_hi, w1_lo, w2_hi, w2_lo = wbuf[b]
                pe.wait_ge(xgT_a, t + 1)
                pe.wait_ge(xgT_v, t + 1)
                pe.wait_ge(w_lo_done, CH * t + KC)
                for f in range(FC):
                    at_least(pe, gelu_done, FC * t + f - 3)
                    terms = [(w, c, s) for c in range(KC) for w, s in ((w1_hi, 0), (w1_hi, 1), (w1_lo, 0))]
                    for i, (w, c, s) in enumerate(terms):
                        ins = pe.matmul(bank[f % 4][:, 0:SLOT], w[:, c, f * P:(f + 1) * P], xgT[b][:, s, c, :], start=(i == 0), stop=(i == len(terms) - 1))
                    ins.then_inc(up_mm, 1)
                pe.wait_ge(w_lo_done, CH * t + CH)
                for tt in range(TT):
                    if tt == 1 and ahead:
                        token_transposes(t + 1)
                    at_least(pe, y_done, TT * t + tt - 1)
                    for f in range(FC):
                        if tt == 0:
                            pe.wait_ge(hid_lo, FC * t + f + 1)
                        for i, (s, w) in enumerate(((0, w2_hi), (0, w2_lo), (1, w2_hi))):
                            ins = pe.matmul(bank[4 + tt], hidT[:, s, f, tt * P:(tt + 1) * P], w[:, f, :], start=(f == 0 and i == 0), stop=(f == FC - 1 and i == 2))
                    ins.then_inc(down_mm, 1)

            token_transposes(0)
            slot_loop(pe, slot)


_INS = ['x', 'adj', 'L0_gnn_W_seq', 'L0_gnn_a1', 'L0_gnn_a2', 'L0_gnn_W_out', 'L0_gnn_b_out', 'L0_ffn_router_w',
        'L0_ffn_w1', 'L0_ffn_b1', 'L0_ffn_w2', 'L0_ffn_b2']
_OUTS = [((2048, 512), 'float32')]


def kernel(**inputs):
    import numpy as _np
    import concourse.bacc as _bacc
    from concourse import mybir as _mybir
    from concourse.bass_utils import run_bass_kernel_spmd as _run

    nc = _bacc.Bacc("TRN2", target_bir_lowering=False, num_devices=1)
    arrays, args = {}, []
    for name in _INS:
        a = _np.ascontiguousarray(inputs[name])
        arrays[f"in_{name}_dram"] = a
        args.append(nc.dram_tensor(f"in_{name}_dram", a.shape, _mybir.dt.from_np(a.dtype), kind="ExternalInput").ap())
    for i, (shape, dtype) in enumerate(_OUTS):
        dt = _mybir.dt.from_np(_np.dtype(dtype))
        args.append(nc.dram_tensor(f"out_{i}_dram", shape, dt, kind="ExternalOutput").ap())
    gat_moe_kernel(nc, *args)
    r = _run(nc, [arrays], core_ids=[0])
    return r.results[0]["out_0_dram"]
```

```python
import concourse.bass as bass
from concourse import mybir
from contextlib import ExitStack




def gat_moe_kernel(nc, x, adj, w_seq, a1, a2, w_out, b_out, router_w, w1, b1, w2, b2, out):
    fp32, fp16, bf16, i32 = mybir.dt.float32, mybir.dt.float16, mybir.dt.bfloat16, mybir.dt.int32
    ALU = mybir.AluOpType
    ACT = mybir.ActivationFunctionType
    X = mybir.AxisListType.X
    ds = bass.ds

    P = 128
    N, D = x.shape
    DH = a1.shape[0]
    H = D // DH
    NT = N // P
    KC = D // P
    C = DH + 1
    BD = 2 * C
    Q = 3
    ALPHA = 0.2
    EPS = 1e-5

    SCALE = 256.0
    UNSCALE = 1.0 / (SCALE * SCALE)
    STEEP = 2.0 ** 100

    PAIRS = H // 2
    HALF = NT // 2
    SLOTS = 6
    RING = 4
    G_RING = 8
    COMB_BASE = 1
    BD_STEPS = 8
    LOGITS_AT = 5
    EXP_AT = LOGITS_AT + 9
    ONEHOT_AT = EXP_AT + 7
    ROUTE_STEPS = ONEHOT_AT + 18
    FUSED = (5, 13)
    FUSED_LAST = (3, 8, 13)
    MADE = NT - len(FUSED)
    G_BASE = 2 * NT

    E, F = b1.shape
    FC = F // P
    SLOT = 2 * P
    TT = SLOT // P
    SLOTS_MOE = (N + E * (SLOT - 1)) // SLOT
    CH = 2 * KC
    W = D + 2
    HSCALE = 64.0

    ctx = ExitStack()
    with ctx:
        at = [16512]

        def sb(name, shape, dt, offset=None):
            size = {fp32: 4, i32: 4, fp16: 2, bf16: 2}[dt]
            for n in shape[1:]:
                size *= n
            if offset is None:
                offset = at[0]
                at[0] += (size + 31) // 32 * 32
            return nc.alloc_sbuf_tensor_at(name, shape, dt, offset=offset)

        ident16 = sb("ident16", [P, P], fp16)
        identb = sb("identb", [P, P], bf16)
        identf = sb("identf", [P, P], fp32)
        ones = sb("ones", [P, P], fp32)
        eps_col = sb("eps_col", [P, 1], fp32)
        rw = sb("rw", [P, KC, E], fp32)
        rw_sum = sb("rw_sum", [P, E], fp32)
        mv2 = sb("mv2", [P, NT, 2], fp32)
        std2 = sb("std2", [P, NT], fp32)
        rstd2 = sb("rstd2", [P, NT], fp32)
        token_no = sb("token_no", [P, NT], fp32)
        slot_no = sb("slot_no", [P, SLOTS_MOE], fp32)
        slot_low = sb("slot_low", [P, E, N // SLOT], fp32)
        per_token = sb("per_token", [P, NT], fp32)
        zero_t = sb("zero_t", [P, NT], fp32)
        after = sb("after", [P, P], fp32)
        row_of = sb("row_of", [P, NT], i32)
        to_token = [sb(f"to_token{b}", [P, TT], i32) for b in range(2)]
        row_in_slot = sb("row_in_slot", [P, TT], fp32)
        token_f = sb("token_f", [P, TT], fp32)
        from_token = [sb(f"from_token{b}", [P, TT], i32) for b in range(2)]
        expert_of = sb("expert_of", [P, SLOTS_MOE], i32)
        b1_all = sb("b1_all", [P, E * FC], fp32)
        b1_now = [sb(f"b1_now{b}", [P, FC], fp32) for b in range(2)]
        eps1 = sb("eps1", [P, 1], fp32)
        factors_region = at[0]
        fac_a = sb("fac_a", [P, NT, H], fp32)
        fac_c = sb("fac_c", [P, NT, H], fp32)
        den = sb("den", [P, NT, H], fp32)
        routing_region = at[0]
        steep_bias = sb("steep_bias", [P, NT, H], fp32)
        neg_s2 = sb("neg_s2", [P, NT, H], fp32)
        fac_b = sb("fac_b", [P, NT, H], fp32)
        fac_d = sb("fac_d", [P, NT, H], fp32)
        bias_now = [sb(f"bias_now{b}", [P, NT], fp32) for b in range(2)]
        w0_region = at[0]
        adjT = sb("adjT", [P, NT, N], bf16)
        vals = sb("vals", [P, NT, D], fp32)
        bd_region = at[0]
        bd = sb("bd", [P, SLOTS * NT * Q * BD], bf16)
        tsum = sb("tsum", [P, 2 * NT * 2 * C], fp32)
        s1row = [sb(f"s1row{b}", [P, N], fp32) for b in range(2)]
        gr_region = at[0]
        gmask = [sb(f"gmask{i}", [P, N // 2], bf16) for i in range(G_RING)]
        steps = [sb(f"steps{i}", [P, N // 2], bf16) for i in range(RING)]
        bdf = sb("bdf", [P, NT, BD], fp32)
        branch_a = sb("branch_a", [P, HALF, C], fp32)
        branch_c = sb("branch_c", [P, HALF, C], fp32)
        sums_region = at[0]
        ssum = [sb(f"ssum{b}", [P, HALF, BD], fp32) for b in range(2)]
        assert at[0] <= 229344, at[0]
        attention_end = at[0]
        bdf_first = sb("bdf_first", [P, NT, BD], fp32, offset=sums_region)
        zeros = sb("zeros", [P, W], fp32)
        assert at[0] <= 229344, at[0]
        stage_region = 229344 - 2 * 4 * F

        at[0] = bd_region
        x_in = [sb(f"x_in{b}", [P, D], fp32) for b in range(2)]
        adj_in = [sb(f"adj_in{b}", [P, N], fp32) for b in range(2)]
        adj_b = [sb(f"adj_b{b}", [P, N], bf16) for b in range(2)]
        xs = [sb(f"xs{b}", [P, D], fp32) for b in range(2)]
        x_hl = [sb(f"x_hl{b}", [P, 2, D], fp16) for b in range(2)]
        xT = [sb(f"xT{b}", [P, 2, KC, P], fp16) for b in range(2)]
        stats = [sb(f"stats{b}", [P, 6], fp32) for b in range(2)]
        mv = [sb(f"mv{b}", [P, 2], fp32) for b in range(2)]
        std = [sb(f"std{b}", [P, 1], fp32) for b in range(2)]
        rstd = [sb(f"rstd{b}", [P, 1], fp32) for b in range(2)]
        degree = [sb(f"degree{b}", [P, 1], fp32) for b in range(2)]
        alone = [sb(f"alone{b}", [P, 1], fp32) for b in range(2)]
        wf = sb("wf", [P, KC, D], fp32)
        wq_hi = sb("wq_hi", [P, KC, D], fp16)
        wq_lo = sb("wq_lo", [P, KC, D], fp16)
        aw = sb("aw", [P, 2, DH], fp32)
        wa = sb("wa", [P, KC, 2 * H], fp32)
        wa_hi = sb("wa_hi", [P, KC, 2 * H], fp16)
        wa_lo = sb("wa_lo", [P, KC, 2 * H], fp16)
        assert at[0] <= gr_region
        at[0] = gr_region
        s_row = sb("s_row", [2 * H, N], fp32)
        s_tok = sb("s_tok", [P, NT, 2 * H], fp32)
        top_tile = sb("top_tile", [2 * H, NT], fp32)
        top_row = sb("top_row", [2 * H, 1], fp32)
        top_diag = sb("top_diag", [2 * H, 2 * H], fp32)
        top = sb("top", [P, 2 * H], fp32)
        sx = sb("sx", [P, NT, H], fp32)
        sa = sb("sa", [P, NT, H], fp32)
        sc = sb("sc", [P, NT, H], fp32)
        sy = sb("sy", [P, NT, H], fp32)
        assert at[0] <= attention_end
        wprod = [vals[:, i * KC:(i + 1) * KC, :] for i in range(2)]

        at[0] = bd_region
        wo_f = sb("wo_f", [P, KC, D], fp32, offset=bd_region)
        hT = [sb(f"hT{b}", [P, 2, KC, P], fp16) for b in range(2)]
        px = [sb(f"px{b}", [P, D], fp32) for b in range(2)]
        assert at[0] == bd_region + 4 * KC * D
        hn = [sb(f"hn{b}", [P, D], fp32) for b in range(2)]
        h_hl = [sb(f"h_hl{b}", [P, 2, D], fp16) for b in range(2)]
        rden = [sb(f"rden{b}", [P, H], fp32) for b in range(2)]
        z = [sb(f"z{b}", [P, D], fp32) for b in range(2)]
        zneg = [sb(f"zneg{b}", [P, D], fp32) for b in range(2)]
        assert (PAIRS - 1) % 3 == 1
        assert at[0] <= bd_region + 4 * (2 * NT * Q * BD)
        at[0] = bd_region + 4 * (2 * NT * Q * BD)
        wo_hi = sb("wo_hi", [P, KC, D], fp16)
        wo_lo = sb("wo_lo", [P, KC, D], fp16)
        bo_bc = sb("bo_bc", [P, D], fp32)
        assert at[0] <= bd_region + 6 * (2 * NT * Q * BD)
        ez = [sb(f"ez{b}", [P, D], fp32) for b in range(2)]
        x1 = sb("x1", [P, NT, D], fp32)
        x1_now = [sb(f"x1_now{b}", [P, D], fp32) for b in range(2)]
        x1T = [sb(f"x1T{b}", [P, KC, P], fp32) for b in range(2)]
        stats2 = sb("stats2", [P, NT, 6], fp32)
        assert at[0] <= stage_region
        at[0] = stage_region
        stage = [sb(f"stage{b}", [P, F], fp32) for b in range(2)]

        xn = sb("xn", [P, NT, W], fp32, offset=bd_region - 4 * NT * D)
        assert 4 * NT * (W - D) <= 2 * 2 * KC * P

        at[0] = routing_region
        raw = sb("raw", [P, NT, E], fp32)
        shift = sb("shift", [P, NT, E], fp32)
        logit = sb("logit", [P, NT, E], fp32)
        upto = sb("upto", [P, NT, E], fp32)
        before = sb("before", [P, NT, E], fp32)
        ctx_l = sb("ctx_l", [P, NT, E], fp32)
        expd = sb("expd", [P, NT, E], fp32)
        same = sb("same", [P, NT, E], fp32)
        onehot = sb("onehot", [P, NT, E], fp32)
        seen = sb("seen", [P, NT, E], fp32)
        largest = sb("largest", [P, NT], fp32)
        total = sb("total", [P, NT], fp32)
        above = sb("above", [P, E, N // SLOT], fp32)
        slot_f = sb("slot_f", [P, SLOTS_MOE], fp32)
        n_slots = sb("n_slots", [P, E], fp32)
        last_slot = sb("last_slot", [P, E], fp32)
        first_slot = sb("first_slot", [P, E], fp32)
        past = sb("past", [P, SLOTS_MOE, E - 1], fp32)
        assert at[0] <= w0_region

        assert w0_region + 2 * 8 * KC * F // 2 <= bd_region + 4 * NT * D
        wbuf = []
        for b in range(2):
            at[0] = w0_region + b * (8 * KC * F)
            wbuf.append([sb(f"w1_hi{b}", [P, KC, F], fp16), sb(f"w1_lo{b}", [P, KC, F], fp16),
                         sb(f"w2_hi{b}", [P, FC, D], fp16), sb(f"w2_lo{b}", [P, FC, D], fp16)])
        xg = [sb(f"xg{b}", [P, TT, W], fp32) for b in range(2)]
        x1g = [sb(f"x1g{b}", [P, TT, D], fp32) for b in range(2)]
        xg_hl = sb("xg_hl", [P, TT, 2, D], fp16)
        xgT = [sb(f"xgT{b}", [P, 2, KC, SLOT], fp16) for b in range(2)]
        hidT = sb("hidT", [P, 2, FC, SLOT], fp16)
        hid = [sb(f"hid{i}", [P, SLOT], fp32) for i in range(4)]
        y_sb = [sb(f"y_sb{b}", [P, D], fp32) for b in range(2)]
        assert at[0] <= stage_region, at[0] - stage_region
        at[0] = factors_region
        b2_now = [sb(f"b2_now{b}", [P, D], fp32) for b in range(2)]
        assert at[0] <= w0_region

        psum = ctx.enter_context(nc.psum_tensor("psum", [P, 8, 512], fp32))
        bank = [psum[:, i, :] for i in range(8)]
        sums = psum[:, 0:4, :].rearrange("p a (b c) -> p (a b) c", b=2)
        tails = [psum[:, 4 + 2 * i:6 + 2 * i, :].rearrange("p a (b c) -> p (a b) c", b=2) for i in range(2)]

        sorted_x = nc.dram_tensor("sorted_x", [SLOTS_MOE * SLOT, W], fp32, kind="Internal").ap()
        x1_dram = nc.dram_tensor("x1_dram", [N, D], fp32, kind="Internal").ap()
        s1_dram = nc.dram_tensor("s1_dram", [H, N], fp32, kind="Internal").ap()

        def sem(name):
            return ctx.enter_context(nc.semaphore(name))

        passed = sem("passed")
        consts, consts0 = sem("consts"), sem("consts0")
        x_loaded = [sem(f"x_loaded{b}") for b in range(2)]
        adj_loaded = [sem(f"adj_loaded{b}") for b in range(2)]
        wq_loaded, wo_loaded, a_loaded, bo_loaded = sem("wq_loaded"), sem("wo_loaded"), sem("a_loaded"), sem("bo_loaded")
        wprod_done = sem("wprod_done")
        wprep = sem("wprep")
        whi_done = sem("whi_done")
        wlo_done = sem("wlo_done")
        stats_done, mv_done, std_done, rstd_done, xs_done = (sem(n) for n in ("stats_done", "mv_done", "std_done", "rstd_done", "xs_done"))
        hi_done, lo_done, xtr_done, xT_done = (sem(n) for n in ("hi_done", "lo_done", "xtr_done", "xT_done"))
        cast_done, alone_done, amax_done, atr_done, adjT_a, adjT_v = (sem(n) for n in ("cast_done", "alone_done", "amax_done", "atr_done", "adjT_a", "adjT_v"))
        proj_done, s_done, vals_done, s_copied = (sem(n) for n in ("proj_done", "s_done", "vals_done", "s_copied"))
        factors, top_mm, factors_act = sem("factors"), sem("top_mm"), sem("factors_act")
        s1_stored = sem("s1_stored")
        s1_loaded = [sem(f"s1_loaded{b}") for b in range(2)]
        bd_first = sem("bd_first")
        bd_chain = sem("bd_chain")
        bias_done = sem("bias_done")
        step_ready, g_ready, g_used = sem("step_ready"), sem("g_ready"), sem("g_used")
        t_done, t_free = sem("t_done"), sem("t_free")
        sum_used = sem("sum_used")
        comb, comb_done = sem("comb"), sem("comb_done")
        px_loaded = [sem(f"px_loaded{b}") for b in range(2)]
        rden_done, hn_done, h_hi_done, h_lo_done, htr_done, hT_done = (sem(n) for n in ("rden_done", "hn_done", "h_hi_done", "h_lo_done", "htr_done", "hT_done"))
        out_mm, z_done, zneg_done, ez_done, elu_done, x1_done = (sem(n) for n in ("out_mm", "z_done", "zneg_done", "ez_done", "elu_done", "x1_done"))
        rw_loaded, b1_loaded, cleared = sem("rw_loaded"), sem("b1_loaded"), sem("cleared")
        x1_stored, x1_kept = sem("x1_stored"), sem("x1_kept")
        bn2_done, mv2_done, x1tr_done, x1T_done, logit_mm, srw_mm = (sem(n) for n in ("bn2_done", "mv2_done", "x1tr_done", "x1T_done", "logit_mm", "srw_mm"))
        route, route_mm, route_act, xn_done = sem("route"), sem("route_mm"), sem("route_act"), sem("xn_done")
        scattered = sem("scattered")
        stage_loaded = [sem(f"stage_loaded{b}") for b in range(2)]
        bias_loaded = [sem(f"bias_loaded{b}") for b in range(2)]
        xg_loaded = [sem(f"xg_loaded{b}") for b in range(2)]
        w_hi_done, w_lo_done = sem("w_hi_done"), sem("w_lo_done")
        xg_hi_done, xg_lo_done, xgtr_done, xgT_a, xgT_v = (sem(n) for n in ("xg_hi_done", "xg_lo_done", "xgtr_done", "xgT_a", "xgT_v"))
        up_mm, gelu_done, hid_hi, hid_lo, down_mm, y_done = (sem(n) for n in ("up_mm", "gelu_done", "hid_hi", "hid_lo", "down_mm", "y_done"))
        out_stored = [sem(f"out_stored{b}") for b in range(2)]
        x1g_loaded = [sem(f"x1g_loaded{b}") for b in range(2)]
        token_chain, tokens_known, row_done = sem("token_chain"), sem("tokens_known"), sem("row_done")

        def at_least(eng, s, n):
            if not isinstance(n, int) or n > 0:
                eng.wait_ge(s, n)

        def wait_apart(eng, s, n):
            eng.wait_ge(s, n)
            eng.sem_inc(passed, 1)

        def chain(eng, s, ins, n):
            ins.then_inc(s, 1)
            eng.wait_ge(s, n)

        def chain_apart(eng, s, ins, n):
            ins.then_inc(s, 1)
            wait_apart(eng, s, n)

        x_t = x.rearrange("(t p) d -> p t d", p=P)
        adj_t = adj.rearrange("(t p) n -> p t n", p=P)

        x1_t = x1_dram.rearrange("(t p) d -> p t d", p=P)
        sorted_x_t = sorted_x.rearrange("(s p) d -> p s d", p=P)

        def pipeline(eng, first, steady, ebbing, end, body):
            def turn(i, b, k):
                def tile(lag):
                    if isinstance(i, int):
                        t = i + lag
                        return (t, t % 2, t // 2) if 0 <= t < NT else None
                    return i + lag, (b + lag) % 2, k + (b + lag) // 2
                return tile
            for i in range(first, steady):
                body(i, turn(i, i % 2, i // 2))
            with eng.Fori(steady // 2, ebbing // 2) as k:
                for b in range(2):
                    body(None, turn(2 * k + b, b, k))
            for i in range(ebbing, end):
                body(i, turn(i, i % 2, i // 2))

        FIRST_STAGE = (-2, 4, NT - 2, NT + 1)
        LAST_STAGE = (-1, KC + 2, NT - 2, NT + 5)

        def slot_loop(eng, body):
            body(0, 0, 0, True)
            body(1, 1, 0, True)
            with eng.Fori(1, SLOTS_MOE // 2) as k:
                body(2 * k, 0, k, True)
                body(2 * k + 1, 1, k, True)
            assert SLOTS_MOE % 2
            body(SLOTS_MOE - 1, 0, SLOTS_MOE // 2, False)

        def multiply_weights(eng, i):
            return eng.tensor_tensor(wprod[i].rearrange("p c (h d) -> p (c h) d", d=DH), wf[:, :, :].rearrange("p c (h d) -> p (c h) d", d=DH),
                                     aw[:, i:i + 1, :].to_broadcast([P, KC * H, DH]), ALU.mult)

        def make_bd(eng, made, work, h, slot, n):
            v = vals[:, :, ds(h * DH, DH)]
            fb = fac_b[:, :, ds(h, 1)]
            fd = fac_d[:, :, ds(h, 1)]
            dst = bd[:, ds(slot * (NT * Q * BD), NT * Q * BD)].rearrange("p (t q c) -> p t q c", t=NT, q=Q)
            eng.tensor_tensor(work[:, :, 0:DH], v, fb.to_broadcast([P, NT, DH]), ALU.mult).then_inc(made, 1)
            eng.tensor_tensor(work[:, :, C:C + DH], v, fd.to_broadcast([P, NT, DH]), ALU.mult).then_inc(made, 1)
            eng.tensor_copy(work[:, :, DH:C], fb).then_inc(made, 1)
            chain_apart(eng, made, eng.tensor_copy(work[:, :, C + DH:BD], fd), n + 4)
            chain_apart(eng, made, eng.tensor_copy(dst[:, :, 0, :], work[:, :, :]), n + 5)
            chain_apart(eng, made, eng.tensor_tensor(work[:, :, :], work[:, :, :], dst[:, :, 0, :], ALU.subtract), n + 6)
            chain_apart(eng, made, eng.tensor_copy(dst[:, :, 1, :], work[:, :, :]), n + 7)
            chain_apart(eng, made, eng.tensor_tensor(dst[:, :, 2, :], work[:, :, :], dst[:, :, 1, :], ALU.subtract), n + 8)

        block = ctx.enter_context(nc.Block())

        @block.sync
        def _(sp):
            def load_tile(t, b):
                at_least(sp, xs_done, t - 1)
                sp.dma_start(x_in[b][:, :], x_t[:, ds(t, 1), :]).then_inc(x_loaded[b], 16)
                at_least(sp, cast_done, t - 1)
                sp.dma_start(adj_in[b][:, :], adj_t[:, ds(t, 1), :]).then_inc(adj_loaded[b], 16)

            sp.dma_start(x_in[0][:, :], x_t[:, 0, :]).then_inc(x_loaded[0], 16)
            sp.dma_start(wf[:, :, :], w_seq.rearrange("(c p) n -> p c n", p=P)).then_inc(wq_loaded, 16)
            sp.dma_start(aw[:, 0, :], a1.partition_broadcast(P)).then_inc(a_loaded, 16)
            sp.dma_start(aw[:, 1, :], a2.partition_broadcast(P)).then_inc(a_loaded, 16)
            sp.dma_start(adj_in[0][:, :], adj_t[:, 0, :]).then_inc(adj_loaded[0], 16)
            load_tile(1, 1)
            sp.dma_start(rw[:, :, :], router_w.rearrange("(c p) e -> p c e", p=P)).then_inc(rw_loaded, 16)
            with sp.Fori(1, NT // 2) as k:
                t = 2 * k
                load_tile(t, 0)
                load_tile(t + 1, 1)

            sp.wait_ge(s_copied, 3 * NT)
            sp.dma_start(s1_dram, s_row[0:H, :]).then_inc(s1_stored, 16)
            sp.wait_ge(s1_stored, 16)

            def load_row(h, b):
                at_least(sp, step_ready, 2 * MADE * (h - 1))
                if not isinstance(h, int):
                    sp.wait_ge(g_ready, G_BASE + 2 * NT * (h - 1))
                sp.dma_start(s1row[b][:, :], s1_dram[ds(h, 1), :].partition_broadcast(P)).then_inc(s1_loaded[b], 16)

            sp.wait_ge(factors, 9)
            load_row(0, 0)
            load_row(1, 1)
            with sp.Fori(1, H // 2) as k:
                h = 2 * k
                load_row(h, 0)
                load_row(h + 1, 1)

            sp.wait_ge(g_used, G_RING + 4 * NT * (PAIRS - 1))
            sp.dma_start(wo_f[:, :, :], w_out.rearrange("(c p) n -> p c n", p=P)).then_inc(wo_loaded, 16)
            sp.dma_start(bo_bc[:, :], b_out.partition_broadcast(P)).then_inc(bo_loaded, 16)

            sp.wait_ge(comb_done, COMB_BASE + 2 * H)

            def load_chunk(t, e, c):
                g = CH * t + c
                at_least(sp, w_hi_done, g - 1)
                at_least(sp, w_lo_done, g - 1)
                if c < KC:
                    src = w1[ds(e, 1), c * P:(c + 1) * P, :].rearrange("a p f -> p (a f)")
                    dst = stage[g % 2][:, :]
                else:
                    r = (c - KC) * (F // KC)
                    src = w2[ds(e, 1), r:r + F // KC, :].rearrange("a (q p) d -> p (a q) d", p=P)
                    dst = stage[g % 2][:, :].rearrange("p (q d) -> p q d", d=D)
                sp.dma_start(dst, src).then_inc(stage_loaded[g % 2], 16)

            sp.wait_ge(wlo_done, 3)
            sp.wait_ge(cleared, 16)
            for t in range(2):
                sp.dma_start(px[t][:, :], x_t[:, t, :]).then_inc(px_loaded[t], 16)
            for c in range(3):
                load_chunk(0, 0, c)
            for t in range(2, NT):
                sp.wait_ge(x1_done, t - 1)
                sp.dma_start(px[t % 2][:, :], x_t[:, t, :]).then_inc(px_loaded[t % 2], 16)
                if t + 1 < KC + 2:
                    load_chunk(0, 0, t + 1)
                sp.wait_ge(x1_kept, t - 1)
                sp.dma_start(x1_t[:, t - 2, :], x1[:, t - 2, :]).then_inc(x1_stored, 16)
            for t in range(NT - 2, NT):
                sp.wait_ge(x1_kept, t + 1)
                sp.dma_start(x1_t[:, t, :], x1[:, t, :]).then_inc(x1_stored, 16)

            for c in range(KC + 2, CH):
                load_chunk(0, 0, c)

            sp.wait_ge(b1_loaded, 16)
            sp.wait_ge(route, ROUTE_STEPS)
            for t in range(SLOTS_MOE):
                b = t % 2
                e = sp.value_load(expert_of[0:1, t:t + 1], min_val=0, max_val=E - 1)
                if t == 1:
                    sp.wait_ge(xg_loaded[0], 16)
                if t > 0:
                    for c in range(CH):
                        load_chunk(t, e, c)
                at_least(sp, gelu_done, FC * (t - 1))
                at_least(sp, y_done, TT * (t - 1))
                sp.dma_start(b1_now[b][:, :], b1_all[:, ds(e * FC, FC)]).then_inc(bias_loaded[b], 16)
                sp.dma_start(b2_now[b][:, :], b2[ds(e, 1), :].partition_broadcast(P)).then_inc(bias_loaded[b], 16)

        @block.gpsimd
        def _(pool):
            pool.sem_inc(comb_done, COMB_BASE)
            pool.memset(ones[:, :], 1.0).then_inc(consts0, 1)
            pool.memset(eps_col[:, :], EPS / (SCALE * SCALE)).then_inc(consts0, 1)
            pool.memset(eps1[:, :], EPS).then_inc(consts0, 1)
            pool.memset(zeros[:, :], 0.0).then_inc(consts0, 1)
            pool.memset(after[:, :], 0.0).then_inc(consts0, 1)
            pool.memset(zero_t[:, :], 0.0).then_inc(consts0, 1)
            pool.wait_ge(consts0, 6)
            pool.affine_select(out=after[:, :], in_=after[:, :], compare_op=ALU.is_ge, fill=-1.0,
                               base=0, pattern=[[1, P]], channel_multiplier=-1).then_inc(consts, 1)
            pool.iota(token_no[:, :], pattern=[[P, NT]], base=1, channel_multiplier=1, allow_small_or_imprecise_dtypes=True).then_inc(consts, 1)
            pool.iota(row_in_slot[:, :], pattern=[[P, TT]], base=0, channel_multiplier=1, allow_small_or_imprecise_dtypes=True).then_inc(consts, 1)
            pool.iota(slot_no[:, :], pattern=[[1, SLOTS_MOE]], base=0, channel_multiplier=0, allow_small_or_imprecise_dtypes=True).then_inc(consts, 1)
            pool.iota(slot_low[:, :, :], pattern=[[0, E], [SLOT, N // SLOT]], base=0, channel_multiplier=0, allow_small_or_imprecise_dtypes=True).then_inc(consts, 1)
            pool.wait_ge(consts, 5)
            pool.memset(slot_low[:, 0, 0:1], -1.0).then_inc(consts, 1)
            for m in (ident16, identb, identf):
                pool.affine_select(out=m[:, :], in_=ones[:, :], compare_op=ALU.is_equal, fill=0.0,
                                   base=0, pattern=[[-1, P]], channel_multiplier=1).then_inc(consts, 1)
            pool.wait_ge(wq_loaded, 16)
            pool.wait_ge(a_loaded, 32)
            multiply_weights(pool, 1).then_inc(wprod_done, 1)
            with nc.allow_non_contiguous_dma(reason="one bias per partition, once"):
                pool.dma_start(b1_all[:, :].rearrange("p (e c) -> p e c", e=E), b1.rearrange("e (c p) -> p e c", p=P)).then_inc(b1_loaded, 16)

            COMB_STEPS = 4

            def combine(h, half, b, tbuf, hh, w):
                n = w * COMB_STEPS
                i0 = half * HALF
                pool.wait_ge(comb_done, COMB_BASE + w)
                wait_apart(pool, sum_used, w + 1)
                fa = fac_a[:, i0:i0 + HALF, ds(h, 1)].to_broadcast([P, HALF, C])
                fc = fac_c[:, i0:i0 + HALF, ds(h, 1)].to_broadcast([P, HALF, C])
                t_all = tsum[:, ds(tbuf * (NT * 2 * C), NT * 2 * C)].rearrange("p (t g c) -> p t g c", t=NT, g=2)
                pool.tensor_tensor(branch_a[:, :, :], ssum[b][:, :, 0:C], fa, ALU.mult).then_inc(comb, 1)
                chain_apart(pool, comb, pool.tensor_tensor(branch_c[:, :, :], t_all[:, i0:i0 + HALF, hh, :], ssum[b][:, :, C:BD], ALU.subtract), n + 2)
                chain_apart(pool, comb, pool.tensor_tensor(branch_c[:, :, :], branch_c[:, :, :], fc, ALU.mult), n + 3)
                chain_apart(pool, comb, pool.tensor_tensor(vals[:, i0:i0 + HALF, ds(h * DH, DH)], branch_a[:, :, 0:DH], branch_c[:, :, 0:DH], ALU.add), n + 4)
                pool.tensor_tensor(den[:, i0:i0 + HALF, ds(h, 1)], branch_a[:, :, DH:C], branch_c[:, :, DH:C], ALU.add).then_inc(comb_done, 1)

            pool.wait_ge(factors_act, 4)
            pool.wait_ge(vals_done, NT)
            pool.wait_ge(s1_stored, 16)
            pool.dma_start(sorted_x_t, zeros[:, :].rearrange("p (a d) -> p a d", a=1).to_broadcast([P, SLOTS_MOE * TT, W])).then_inc(cleared, 16)
            for h in range(2, 4):
                make_bd(pool, bd_chain, bdf, h, h, (h - 2) * BD_STEPS)

            def pair(p, prepare):
                if prepare:
                    wait_apart(pool, g_used, G_RING + 4 * NT * p)
                for hh in range(2):
                    for half in range(2):
                        if prepare and hh == 0:
                            h = 2 * p + 4 + half
                            make_bd(pool, bd_chain, bdf, h, h % SLOTS, (h - 2) * BD_STEPS)
                        combine(2 * p + hh, half, half, p % 2, hh, 4 * p + 2 * hh + half)

            with pool.Fori(0, PAIRS - 2) as p:
                pair(p, True)
            with pool.Fori(PAIRS - 2, PAIRS) as p:
                pair(p, False)

            pool.wait_ge(comb_done, COMB_BASE + 2 * H)

            def last_stage(i, tile):
                if tile(1):
                    t, b, k = tile(1)
                    if not isinstance(t, int) or t > 1:
                        wait_apart(pool, h_hi_done, t - 1)
                    wait_apart(pool, rden_done, t + 1)
                    pool.tensor_tensor(hn[b][:, :].rearrange("p (h d) -> p h d", d=DH),
                                       vals[:, ds(t, 1), :].rearrange("p a (h d) -> p (a h) d", d=DH),
                                       rden[b][:, :].rearrange("p (h a) -> p h a", a=1).to_broadcast([P, H, DH]), ALU.mult).then_inc(hn_done, 1)
                if tile(-4):
                    t, b, k = tile(-4)
                    wait_apart(pool, x1_done, t + 1)
                    pool.tensor_copy(x1[:, ds(t, 1), :].rearrange("p a d -> p (a d)"), x1_now[b][:, :]).then_inc(x1_kept, 1)

            pipeline(pool, *LAST_STAGE, last_stage)

            pool.wait_ge(cleared, 16)
            pool.wait_ge(route, ROUTE_STEPS)
            for t in range(NT):
                pool.wait_ge(xn_done, t + 1)
                pool.indirect_dma_start(out=sorted_x, out_offset=bass.IndirectOffsetOnAxis(ap=row_of[:, t:t + 1], axis=0),
                                        in_=xn[:, t, :], in_offset=None).then_inc(scattered, 16)
            pool.wait_ge(scattered, 16 * NT)
            pool.wait_ge(x1_stored, 16 * NT)

            def load_slot(t, b):
                if not isinstance(t, int):
                    wait_apart(pool, xg_lo_done, t - 1)
                else:
                    at_least(pool, xg_lo_done, t - 1)
                pool.dma_start(xg[b][:, :, :], sorted_x_t[:, ds(t * TT, TT), :]).then_inc(xg_loaded[b], 16)

            def slot(t, b, k, ahead):
                if ahead:
                    load_slot(t + 1, 1 - b)
                for tt in range(TT):
                    wait_apart(pool, row_done, TT * t + tt + 1)
                    pool.indirect_dma_start(out=out, out_offset=bass.IndirectOffsetOnAxis(ap=to_token[b][:, tt:tt + 1], axis=0),
                                            in_=y_sb[tt][:, :], in_offset=None).then_inc(out_stored[tt], 16)
                    if tt == 0 and ahead:
                        load_x1(t + 1, 1 - b)

            def load_x1(t, b):
                wait_apart(pool, tokens_known, t + 1)
                for tt in range(TT):
                    pool.indirect_dma_start(out=x1g[b][:, tt, :], out_offset=None, in_=x1_dram,
                                            in_offset=bass.IndirectOffsetOnAxis(ap=from_token[b][:, tt:tt + 1], axis=0)).then_inc(x1g_loaded[b], 16)

            load_slot(0, 0)
            load_x1(0, 0)
            slot_loop(pool, slot)
            for tt in range(TT):
                pool.wait_ge(out_stored[tt], 16 * SLOTS_MOE)

        @block.scalar
        def _(act):
            act.wait_ge(consts0, 2)

            def cast_adj(t, b, k):
                act.wait_ge(adj_loaded[b], 16 * (k + 1))
                at_least(act, atr_done, 2 * (t - 1))
                at_least(act, alone_done, t - 1)
                act.activation(adj_b[b][:, :], adj_in[b][:, :], ACT.Copy, accum_out=degree[b][:, :]).then_inc(cast_done, 1)

            def first_stage(i, tile):
                if i == 0:
                    act.wait_ge(wprep, 4)
                    act.activation(wa_hi[:, :, :], wa[:, :, :], ACT.Copy, scale=SCALE).then_inc(whi_done, 1)
                if tile(1):
                    t, b, k = tile(1)
                    act.wait_ge(mv_done, t + 1)
                    act.activation(std[b][:, :], mv[b][:, 1:2], ACT.Sqrt, bias=eps_col[:, :],
                                   scale=1.0 / (SCALE * SCALE)).then_inc(std_done, 1)
                if tile(0):
                    t, b, k = tile(0)
                    act.wait_ge(atr_done, 2 * t + 1)
                    act.activation(adjT[:, 0:NT // 2, ds(t * P, P)],
                                   bank[4].bitcast(bf16).rearrange("p (j c) -> p j c", c=P), ACT.Copy).then_inc(adjT_a, 1)
                if tile(1):
                    t, b, k = tile(1)
                    act.wait_ge(xs_done, t + 1)
                    at_least(act, xtr_done, t - 1)
                    act.activation(x_hl[b][:, 0, :], xs[b][:, :], ACT.Copy).then_inc(hi_done, 1)
                if i == -1:
                    act.wait_ge(wq_loaded, 16)
                    act.activation(wq_hi[:, :, :], wf[:, :, :], ACT.Copy, scale=SCALE).then_inc(whi_done, 1)
                    cast_adj(0, 0, 0)
                if tile(2) and i != -2:
                    cast_adj(*tile(2))
                if tile(-1):
                    t, b, k = tile(-1)
                    act.wait_ge(proj_done, t + 1)
                    act.activation(vals[:, ds(t, 1), :], bank[2 + b], ACT.Copy, scale=UNSCALE).then_inc(vals_done, 1)

            pipeline(act, *FIRST_STAGE, first_stage)

            act.wait_ge(factors, 8)
            act.activation(fac_b[:, :, :], sy[:, :, :], ACT.Exp).then_inc(factors_act, 1)
            act.activation(fac_d[:, :, :], sy[:, :, :], ACT.Exp, scale=ALPHA).then_inc(factors_act, 1)
            act.activation(fac_a[:, :, :], sa[:, :, :], ACT.Exp).then_inc(factors_act, 1)
            act.activation(fac_c[:, :, :], sc[:, :, :], ACT.Exp).then_inc(factors_act, 1)
            act.wait_ge(factors_act, 4)
            act.wait_ge(factors, 9)

            def pair(p, fused):
                made = 0
                for hh in range(2):
                    h = 2 * p + hh
                    act.activation(bias_now[hh][:, :], steep_bias[:, :, ds(h, 1)].rearrange("p t a -> p (t a)"), ACT.Copy).then_inc(bias_done, 1)
                    act.wait_ge(bias_done, h + 1)
                    act.wait_ge(s1_loaded[hh], 16 * (p + 1))
                    for half in range(2):
                        w = 2 * hh + half
                        for j in range(NT):
                            if j in fused:
                                continue
                            back = [(ww, jj) for ww in range(-1, w + 1) for jj in range(NT)
                                    if jj not in (fused if ww >= 0 else FUSED) and (ww, jj) < (w, j)][-RING]
                            act.wait_ge(g_ready, G_BASE + 4 * NT * p + back[0] * NT + back[1] + 1)
                            ins = act.activation(steps[made % RING][:, :], s1row[hh][:, half * (N // 2):(half + 1) * (N // 2)],
                                                 ACT.Relu, bias=bias_now[hh][:, j:j + 1], scale=STEEP)
                            ins.then_inc(step_ready, 1)
                            made += 1

            with act.Fori(0, PAIRS - 1) as p:
                pair(p, FUSED)
            pair(PAIRS - 1, FUSED_LAST)

            def chunk_hi(t, b, c, k):
                act.wait_ge(stage_loaded[c % 2], 16 * ((CH // 2) * t + c // 2 + 1))
                if c == 0:
                    at_least(act, down_mm, TT * (t - 1))
                dst = wbuf[b][0][:, c, :] if c < KC else wbuf[b][2][:, (c - KC) * KC:(c - KC + 1) * KC, :].rearrange("p q d -> p (q d)")
                act.activation(dst, stage[c % 2][:, :], ACT.Copy, scale=SCALE).then_inc(w_hi_done, 1)

            act.wait_ge(wo_loaded, 16)
            act.activation(wo_hi[:, :, :], wo_f[:, :, :], ACT.Copy, scale=SCALE).then_inc(whi_done, 1)

            def last_stage(i, tile):
                if i is not None and 2 <= i < KC + 2:
                    chunk_hi(0, 0, i - 2, 0)
                if i is not None and NT + 1 <= i < NT + 3:
                    chunk_hi(0, 0, i - (NT + 1) + KC, 0)
                if tile(-4):
                    t, b, k = tile(-4)
                    act.wait_ge(x1tr_done, t + 1)
                    at_least(act, logit_mm, t - 1)
                    act.activation(x1T[b][:, :, :].rearrange("p c q -> p (c q)"), bank[4 + b], ACT.Copy).then_inc(x1T_done, 1)
                if tile(0):
                    t, b, k = tile(0)
                    act.wait_ge(htr_done, t + 1)
                    at_least(act, out_mm, t - 1)
                    act.activation(hT[b][:, :, :, :].rearrange("p a b c -> p (a b c)"), bank[b].bitcast(fp16), ACT.Copy).then_inc(hT_done, 1)
                if tile(-2):
                    t, b, k = tile(-2)
                    act.wait_ge(z_done, t + 1)
                    at_least(act, ez_done, t - 1)
                    act.activation(zneg[b][:, :], z[b][:, :], ACT.Relu, scale=-1.0).then_inc(zneg_done, 1)
                    act.wait_ge(zneg_done, t + 1)
                    at_least(act, elu_done, t - 1)
                    act.activation(ez[b][:, :], zneg[b][:, :], ACT.Exp, scale=-1.0).then_inc(ez_done, 1)
                if tile(1):
                    t, b, k = tile(1)
                    act.wait_ge(hn_done, t + 1)
                    at_least(act, htr_done, t - 1)
                    act.activation(h_hl[b][:, 0, :], hn[b][:, :], ACT.Copy, scale=SCALE).then_inc(h_hi_done, 1)

            pipeline(act, *LAST_STAGE, last_stage)
            act.wait_ge(mv2_done, NT)
            act.activation(std2[:, :].rearrange("p (t a) -> p t a", a=1), mv2[:, :, 1:2], ACT.Sqrt, bias=eps1[:, :]).then_inc(route_act, 1)
            act.wait_ge(route, EXP_AT)
            act.activation(expd[:, :, :], ctx_l[:, :, :], ACT.Exp).then_inc(route_act, 1)
            for c in range(KC + 2, CH):
                chunk_hi(0, 0, c, 0)

            def tokens_hi(t, b, k):
                act.wait_ge(xg_loaded[b], 16 * (k + 1))
                at_least(act, xgtr_done, TT * t)
                act.activation(xg_hl[:, :, 0, :], xg[b][:, :, 0:D], ACT.Copy, scale=SCALE).then_inc(xg_hi_done, 1)

            def tokens_T(t, b):
                act.wait_ge(xgtr_done, TT * t + 1)
                at_least(act, up_mm, FC * (t - 1))
                act.activation(xgT[b][:, :, :, 0:P].rearrange("p a c q -> p (a c) q"), bank[6].bitcast(fp16).rearrange("p (a q) -> p a q", q=P), ACT.Copy).then_inc(xgT_a, 1)

            def slot(t, b, k, ahead):
                act.wait_ge(bias_loaded[b], 32 * (k + 1))
                for f in range(FC):
                    act.wait_ge(up_mm, FC * t + f + 1)
                    at_least(act, hid_lo, FC * t + f - 3)
                    act.activation(hid[f % 4][:, :], bank[f % 4][:, 0:SLOT], ACT.Gelu_apprx_tanh, bias=b1_now[b][:, f:f + 1], scale=UNSCALE).then_inc(gelu_done, 1)
                    if ahead and f % 4 == 3:
                        chunk_hi(t + 1, 1 - b, f // 4, k)
                if ahead:
                    tokens_hi(t + 1, 1 - b, k + b)
                    for c in range(KC, CH - 1):
                        chunk_hi(t + 1, 1 - b, c, k)
                    tokens_T(t + 1, 1 - b)
                    chunk_hi(t + 1, 1 - b, CH - 1, k)

            tokens_hi(0, 0, 0)
            tokens_T(0, 0)
            slot_loop(act, slot)

        @block.vector
        def _(dve):
            dve.sem_inc(g_ready, G_BASE)
            def weights():
                dve.wait_ge(wq_loaded, 16)
                dve.wait_ge(a_loaded, 32)
                multiply_weights(dve, 0).then_inc(wprep, 1)
                for i in range(2):
                    if i == 0:
                        dve.wait_ge(wprep, 1)
                    else:
                        dve.wait_ge(wprod_done, 1)
                    dve.tensor_reduce(wa[:, :, i * H:(i + 1) * H], wprod[i].rearrange("p c (h d) -> p c h d", d=DH), X, ALU.add).then_inc(wprep, 1)
                dve.wait_ge(consts, 9)
                dve.reciprocal(per_token[:, :], token_no[:, :]).then_inc(wprep, 1)
                dve.wait_ge(whi_done, 1)
                dve.scalar_tensor_tensor(wq_lo[:, :, :].rearrange("p c n -> p (c n)"), wf[:, :, :].rearrange("p c n -> p (c n)"), SCALE, wq_hi[:, :, :].rearrange("p c n -> p (c n)"), ALU.mult, ALU.subtract).then_inc(wlo_done, 1)

            def weights_low():
                dve.wait_ge(whi_done, 2)
                dve.scalar_tensor_tensor(wa_lo[:, :, :], wa[:, :, :], SCALE, wa_hi[:, :, :], ALU.mult, ALU.subtract).then_inc(wlo_done, 1)

            def first_stage(i, tile):
                if i == 1:
                    weights_low()
                if tile(1):
                    t, b, k = tile(1)
                    dve.wait_ge(x_loaded[b], 16 * (k + 1))
                    dve.bn_stats(stats[b][:, :], x_in[b][:, :]).then_inc(stats_done, 1)
                    at_least(dve, std_done, t - 1)
                    wait_apart(dve, stats_done, t + 1)
                    dve.bn_aggr(mv[b][:, :], stats[b][:, :]).then_inc(mv_done, 1)
                if tile(0):
                    t, b, k = tile(0)
                    dve.wait_ge(xtr_done, t + 1)
                    at_least(dve, s_done, t - 1)
                    dve.tensor_copy(xT[b][:, :, :, :].rearrange("p a b c -> p (a b c)"), bank[b].bitcast(fp16)).then_inc(xT_done, 1)
                if tile(1):
                    t, b, k = tile(1)
                    dve.wait_ge(std_done, t + 1)
                    dve.reciprocal(rstd[b][:, :], std[b][:, :]).then_inc(rstd_done, 1)
                    dve.wait_ge(rstd_done, t + 1)
                    at_least(dve, hi_done, t - 1)
                    dve.tensor_scalar(xs[b][:, :], x_in[b][:, :], mv[b][:, 0:1], rstd[b][:, :], ALU.subtract, ALU.mult).then_inc(xs_done, 1)
                    if i == -1:
                        weights()
                    dve.wait_ge(cast_done, t + 1)
                    dve.tensor_scalar(alone[b][:, :], degree[b][:, :], 0.5, None, ALU.is_lt).then_inc(alone_done, 1)
                    dve.wait_ge(alone_done, t + 1)
                    dve.tensor_scalar(adj_b[b][:, :], adj_b[b][:, :], alone[b][:, :], None, ALU.max).then_inc(amax_done, 1)
                if tile(1):
                    t, b, k = tile(1)
                    dve.wait_ge(hi_done, t + 1)
                    dve.tensor_tensor(x_hl[b][:, 1, :], xs[b][:, :], x_hl[b][:, 0, :], ALU.subtract).then_inc(lo_done, 1)
                if tile(0):
                    t, b, k = tile(0)
                    dve.wait_ge(atr_done, 2 * t + 2)
                    dve.tensor_copy(adjT[:, NT // 2:NT, ds(t * P, P)], bank[5].bitcast(bf16).rearrange("p (j c) -> p j c", c=P)).then_inc(adjT_v, 1)
                if tile(-1):
                    t, b, k = tile(-1)
                    dve.wait_ge(s_done, t + 1)
                    dve.tensor_scalar(s_tok[:, ds(t, 1), :], bank[6 + b][:, 0:2 * H], UNSCALE, None, ALU.mult).then_inc(s_copied, 1)
                    dve.tensor_scalar(s_row[:, ds(t * P, P)], bank[6 + b][0:2 * H, P:2 * P], UNSCALE, None, ALU.mult).then_inc(s_copied, 1)
                    dve.reduce_max(top_tile[:, ds(t, 1)], bank[6 + b][0:2 * H, P:2 * P], X).then_inc(s_copied, 1)

            pipeline(dve, *FIRST_STAGE, first_stage)

            dve.wait_ge(s_copied, 3 * NT)
            chain(dve, factors, dve.reduce_max(top_row[:, :], top_tile[:, :], X), 1)
            chain(dve, factors, dve.tensor_scalar(top_diag[:, :], identf[0:2 * H, 0:2 * H], top_row[:, :], UNSCALE, ALU.mult, ALU.mult), 2)
            dve.wait_ge(top_mm, 1)
            chain(dve, factors, dve.tensor_copy(top[:, :], bank[0][:, 0:2 * H]), 3)
            top2 = top[:, H:2 * H].rearrange("p (a h) -> p a h", a=1).to_broadcast([P, NT, H])
            chain(dve, factors, dve.tensor_tensor(sx[:, :, :], s_tok[:, :, 0:H], top2, ALU.add), 4)
            dve.tensor_scalar(sa[:, :, :], sx[:, :, :], 1.0 - ALPHA, 0.0, ALU.mult, ALU.min).then_inc(factors, 1)
            dve.tensor_scalar(sc[:, :, :], sx[:, :, :], ALPHA - 1.0, 0.0, ALU.mult, ALU.min).then_inc(factors, 1)
            dve.tensor_tensor(sy[:, :, :], s_tok[:, :, H:2 * H], top2, ALU.subtract).then_inc(factors, 1)
            dve.tensor_scalar(steep_bias[:, :, :], s_tok[:, :, H:2 * H], STEEP, None, ALU.mult).then_inc(factors, 1)
            dve.tensor_scalar(neg_s2[:, :, :], s_tok[:, :, H:2 * H], -1.0, None, ALU.mult).then_inc(factors, 1)
            dve.wait_ge(factors_act, 2)
            dve.wait_ge(vals_done, NT)
            for h in range(2):
                make_bd(dve, bd_first, bdf_first, h, h, h * BD_STEPS)

            def copy_tails(pair, r):
                dst = tsum[:, ds((pair % 2) * (NT * 2 * C), NT * 2 * C)].rearrange("p (t g c) -> p t g c", t=NT, g=2)
                for g in range(2):
                    src = tails[r % 2][:, :, g * Q * C:(g + 1) * Q * C].rearrange("p t (q c) -> p t c q", q=Q)
                    ins = dve.tensor_reduce(dst[:, 4 * r:4 * r + 4, g, :], src, X, ALU.add)
                ins.then_inc(t_free, 1)

            for r in range(2):
                dve.wait_ge(t_done, r + 1)
                copy_tails(0, r)

            def pair(p, ahead, fused):
                made = 0
                for hh in range(2):
                    h = 2 * p + hh
                    dve.wait_ge(s1_loaded[hh], 16 * (p + 1))
                    for half in range(2):
                        w = 4 * p + 2 * hh + half
                        q0 = half * (N // 2)
                        for j in range(NT):
                            dve.wait_ge(g_used, NT * w + j + 1)
                            mask = adjT[:, j, q0:q0 + N // 2]
                            if j in fused:
                                ins = dve.scalar_tensor_tensor(gmask[j % G_RING][:, :], s1row[hh][:, q0:q0 + N // 2],
                                                               neg_s2[:, j, ds(h, 1)], mask, ALU.is_gt, ALU.mult)
                            else:
                                dve.wait_ge(step_ready, 4 * MADE * p + made + 1)
                                ins = dve.tensor_tensor(gmask[j % G_RING][:, :], steps[made % RING][:, :], mask, ALU.min)
                                made += 1
                            ins.then_inc(g_ready, 1)
                            if j == 5 and (hh == 0 or ahead):
                                dve.wait_ge(t_done, w + 3)
                                if hh == 1:
                                    dve.wait_ge(comb_done, COMB_BASE + 4 * p)
                                copy_tails(p + hh, 2 * (1 - hh) + half)
                        dve.wait_ge(g_used, G_RING + NT * (w + 1))
                        src = sums[:, :, 0:Q * BD].rearrange("p t (q c) -> p t c q", q=Q)
                        at_least(dve, comb_done, w)
                        dve.tensor_reduce(ssum[half][:, :, :], src, X, ALU.add).then_inc(sum_used, 1)

            pair(0, True, FUSED)
            with dve.Fori(1, PAIRS - 1) as p:
                pair(p, True, FUSED)
            pair(PAIRS - 1, False, FUSED_LAST)

            def chunk_lo(t, b, c):
                dve.wait_ge(w_hi_done, CH * t + c + 1)
                if c < KC:
                    hi, lo = wbuf[b][0][:, c, :], wbuf[b][1][:, c, :]
                else:
                    hi, lo = (wbuf[b][i][:, (c - KC) * KC:(c - KC + 1) * KC, :].rearrange("p q d -> p (q d)") for i in (2, 3))
                dve.scalar_tensor_tensor(lo, stage[c % 2][:, :], SCALE, hi, ALU.mult, ALU.subtract).then_inc(w_lo_done, 1)

            def last_stage(i, tile):
                if tile(0):
                    t, b, k = tile(0)
                    dve.wait_ge(h_hi_done, t + 1)
                    dve.scalar_tensor_tensor(h_hl[b][:, 1, :], hn[b][:, :], SCALE, h_hl[b][:, 0, :], ALU.mult, ALU.subtract).then_inc(h_lo_done, 1)
                if tile(-2):
                    t, b, k = tile(-2)
                    if i == 2:
                        dve.wait_ge(comb_done, COMB_BASE + 2 * H)
                    at_least(dve, x1_done, t - 1)
                    dve.wait_ge(out_mm, t + 1)
                    dve.scalar_tensor_tensor(z[b][:, :], bank[2 + b], UNSCALE, bo_bc[:, :], ALU.mult, ALU.add).then_inc(z_done, 1)
                if tile(1):
                    t, b, k = tile(1)
                    at_least(dve, hn_done, t - 1)
                    dve.reciprocal(rden[b][:, :], den[:, ds(t, 1), :].rearrange("p a h -> p (a h)")).then_inc(rden_done, 1)
                if tile(-3):
                    t, b, k = tile(-3)
                    dve.wait_ge(ez_done, t + 1)
                    dve.scalar_tensor_tensor(z[b][:, :], z[b][:, :], 0.0, ez[b][:, :], ALU.max, ALU.add).then_inc(elu_done, 1)
                    dve.wait_ge(elu_done, t + 1)
                    dve.wait_ge(px_loaded[b], 16 * (k + 1))
                    at_least(dve, x1_kept, t - 1)
                    at_least(dve, x1tr_done, t - 1)
                    dve.scalar_tensor_tensor(x1_now[b][:, :], z[b][:, :], -1.0, px[b][:, :], ALU.add, ALU.add).then_inc(x1_done, 1)
                    dve.wait_ge(x1_done, t + 1)
                    dve.bn_stats(stats2[:, ds(t, 1), :].rearrange("p a d -> p (a d)"), x1_now[b][:, :]).then_inc(bn2_done, 1)
                if i is not None and 2 <= i < KC + 2:
                    chunk_lo(0, 0, i - 2)

            dve.wait_ge(whi_done, 3)
            dve.scalar_tensor_tensor(wo_lo[:, :, :], wo_f[:, :, :], SCALE, wo_hi[:, :, :], ALU.mult, ALU.subtract).then_inc(wlo_done, 1)
            dve.wait_ge(comb_done, COMB_BASE + 2 * H - 1)
            dve.wait_ge(bo_loaded, 16)
            pipeline(dve, *LAST_STAGE, last_stage)

            steps_done = [0]

            def step(ins):
                steps_done[0] += 1
                chain(dve, route, ins, steps_done[0])

            def free_step(ins):
                steps_done[0] += 1
                ins.then_inc(route, 1)

            def await_steps():
                dve.wait_ge(route, steps_done[0])

            def over_e(a):
                return a.rearrange("p (t a) -> p t a", a=1).to_broadcast([P, NT, E])

            def over_t(a):
                return a.rearrange("p (a e) -> p a e", a=1).to_broadcast([P, NT, E])

            dve.wait_ge(bn2_done, NT)
            for t in range(NT):
                dve.bn_aggr(mv2[:, t, :], stats2[:, t, :]).then_inc(mv2_done, 1)
            dve.wait_ge(srw_mm, 1)
            step(dve.tensor_copy(rw_sum[:, :], bank[7][:, 0:E]))
            chunk_lo(0, 0, KC)
            dve.wait_ge(logit_mm, NT)
            dve.wait_ge(mv2_done, NT)
            step(dve.tensor_tensor(shift[:, :, :], mv2[:, :, 0:1].to_broadcast([P, NT, E]), over_t(rw_sum[:, :]), ALU.mult))
            free_step(dve.tensor_tensor(raw[:, :, :], bank[6][:, 0:NT * E].rearrange("p (t e) -> p t e", e=E), shift[:, :, :], ALU.subtract))
            dve.wait_ge(route_act, 1)
            step(dve.reciprocal(rstd2[:, :], std2[:, :]))
            step(dve.tensor_tensor(logit[:, :, :], raw[:, :, :], over_e(rstd2[:, :]), ALU.mult))
            assert steps_done[0] == LOGITS_AT
            dve.wait_ge(x1_kept, NT)

            def normalise(t0, t1):
                for t in range(t0, t1):
                    dve.tensor_scalar(xn[:, t, 0:D], x1[:, t, :], mv2[:, t, 0:1], rstd2[:, t:t + 1], ALU.subtract, ALU.mult).then_inc(xn_done, 1)

            def running(mm, all_sums, after):
                dve.wait_ge(route_mm, mm)
                tile_sums = all_sums.rearrange("p (t e) -> p t e", e=E)
                for e in range(E):
                    free_step(dve.tensor_tensor_scan(before[:, :, e], zero_t[:, :], tile_sums[:, :, e], 0.0, ALU.add, ALU.add))
                await_steps()
                step(dve.tensor_tensor(upto[:, :, :], before[:, :, :], after.rearrange("p (t e) -> p t e", e=E), ALU.add))

            free_step(dve.tensor_scalar(xn[:, :, D + 1], token_no[:, :], -1.0, float(N + 1), ALU.mult, ALU.add))
            normalise(0, 5)
            running(1, bank[1][:, 0:NT * E], bank[0][:, 0:NT * E])
            step(dve.tensor_tensor(ctx_l[:, :, :], upto[:, :, :], over_e(per_token[:, :]), ALU.mult))
            step(dve.reduce_max(largest[:, :], ctx_l[:, :, :], X))
            step(dve.tensor_tensor(ctx_l[:, :, :], ctx_l[:, :, :], over_e(largest[:, :]), ALU.subtract))
            assert steps_done[0] == EXP_AT
            step(dve.tensor_scalar(same[:, :, :], ctx_l[:, :, :], 0.0, None, ALU.is_equal))
            free_step(dve.tensor_copy(onehot[:, :, 0], same[:, :, 0]))
            for e in range(1, E):
                before_e = same[:, :, 0] if e == 1 else seen[:, :, e - 1]
                free_step(dve.tensor_tensor(onehot[:, :, e], same[:, :, e], before_e, ALU.is_gt))
                if e < E - 1:
                    step(dve.tensor_tensor(seen[:, :, e], same[:, :, e], before_e, ALU.max))
            await_steps()
            assert steps_done[0] == ONEHOT_AT
            dve.wait_ge(route_act, 2)
            free_step(dve.reduce_sum(total[:, :], expd[:, :, :], X))
            normalise(5, 6)
            await_steps()
            free_step(dve.reciprocal(xn[:, :, D], total[:, :]))
            normalise(6, 9)
            running(2, bank[3][:, 0:NT * E], bank[2][:, 0:NT * E])
            counts = before[:, NT - 1, :]
            step(dve.tensor_tensor(above[:, :, :], counts.rearrange("p (e a) -> p e a", a=1).to_broadcast([P, E, N // SLOT]),
                                   slot_low[:, :, :], ALU.is_gt))
            step(dve.reduce_sum(n_slots[:, :], above[:, :, :], X))
            step(dve.tensor_tensor_scan(last_slot[:, :], zero_t[:, 0:E], n_slots[:, :], 0.0, ALU.add, ALU.add))
            free_step(dve.tensor_tensor(first_slot[:, :], last_slot[:, :], n_slots[:, :], ALU.subtract))
            step(dve.tensor_tensor(past[:, :, :], slot_no[:, :].rearrange("p (s a) -> p s a", a=1).to_broadcast([P, SLOTS_MOE, E - 1]),
                                   last_slot[:, 0:E - 1].rearrange("p (a e) -> p a e", a=1).to_broadcast([P, SLOTS_MOE, E - 1]), ALU.is_ge))
            free_step(dve.reduce_sum(slot_f[:, :], past[:, :, :], X))
            step(dve.scalar_tensor_tensor(upto[:, :, :], over_t(first_slot[:, :]), float(SLOT), upto[:, :, :], ALU.mult, ALU.add))
            free_step(dve.tensor_copy(expert_of[:, :], slot_f[:, :]))
            step(dve.tensor_tensor(upto[:, :, :], upto[:, :, :], onehot[:, :, :], ALU.mult))
            step(dve.reduce_sum(total[:, :], upto[:, :, :], X))
            step(dve.tensor_scalar(row_of[:, :], total[:, :], -1.0, None, ALU.add))
            assert steps_done[0] == ROUTE_STEPS, steps_done
            normalise(9, NT)
            for c in range(KC + 1, CH):
                chunk_lo(0, 0, c)

            def tokens_lo(t, b):
                dve.wait_ge(xg_hi_done, t + 1)
                dve.scalar_tensor_tensor(xg_hl[:, :, 1, :], xg[b][:, :, 0:D], SCALE, xg_hl[:, :, 0, :], ALU.mult, ALU.subtract).then_inc(xg_lo_done, 1)
                for tt in range(TT):
                    at_least(dve, out_stored[tt], 16 * (t - 1))
                last = xg[b][:, :, D + 1:W].rearrange("p t a -> p (t a)")
                n = 3 * t
                chain(dve, token_chain, dve.scalar_tensor_tensor(token_f[:, :], last, 0.0, row_in_slot[:, :], ALU.is_equal, ALU.mult), n + 1)
                chain(dve, token_chain, dve.tensor_tensor(token_f[:, :], token_f[:, :], last, ALU.subtract), n + 2)
                dve.tensor_scalar(to_token[b][:, :], token_f[:, :], float(N), None, ALU.add).then_inc(token_chain, 1)
                dve.tensor_scalar(from_token[b][:, :], token_f[:, :], -1.0, float(N), ALU.min, ALU.add).then_inc(tokens_known, 1)

            def tokens_T(t, b):
                dve.wait_ge(xgtr_done, TT * t + 2)
                dve.tensor_copy(xgT[b][:, :, :, P:2 * P].rearrange("p a c q -> p (a c) q"), bank[7].bitcast(fp16).rearrange("p (a q) -> p a q", q=P)).then_inc(xgT_v, 1)

            def finish_rows(t, tt, b, k):
                dve.wait_ge(down_mm, TT * t + tt + 1)
                at_least(dve, out_stored[tt], 16 * t)
                dve.scalar_tensor_tensor(y_sb[tt][:, :], bank[4 + tt], 1.0 / (SCALE * HSCALE), b2_now[b][:, :], ALU.mult, ALU.add).then_inc(y_done, 1)
                dve.wait_ge(y_done, TT * t + tt + 1)
                dve.wait_ge(x1g_loaded[b], 16 * TT * (k + 1))
                dve.scalar_tensor_tensor(y_sb[tt][:, :], y_sb[tt][:, :], xg[b][:, tt, D:D + 1], x1g[b][:, tt, :], ALU.mult, ALU.add).then_inc(row_done, 1)

            def slot(t, b, k, ahead):
                for f in range(FC):
                    n = FC * t + f
                    dve.wait_ge(gelu_done, n + 1)
                    if f == 0:
                        at_least(dve, down_mm, TT * t)
                    dve.tensor_scalar(hidT[:, 0, f, :], hid[f % 4][:, :], HSCALE, None, ALU.mult).then_inc(hid_hi, 1)
                    dve.wait_ge(hid_hi, n + 1)
                    dve.scalar_tensor_tensor(hidT[:, 1, f, :], hid[f % 4][:, :], HSCALE, hidT[:, 0, f, :], ALU.mult, ALU.subtract).then_inc(hid_lo, 1)
                    if ahead and f % 4 == 3:
                        chunk_lo(t + 1, 1 - b, f // 4)
                if ahead:
                    tokens_lo(t + 1, 1 - b)
                    for c in range(KC, CH - 1):
                        chunk_lo(t + 1, 1 - b, c)
                finish_rows(t, 0, b, k)
                if ahead:
                    tokens_T(t + 1, 1 - b)
                    chunk_lo(t + 1, 1 - b, CH - 1)
                finish_rows(t, 1, b, k)

            tokens_lo(0, 0)
            tokens_T(0, 0)
            slot_loop(dve, slot)

        @block.tensor
        def _(pe):
            pe.wait_ge(consts, 9)

            terms = [(c, s, w) for c in range(KC) for s, w in ((0, 0), (0, 1), (1, 0))]
            ends = {0: dict(start=True, stop=False), len(terms) - 1: dict(start=False, stop=True)}

            def first_stage(i, tile):
                if tile(0):
                    t, b, k = tile(0)
                    pe.wait_ge(lo_done, t + 1)
                    at_least(pe, xT_done, t - 1)
                    dst = bank[b].bitcast(fp16)
                    for n in range(2 * KC):
                        ins = pe.transpose(dst[:, n * P:(n + 1) * P], x_hl[b][:, n // KC, (n % KC) * P:(n % KC + 1) * P], ident16[:, :])
                    ins.then_inc(xtr_done, 1)
                    pe.wait_ge(amax_done, t + 1)
                    for half, copied in enumerate((adjT_a, adjT_v)):
                        at_least(pe, copied, t)
                        dst = bank[4 + half].bitcast(bf16)
                        for n in range(NT // 2):
                            j = half * (NT // 2) + n
                            ins = pe.transpose(dst[:, n * P:(n + 1) * P], adj_b[b][:, j * P:(j + 1) * P], identb[:, :])
                        ins.then_inc(atr_done, 1)
                if tile(-1):
                    t, b, k = tile(-1)
                    if i == 1:
                        pe.wait_ge(wlo_done, 2)
                    pe.wait_ge(xT_done, t + 1)
                    at_least(pe, vals_done, t - 1)
                    at_least(pe, s_copied, 3 * (t - 1))
                    for n, (c, s, w) in enumerate(terms):
                        ins = pe.matmul(bank[2 + b], xT[b][:, s, c, :], (wq_hi, wq_lo)[w][:, c, :], **ends.get(n, dict(start=False, stop=False)))
                    ins.then_inc(proj_done, 1)
                    for n, (c, s, w) in enumerate(terms):
                        pe.matmul(bank[6 + b][:, 0:2 * H], xT[b][:, s, c, :], (wa_hi, wa_lo)[w][:, c, :], **ends.get(n, dict(start=False, stop=False)))
                    for n, (c, s, w) in enumerate(terms):
                        ins = pe.matmul(bank[6 + b][0:2 * H, P:2 * P], (wa_hi, wa_lo)[w][:, c, :], xT[b][:, s, c, :], **ends.get(n, dict(start=False, stop=False)))
                    ins.then_inc(s_done, 1)

            pipeline(pe, *FIRST_STAGE, first_stage)

            pe.wait_ge(factors, 2)
            pe.matmul(bank[0][:, 0:2 * H], ones[0:2 * H, :], top_diag[:, :], start=True, stop=True).then_inc(top_mm, 1)

            def all_neighbours(pair, r):
                src = bd[:, ds((pair % 3) * (2 * NT * Q * BD), 2 * NT * Q * BD)].rearrange("p (g t q c) -> p t g q c", g=2, t=NT, q=Q)
                for i in range(4):
                    it = 4 * r + i
                    for j in range(NT):
                        ins = pe.matmul(tails[r % 2][:, i, 0:2 * Q * C], adjT[:, j, it * P:(it + 1) * P], src[:, j, :, :, C:BD],
                                        start=(j == 0 and i % 2 == 0), stop=(j == NT - 1), skip_group_check=True)
                ins.then_inc(t_done, 1)

            pe.wait_ge(adjT_a, NT)
            pe.wait_ge(adjT_v, NT)
            src = bd[:, 0:2 * NT * Q * BD].rearrange("p (g t q c) -> p t g q c", g=2, t=NT, q=Q)
            for g in range(2):
                pe.wait_ge(bd_first, (g + 1) * BD_STEPS)
                for i in range(4):
                    for j in range(NT):
                        ins = pe.matmul(tails[0][:, i, g * Q * C:(g + 1) * Q * C], adjT[:, j, i * P:(i + 1) * P], src[:, j, g, :, C:BD],
                                        start=(g == 0 and j == 0 and i % 2 == 0), stop=(j == NT - 1), skip_group_check=True)
            ins.then_inc(t_done, 1)
            all_neighbours(0, 1)
            pe.sem_inc(g_used, G_RING)

            def pair(p, ahead):
                for hh in range(2):
                    if hh == 1 and ahead:
                        pe.wait_ge(bd_chain, BD_STEPS * (2 * p + 2))
                    src = bd[:, ds((p % 3) * (2 * NT * Q * BD) + hh * (NT * Q * BD), NT * Q * BD)].rearrange("p (t c) -> p t c", t=NT)
                    for half in range(2):
                        w = 4 * p + 2 * hh + half
                        if hh == 0 or ahead:
                            pe.wait_ge(t_free, w + 1)
                            all_neighbours(p + hh, 2 * (1 - hh) + half)
                        at_least(pe, sum_used, w)
                        for j in range(NT):
                            pe.wait_ge(g_ready, G_BASE + NT * w + j + 1)
                            for i in range(HALF):
                                ins = pe.matmul(sums[:, i, 0:Q * BD], gmask[j % G_RING][:, i * P:(i + 1) * P], src[:, j, :],
                                                start=(j == 0 and i % 2 == 0), stop=(j == NT - 1), skip_group_check=True)
                            ins.then_inc(g_used, 1)

            pair(0, True)
            with pe.Fori(1, PAIRS - 1) as p:
                pair(p, True)
            pair(PAIRS - 1, False)

            pe.wait_ge(rw_loaded, 16)
            for c in range(KC):
                ins = pe.matmul(bank[7][:, 0:E], ones[:, :], rw[:, c, :], start=(c == 0), stop=(c == KC - 1))
            ins.then_inc(srw_mm, 1)

            def last_stage(i, tile):
                if tile(-4):
                    t, b, k = tile(-4)
                    pe.wait_ge(x1_done, t + 1)
                    at_least(pe, x1T_done, t - 1)
                    for c in range(KC):
                        ins = pe.transpose(bank[4 + b][:, c * P:(c + 1) * P], x1_now[b][:, c * P:(c + 1) * P], identf[:, :])
                    ins.then_inc(x1tr_done, 1)
                if tile(0):
                    t, b, k = tile(0)
                    pe.wait_ge(h_lo_done, t + 1)
                    at_least(pe, hT_done, t - 1)
                    dst = bank[b].bitcast(fp16)
                    for n in range(2 * KC):
                        ins = pe.transpose(dst[:, n * P:(n + 1) * P], h_hl[b][:, n // KC, (n % KC) * P:(n % KC + 1) * P], ident16[:, :])
                    ins.then_inc(htr_done, 1)
                if tile(-1):
                    t, b, k = tile(-1)
                    pe.wait_ge(hT_done, t + 1)
                    at_least(pe, z_done, t - 1)
                    for n, (c, s, w) in enumerate(terms):
                        ins = pe.matmul(bank[2 + b], hT[b][:, s, c, :], (wo_hi, wo_lo)[w][:, c, :], **ends.get(n, dict(start=False, stop=False)))
                    ins.then_inc(out_mm, 1)
                if tile(-5):
                    t, b, k = tile(-5)
                    pe.wait_ge(x1T_done, t + 1)
                    for c in range(KC):
                        ins = pe.matmul(bank[6][:, ds(t * E, E)], x1T[b][:, c, :], rw[:, c, :], start=(c == 0), stop=(c == KC - 1))
                    ins.then_inc(logit_mm, 1)

            pe.wait_ge(wlo_done, 3)
            pipeline(pe, *LAST_STAGE, last_stage)

            for i, (src, known) in enumerate(((logit, LOGITS_AT), (onehot, ONEHOT_AT))):
                pe.wait_ge(route, known)
                flat = src[:, :, :].rearrange("p t e -> p (t e)")
                pe.matmul(bank[2 * i][:, 0:NT * E], after[:, :], flat, start=True, stop=True)
                pe.matmul(bank[2 * i + 1][:, 0:NT * E], ones[:, :], flat, start=True, stop=True).then_inc(route_mm, 1)

            def token_transposes(t):
                pe.wait_ge(xg_lo_done, t + 1)
                for tt, copied in enumerate((xgT_a, xgT_v)):
                    at_least(pe, copied, t)
                    dst = bank[6 + tt].bitcast(fp16)
                    for i in range(2 * KC):
                        ins = pe.transpose(dst[:, i * P:(i + 1) * P], xg_hl[:, tt, i // KC, (i % KC) * P:(i % KC + 1) * P], ident16[:, :])
                    ins.then_inc(xgtr_done, 1)

            def slot(t, b, k, ahead):
                w1_hi, w1_lo, w2_hi, w2_lo = wbuf[b]
                pe.wait_ge(xgT_a, t + 1)
                pe.wait_ge(xgT_v, t + 1)
                pe.wait_ge(w_lo_done, CH * t + KC)
                for f in range(FC):
                    at_least(pe, gelu_done, FC * t + f - 3)
                    terms = [(w, c, s) for c in range(KC) for w, s in ((w1_hi, 0), (w1_hi, 1), (w1_lo, 0))]
                    for i, (w, c, s) in enumerate(terms):
                        ins = pe.matmul(bank[f % 4][:, 0:SLOT], w[:, c, f * P:(f + 1) * P], xgT[b][:, s, c, :], start=(i == 0), stop=(i == len(terms) - 1))
                    ins.then_inc(up_mm, 1)
                pe.wait_ge(w_lo_done, CH * t + CH)
                for tt in range(TT):
                    if tt == 1 and ahead:
                        token_transposes(t + 1)
                    at_least(pe, y_done, TT * t + tt - 1)
                    for f in range(FC):
                        if tt == 0:
                            pe.wait_ge(hid_lo, FC * t + f + 1)
                        for i, (s, w) in enumerate(((0, w2_hi), (0, w2_lo), (1, w2_hi))):
                            ins = pe.matmul(bank[4 + tt], hidT[:, s, f, tt * P:(tt + 1) * P], w[:, f, :], start=(f == 0 and i == 0), stop=(f == FC - 1 and i == 2))
                    ins.then_inc(down_mm, 1)

            token_transposes(0)
            slot_loop(pe, slot)


_INS = ['x', 'adj', 'L0_gnn_W_seq', 'L0_gnn_a1', 'L0_gnn_a2', 'L0_gnn_W_out', 'L0_gnn_b_out', 'L0_ffn_router_w',
        'L0_ffn_w1', 'L0_ffn_b1', 'L0_ffn_w2', 'L0_ffn_b2']
_OUTS = [((2048 + 256, 512), 'float32')]


def kernel(**inputs):
    import numpy as _np
    import concourse.bacc as _bacc
    from concourse import mybir as _mybir
    from concourse.bass_utils import run_bass_kernel_spmd as _run

    nc = _bacc.Bacc("TRN2", target_bir_lowering=False, num_devices=1)
    arrays, args = {}, []
    for name in _INS:
        a = _np.ascontiguousarray(inputs[name])
        arrays[f"in_{name}_dram"] = a
        args.append(nc.dram_tensor(f"in_{name}_dram", a.shape, _mybir.dt.from_np(a.dtype), kind="ExternalInput").ap())
    for i, (shape, dtype) in enumerate(_OUTS):
        dt = _mybir.dt.from_np(_np.dtype(dtype))
        args.append(nc.dram_tensor(f"out_{i}_dram", shape, dt, kind="ExternalOutput").ap())
    gat_moe_kernel(nc, *args)
    r = _run(nc, [arrays], core_ids=[0])
    return r.results[0]["out_0_dram"][:inputs['x'].shape[0]]
```
